# Optimizing a Trainium2 kernel written in Bass

```python
import numpy as np
import jax
import jax.numpy as jnp

def _softmax(x, axis=-1):
    return jax.nn.softmax(x, axis=axis)

def _gelu(x):
    return jax.nn.gelu(x, approximate=True)

def _silu(x):
    return jax.nn.silu(x)

def _sigmoid(x):
    return jax.nn.sigmoid(x)

def _layernorm(x, axis=-1, eps=1e-05):
    m = jnp.mean(x, axis=axis, keepdims=True)
    v = jnp.var(x, axis=axis, keepdims=True)
    return (x - m) / jnp.sqrt(v + eps)

def _scatter_add(tgt, idx, src, axis=0):
    return tgt.at[idx].add(src)

def _segment_sum(src, seg, n):
    return jax.ops.segment_sum(src, seg, n)
kernel_name = 'mk_xattn_seq_d2_seqx_r2_f3b50f'

def setup_inputs(seed: int=0):
    np.random.seed(seed)
    _w = jnp.asarray

    def _rec_inputs():
        import jax
        import jax.numpy as jnp
        _rk = jax.random.key(seed)
        x = -0.0002928 + 1 * jax.random.normal(jax.random.fold_in(_rk, 1), (16, 512, 512), jnp.float32)
        _lenS = 512 - jax.random.randint(jax.random.fold_in(_rk, 7), (16,), 0, max(1, 512 // 4) + 1, jnp.int32)
        _lenS2 = 77 - jax.random.randint(jax.random.fold_in(_rk, 8), (16,), 0, max(1, 77 // 4) + 1, jnp.int32)
        _ctx_1024P = jax.random.normal(jax.random.fold_in(_rk, 11), (16, 16, 512), jnp.float32)
        _ctx_1024c = jax.random.dirichlet(jax.random.fold_in(_rk, 511), 0.3 * jnp.ones((16,), jnp.float32), (16, 77))
        _ctx_1024t = jnp.einsum('bsk,bkd->bsd', _ctx_1024c, _ctx_1024P)
        _ctx_1024t = _ctx_1024t * jax.lax.rsqrt(jnp.mean(jnp.square(_ctx_1024t)) + 1e-12) * 0.953939
        ctx_1024 = -1.39393e-06 + 0.999914 * (_ctx_1024t + 0.3 * jax.random.normal(jax.random.fold_in(_rk, 611), (16, 77, 512), jnp.float32))
        _validS = jnp.arange(512)[None, :] < _lenS[:, None]
        _validS2 = jnp.arange(77)[None, :] < _lenS2[:, None]
        _causal = jnp.tril(jnp.ones((512, 512), dtype=bool))
        mask_Bx1xSxS2_fk0 = jnp.where(jnp.broadcast_to(_validS2[:, None, None, :], (16, 1, 512, 77)), 0.0, 1.0).astype(jnp.float32)
        mask_1xS2_bf0 = jnp.logical_not(jnp.ones((1, 77), dtype=bool))
        return (x, ctx_1024, mask_Bx1xSxS2_fk0, mask_1xS2_bf0)
    x, ctx_1024, mask_Bx1xSxS2_fk0, mask_1xS2_bf0 = _rec_inputs()

    def _L0_xattn_setup():
        import jax, jax.numpy as jnp
        import numpy as np
        ALPHA = 0.5
        SCORES_CLAMP = 50.0
        LN_EPS = 1e-05
        N_HEADS = 16
        key = jax.random.key(seed)
        ks = jax.random.split(key, 16)
        B, Q, K, D = (2, 1024, 1024, 512)
        s = 1.0 / np.sqrt(D)
        return {'query': jax.random.normal(ks[0], (B, Q, D), jnp.float32), 'key_in': jax.random.normal(ks[1], (B, K, D), jnp.float32), 'mask': jax.random.randint(ks[2], (B, 1, Q, K), 0, 2).astype(jnp.float32), 'Wq': jax.random.normal(ks[3], (D, D), jnp.float32) * s, 'bq': jnp.zeros((D,), jnp.float32), 'Wk': jax.random.normal(ks[4], (D, D), jnp.float32) * s, 'bk': jnp.zeros((D,), jnp.float32), 'Wv': jax.random.normal(ks[5], (D, D), jnp.float32) * s, 'bv': jnp.zeros((D,), jnp.float32), 'Wo': jax.random.normal(ks[6], (D, D), jnp.float32) * s, 'bo': jnp.zeros((D,), jnp.float32), 'gamma': jnp.ones((D,), jnp.float32), 'beta': jnp.zeros((D,), jnp.float32)}
    _L0_xattn_all = _L0_xattn_setup()
    _L0_xattn_in = {k: v for k, v in _L0_xattn_all.items() if k in ('Wq', 'bq', 'Wk', 'bk', 'Wv', 'bv', 'Wo', 'bo', 'gamma', 'beta')}
    del _L0_xattn_all

    def _L1_xattn_setup():
        import jax, jax.numpy as jnp
        import numpy as np
        D = 512
        D_STATE = 128
        N_HEADS = 8
        D_INNER = 2 * D
        HEADDIM = 64
        H_M = D_INNER // HEADDIM
        D_CONV = 4
        CONV_DIM = D_INNER + 2 * D_STATE
        D_IN_PROJ = 2 * D_INNER + 2 * D_STATE + H_M
        B = 1
        LQ = 512
        LK = 1024
        EPS = 1e-05

        def _rms(x, w):
            return x * jax.lax.rsqrt(jnp.mean(x * x, axis=-1, keepdims=True) + EPS) * w

        def _ln(x, w, b):
            mu = jnp.mean(x, axis=-1, keepdims=True)
            v = jnp.mean((x - mu) ** 2, axis=-1, keepdims=True)
            return (x - mu) * jax.lax.rsqrt(v + EPS) * w + b

        def _mamba2_block(x, norm_w, in_proj_w, conv_w, conv_b, dt_bias, A_log, D_skip, gnorm_w, out_proj_w):
            b, L, _ = x.shape
            resid = x
            zxbcdt = _rms(x, norm_w) @ in_proj_w
            z = zxbcdt[..., :D_INNER]
            xBC = zxbcdt[..., D_INNER:D_INNER + CONV_DIM]
            dt = jax.nn.softplus(zxbcdt[..., -H_M:] + dt_bias)
            padded = jnp.pad(xBC, ((0, 0), (D_CONV - 1, 0), (0, 0)))
            conv = conv_b + sum((padded[:, k:k + L, :] * conv_w[:, k] for k in range(D_CONV)))
            xBC = jax.nn.silu(conv)
            xh = xBC[..., :D_INNER].reshape(b, L, H_M, HEADDIM)
            Bm = xBC[..., D_INNER:D_INNER + D_STATE]
            Cm = xBC[..., D_INNER + D_STATE:]
            A = -jnp.exp(A_log)
            decay = jnp.exp(dt * A)
            dbx = dt[..., None] * xh

            def step(h, inp):
                dec, u, bt, ct = inp
                h = h * dec[:, :, None, None] + u[..., None] * bt[:, None, None, :]
                y = jnp.einsum('bhpn,bn->bhp', h, ct)
                return (h, y)
            h0 = jnp.zeros((b, H_M, HEADDIM, D_STATE), x.dtype)
            xs = (decay.transpose(1, 0, 2), dbx.transpose(1, 0, 2, 3), Bm.transpose(1, 0, 2), Cm.transpose(1, 0, 2))
            _, ys = jax.lax.scan(step, h0, xs)
            y = ys.transpose(1, 0, 2, 3) + D_skip[None, None, :, None] * xh
            u = _rms(y.reshape(b, L, D_INNER) * jax.nn.silu(z), gnorm_w)
            return resid + u @ out_proj_w

        def _cross_attention(x, enc, pad_mask, ln_w, ln_b, Wq, Wk, Wv, Wo):
            b, Lq, _ = x.shape
            Lk = enc.shape[1]
            dh = D // N_HEADS
            resid = x
            xn = _ln(x, ln_w, ln_b)
            q = (xn @ Wq).reshape(b, Lq, N_HEADS, dh)
            k = (enc @ Wk).reshape(b, Lk, N_HEADS, dh)
            v = (enc @ Wv).reshape(b, Lk, N_HEADS, dh)
            scores = jnp.einsum('bqhd,bkhd->bhqk', q, k) * np.float32(1.0 / np.sqrt(dh))
            scores = jnp.where(pad_mask[:, None, None, :], jnp.float32(-1000000000.0), scores)
            p = jax.nn.softmax(scores, axis=-1)
            ctx = jnp.einsum('bhqk,bkhd->bqhd', p, v).reshape(b, Lq, D)
            return resid + ctx @ Wo
        key = jax.random.key(seed)
        ks = jax.random.split(key, 10)
        s = 0.02
        return {'x': jax.random.normal(ks[0], (B, LQ, D), jnp.float32), 'encoder_out': jax.random.normal(ks[1], (B, LK, D), jnp.float32), 'encoder_padding_mask': jnp.zeros((B, LK), dtype=bool), 'm_norm_w': jnp.ones((D,), jnp.float32), 'in_proj_w': s * jax.random.normal(ks[2], (D, D_IN_PROJ), jnp.float32), 'conv_w': s * jax.random.normal(ks[3], (CONV_DIM, D_CONV), jnp.float32), 'conv_b': jnp.zeros((CONV_DIM,), jnp.float32), 'dt_bias': jnp.full((H_M,), float(np.log(np.expm1(0.01))), jnp.float32), 'A_log': jnp.log(jnp.linspace(1.0, 16.0, H_M)).astype(jnp.float32), 'D_skip': jnp.ones((H_M,), jnp.float32), 'gnorm_w': jnp.ones((D_INNER,), jnp.float32), 'out_proj_w': s * jax.random.normal(ks[4], (D_INNER, D), jnp.float32), 'ca_ln_w': jnp.ones((D,), jnp.float32), 'ca_ln_b': jnp.zeros((D,), jnp.float32), 'Wq': s * jax.random.normal(ks[5], (D, D), jnp.float32), 'Wk': s * jax.random.normal(ks[6], (D, D), jnp.float32), 'Wv': s * jax.random.normal(ks[7], (D, D), jnp.float32), 'Wo': s * jax.random.normal(ks[8], (D, D), jnp.float32)}
    _L1_xattn_all = _L1_xattn_setup()
    _L1_xattn_in = {k: v for k, v in _L1_xattn_all.items() if k in ('m_norm_w', 'in_proj_w', 'conv_w', 'conv_b', 'dt_bias', 'A_log', 'D_skip', 'gnorm_w', 'out_proj_w', 'ca_ln_w', 'ca_ln_b', 'Wq', 'Wk', 'Wv', 'Wo')}
    del _L1_xattn_all
    return {'x': x, 'ctx_1024': ctx_1024, 'mask_Bx1xSxS2_fk0': mask_Bx1xSxS2_fk0, 'mask_1xS2_bf0': mask_1xS2_bf0, 'L0_xattn_Wq': _L0_xattn_in['Wq'], 'L0_xattn_bq': _L0_xattn_in['bq'], 'L0_xattn_Wk': _L0_xattn_in['Wk'], 'L0_xattn_bk': _L0_xattn_in['bk'], 'L0_xattn_Wv': _L0_xattn_in['Wv'], 'L0_xattn_bv': _L0_xattn_in['bv'], 'L0_xattn_Wo': _L0_xattn_in['Wo'], 'L0_xattn_bo': _L0_xattn_in['bo'], 'L0_xattn_gamma': _L0_xattn_in['gamma'], 'L0_xattn_beta': _L0_xattn_in['beta'], 'L1_xattn_m_norm_w': _L1_xattn_in['m_norm_w'], 'L1_xattn_in_proj_w': _L1_xattn_in['in_proj_w'], 'L1_xattn_conv_w': _L1_xattn_in['conv_w'], 'L1_xattn_conv_b': _L1_xattn_in['conv_b'], 'L1_xattn_dt_bias': _L1_xattn_in['dt_bias'], 'L1_xattn_A_log': _L1_xattn_in['A_log'], 'L1_xattn_D_skip': _L1_xattn_in['D_skip'], 'L1_xattn_gnorm_w': _L1_xattn_in['gnorm_w'], 'L1_xattn_out_proj_w': _L1_xattn_in['out_proj_w'], 'L1_xattn_ca_ln_w': _L1_xattn_in['ca_ln_w'], 'L1_xattn_ca_ln_b': _L1_xattn_in['ca_ln_b'], 'L1_xattn_Wq': _L1_xattn_in['Wq'], 'L1_xattn_Wk': _L1_xattn_in['Wk'], 'L1_xattn_Wv': _L1_xattn_in['Wv'], 'L1_xattn_Wo': _L1_xattn_in['Wo']}

def reference(x, ctx_1024, mask_Bx1xSxS2_fk0, mask_1xS2_bf0, L0_xattn_Wq, L0_xattn_bq, L0_xattn_Wk, L0_xattn_bk, L0_xattn_Wv, L0_xattn_bv, L0_xattn_Wo, L0_xattn_bo, L0_xattn_gamma, L0_xattn_beta, L1_xattn_m_norm_w, L1_xattn_in_proj_w, L1_xattn_conv_w, L1_xattn_conv_b, L1_xattn_dt_bias, L1_xattn_A_log, L1_xattn_D_skip, L1_xattn_gnorm_w, L1_xattn_out_proj_w, L1_xattn_ca_ln_w, L1_xattn_ca_ln_b, L1_xattn_Wq, L1_xattn_Wk, L1_xattn_Wv, L1_xattn_Wo):
    import jax
    import jax.numpy as jnp

    def _L0_xattn_ref(query, key_in, mask, Wq, bq, Wk, bk, Wv, bv, Wo, bo, gamma, beta):
        import jax, jax.numpy as jnp
        import numpy as np
        ALPHA = 0.5
        SCORES_CLAMP = 50.0
        LN_EPS = 1e-05
        N_HEADS = 16
        B, Qlen, D = query.shape
        Klen = key_in.shape[1]
        H = N_HEADS
        hd = D // H
        q = (query @ Wq + bq).reshape(B, Qlen, H, hd).transpose(0, 2, 1, 3)
        k = (key_in @ Wk + bk).reshape(B, Klen, H, hd).transpose(0, 2, 1, 3)
        v = (key_in @ Wv + bv).reshape(B, Klen, H, hd).transpose(0, 2, 1, 3)
        scores = jnp.einsum('bhqd,bhkd->bhqk', q, k) / jnp.sqrt(jnp.float32(hd))
        scores = ALPHA * (scores * mask) + (1.0 - ALPHA) * scores
        scores = jnp.clip(scores, -SCORES_CLAMP, SCORES_CLAMP)
        attn = jax.nn.softmax(scores, axis=-1)
        context = jnp.einsum('bhqk,bhkd->bhqd', attn, v)
        context = context.transpose(0, 2, 1, 3).reshape(B, Qlen, D)
        out = context @ Wo + bo
        resid = query + out
        mu = jnp.mean(resid, axis=-1, keepdims=True)
        var = jnp.mean(jnp.square(resid - mu), axis=-1, keepdims=True)
        return (resid - mu) * jax.lax.rsqrt(var + LN_EPS) * gamma + beta

    def _L1_xattn_ref(x, encoder_out, encoder_padding_mask, m_norm_w, in_proj_w, conv_w, conv_b, dt_bias, A_log, D_skip, gnorm_w, out_proj_w, ca_ln_w, ca_ln_b, Wq, Wk, Wv, Wo):
        import jax, jax.numpy as jnp
        import numpy as np
        D = 512
        D_STATE = 128
        N_HEADS = 8
        D_INNER = 2 * D
        HEADDIM = 64
        H_M = D_INNER // HEADDIM
        D_CONV = 4
        CONV_DIM = D_INNER + 2 * D_STATE
        D_IN_PROJ = 2 * D_INNER + 2 * D_STATE + H_M
        B = 1
        LQ = 512
        LK = 1024
        EPS = 1e-05

        def _rms(x, w):
            return x * jax.lax.rsqrt(jnp.mean(x * x, axis=-1, keepdims=True) + EPS) * w

        def _ln(x, w, b):
            mu = jnp.mean(x, axis=-1, keepdims=True)
            v = jnp.mean((x - mu) ** 2, axis=-1, keepdims=True)
            return (x - mu) * jax.lax.rsqrt(v + EPS) * w + b

        def _mamba2_block(x, norm_w, in_proj_w, conv_w, conv_b, dt_bias, A_log, D_skip, gnorm_w, out_proj_w):
            b, L, _ = x.shape
            resid = x
            zxbcdt = _rms(x, norm_w) @ in_proj_w
            z = zxbcdt[..., :D_INNER]
            xBC = zxbcdt[..., D_INNER:D_INNER + CONV_DIM]
            dt = jax.nn.softplus(zxbcdt[..., -H_M:] + dt_bias)
            padded = jnp.pad(xBC, ((0, 0), (D_CONV - 1, 0), (0, 0)))
            conv = conv_b + sum((padded[:, k:k + L, :] * conv_w[:, k] for k in range(D_CONV)))
            xBC = jax.nn.silu(conv)
            xh = xBC[..., :D_INNER].reshape(b, L, H_M, HEADDIM)
            Bm = xBC[..., D_INNER:D_INNER + D_STATE]
            Cm = xBC[..., D_INNER + D_STATE:]
            A = -jnp.exp(A_log)
            decay = jnp.exp(dt * A)
            dbx = dt[..., None] * xh

            def step(h, inp):
                dec, u, bt, ct = inp
                h = h * dec[:, :, None, None] + u[..., None] * bt[:, None, None, :]
                y = jnp.einsum('bhpn,bn->bhp', h, ct)
                return (h, y)
            h0 = jnp.zeros((b, H_M, HEADDIM, D_STATE), x.dtype)
            xs = (decay.transpose(1, 0, 2), dbx.transpose(1, 0, 2, 3), Bm.transpose(1, 0, 2), Cm.transpose(1, 0, 2))
            _, ys = jax.lax.scan(step, h0, xs)
            y = ys.transpose(1, 0, 2, 3) + D_skip[None, None, :, None] * xh
            u = _rms(y.reshape(b, L, D_INNER) * jax.nn.silu(z), gnorm_w)
            return resid + u @ out_proj_w

        def _cross_attention(x, enc, pad_mask, ln_w, ln_b, Wq, Wk, Wv, Wo):
            b, Lq, _ = x.shape
            Lk = enc.shape[1]
            dh = D // N_HEADS
            resid = x
            xn = _ln(x, ln_w, ln_b)
            q = (xn @ Wq).reshape(b, Lq, N_HEADS, dh)
            k = (enc @ Wk).reshape(b, Lk, N_HEADS, dh)
            v = (enc @ Wv).reshape(b, Lk, N_HEADS, dh)
            scores = jnp.einsum('bqhd,bkhd->bhqk', q, k) * np.float32(1.0 / np.sqrt(dh))
            scores = jnp.where(pad_mask[:, None, None, :], jnp.float32(-1000000000.0), scores)
            p = jax.nn.softmax(scores, axis=-1)
            ctx = jnp.einsum('bhqk,bkhd->bqhd', p, v).reshape(b, Lq, D)
            return resid + ctx @ Wo
        h = _mamba2_block(x, m_norm_w, in_proj_w, conv_w, conv_b, dt_bias, A_log, D_skip, gnorm_w, out_proj_w)
        return _cross_attention(h, encoder_out, encoder_padding_mask, ca_ln_w, ca_ln_b, Wq, Wk, Wv, Wo)
    x = _L0_xattn_ref(x, ctx_1024, mask_Bx1xSxS2_fk0, L0_xattn_Wq, L0_xattn_bq, L0_xattn_Wk, L0_xattn_bk, L0_xattn_Wv, L0_xattn_bv, L0_xattn_Wo, L0_xattn_bo, L0_xattn_gamma, L0_xattn_beta)
    x = _L1_xattn_ref(x, ctx_1024, mask_1xS2_bf0, L1_xattn_m_norm_w, L1_xattn_in_proj_w, L1_xattn_conv_w, L1_xattn_conv_b, L1_xattn_dt_bias, L1_xattn_A_log, L1_xattn_D_skip, L1_xattn_gnorm_w, L1_xattn_out_proj_w, L1_xattn_ca_ln_w, L1_xattn_ca_ln_b, L1_xattn_Wq, L1_xattn_Wk, L1_xattn_Wv, L1_xattn_Wo)
    return x

_drawn_inputs = setup_inputs


def setup_inputs(seed=0):
    import zlib

    import numpy as np

    out = dict(_drawn_inputs(seed))
    spreads = {'L0_xattn_bq': (0.0, 0.634),
     'L0_xattn_bk': (0.0, 0.8),
     'L0_xattn_bv': (0.0, 0.1),
     'L0_xattn_bo': (0.0, 0.1),
     'L0_xattn_gamma': (1.0, 0.2),
     'L0_xattn_beta': (0.0, 0.1),
     'L1_xattn_m_norm_w': (1.0, 0.2),
     'L1_xattn_conv_b': (0.0, 0.1),
     'L1_xattn_dt_bias': (-4.600165843963623, 0.6),
     'L1_xattn_D_skip': (1.0, 0.2),
     'L1_xattn_gnorm_w': (1.0, 0.2),
     'L1_xattn_ca_ln_w': (1.0, 0.6),
     'L1_xattn_ca_ln_b': (0.0, 0.8)}
    factors = {'L1_xattn_A_log': 8.0, 'L1_xattn_Wq': 8.0, 'L1_xattn_Wk': 8.0}
    for name, (base, spread) in spreads.items():
        noise = np.random.default_rng([zlib.crc32(name.encode()), seed]).standard_normal(out[name].shape)
        drawn = base * np.exp(spread * noise) if base else spread * noise
        out[name] = jnp.asarray(drawn.astype(out[name].dtype))
    for name, factor in factors.items():
        out[name] = (out[name] * factor).astype(out[name].dtype)
    return out
```

```python
from contextlib import ExitStack

import concourse.bass as bass
from concourse import mybir

F32 = mybir.dt.float32
F32R = mybir.dt.float32r
U8 = mybir.dt.uint8
ALU = mybir.AluOpType
ACT = mybir.ActivationFunctionType
AX_X = mybir.AxisListType.X

P = 128
D = 512
KT = D // P
S = 512
TQ = S // P
C = 77
H0, HD0 = 16, 32
H1, HD1 = 8, 64
HPT = P // HD0
DI = 1024
MI = DI // P
HM = 16
NS = 128
CONVD = DI + 2 * NS
TAPS = 4
EPS = 1e-5
CLAMP = 50.0
MASKED = -1.0e9
KV_TILE = 112
DT_COLS = 64

ENGINES = ("tensor", "scalar", "vector", "gpsimd", "sync")


class Region:

    def __init__(self, nc, ctx, name, rows, lags, tables=None):
        self.tables = tables
        self.spare = ctx.enter_context(nc.sbuf_tensor(f"{name}_spare", [1, TQ], F32))
        self.nc, self.ctx, self.name, self.rows, self.lags = nc, ctx, name, rows, lags
        self.queue = {e: [] for e in ENGINES}
        self.count = {}
        self.step = {}
        self.named = {}
        self.placed = {}
        self.places = 0

    def put(self, stage, engine, build, after=(), done=None, dma=None, apart=False, first=None):
        raised = None
        self.places += 1
        if done or dma:
            raised = dma or f"{stage}_{engine}"
            self.count[raised] = self.count.get(raised, 0) + 1
            self.step[raised] = 16 if dma else 1
            for n in [done] if isinstance(done, str) else (done or []):
                assert n not in self.named, n
                self.named[n] = (raised, self.count[raised])
                self.placed[n] = (stage, self.places)
            if dma:
                self.placed[dma] = (stage, self.places)
                self.named[dma] = (raised, self.count[raised])
        self.queue[engine].append((stage, build, list(after), raised, apart, first, self.places))

    def emit(self):
        nc, last = self.nc, max(self.lags.values())
        for q in self.queue.values():
            for stage, _, after, _, _, _, at in q:
                for a in after:
                    n, shift = (a, 0) if isinstance(a, str) else a
                    turns = self.lags[self.placed[n][0]] + shift - self.lags[stage]
                    assert turns < 0 or (turns == 0 and self.placed[n][1] < at), (n, shift, stage)
        sem = {s: self.ctx.enter_context(nc.semaphore(f"{self.name}_{s}")) for s in self.count}
        per = {s: self.count[s] * self.step[s] for s in self.count}
        block = self.ctx.enter_context(nc.Block())

        def turn(eng, q, t, stages):
            waited, base = {}, {}
            for stage, build, after, raised, apart, first, _ in q:
                if stage not in stages:
                    continue
                b = t - self.lags[stage]
                if first:
                    first(eng)
                for a in after:
                    name, shift = (a, 0) if isinstance(a, str) else a
                    s, k = self.named[name]
                    if s not in base:
                        base[s] = t * per[s] if isinstance(t, int) else eng.snap(t * per[s])
                    ahead = (1 + shift - self.lags[stage]) * per[s] + k * self.step[s]
                    if waited.get(s, -10 ** 9) >= ahead:
                        continue
                    waited[s] = ahead
                    eng.wait_ge(sem[s], base[s] + ahead)
                if apart is not False:
                    eng.memset(self.spare[:, apart:apart + 1], 0.0)
                ins = build(eng, b)
                if raised:
                    ins.then_inc(sem[raised], self.step[raised])

        def program(name):
            def body(eng):
                q = self.queue[name]
                if name == "scalar" and self.tables:
                    eng.preload_act_table_set(self.tables)
                if name == "sync":
                    for s in per:
                        eng.sem_inc(sem[s], per[s])
                for t in range(last):
                    turn(eng, q, t, [s for s, lag in self.lags.items() if lag <= t])
                if self.rows > last:
                    if self.rows - last == 1:
                        turn(eng, q, last, list(self.lags))
                    elif q:
                        with eng.Fori(last, self.rows) as t:
                            turn(eng, q, t, list(self.lags))
                for t in range(self.rows, self.rows + last):
                    turn(eng, q, t, [s for s, lag in self.lags.items() if t - lag < self.rows])
                if name == "sync":
                    for s in per:
                        if self.step[s] == 16:
                            eng.wait_ge(sem[s], (self.rows + 1) * per[s])
            return body

        for name in ENGINES:
            if self.queue[name] or name == "sync":
                getattr_block = {"tensor": block.tensor, "scalar": block.scalar, "vector": block.vector,
                                 "gpsimd": block.gpsimd, "sync": block.sync}[name]
                getattr_block(program(name))


def interleave(order, **steps):
    for c in order.replace(" ", ""):
        next(steps[c], None)
    for c, g in steps.items():
        rest = sum(1 for _ in g)
        assert rest == 0, (c, rest)


def mm3(eng, out, w, x, start=True, stop=True):
    eng.matmul(out, w[0], x[0], start=start, stop=False)
    eng.matmul(out, w[0], x[1], start=False, stop=False)
    return eng.matmul(out, w[1], x[0], start=False, stop=stop)


def row(b, n=1):
    return slice(b, b + n) if isinstance(b, int) else bass.ds(b, n)


def tiles(vector, width=P):
    return vector.rearrange("(m p) -> p m", p=width)


def spread(vector, parts=P):
    return vector.rearrange("(a n) -> a n", a=1).broadcast_to([parts, vector.shape[0]])


def root_guess(r, stage, v, y, after, tag):
    r.put(stage, "scalar", lambda e, b: e.activation(y, v, ACT.Ln), after=after, done=f"{tag}_ln")
    r.put(stage, "scalar", lambda e, b: e.activation(y, y, ACT.Exp, scale=-0.5), after=[f"{tag}_ln"], done=f"{tag}_0")


def root_refine(r, stage, v, y, t, tag):
    steps = (lambda e, b: e.tensor_tensor(t, y, y, ALU.mult),
             lambda e, b: e.tensor_tensor(t, t, v, ALU.mult),
             lambda e, b: e.tensor_scalar(t, t, -0.5, 1.5, ALU.mult, ALU.add),
             lambda e, b: e.tensor_tensor(y, y, t, ALU.mult))
    for n, op in enumerate(steps):
        r.put(stage, "vector", op, after=[f"{tag}_{n}"], done=f"{tag}_{n + 1}" if n < 3 else tag)


def keys_values(nc, a, scratch):
    with ExitStack() as ctx:
        def sb(name, shape, dt=F32):
            return ctx.enter_context(nc.sbuf_tensor(f"kv_{name}", shape, dt))
        rows = a["ctxT"].shape[1] // KV_TILE
        wk = [sb(f"wk{l}", [P, KT, D]) for l in range(2)]
        wv_raw = [sb(f"wv{l}", [P, KT, D]) for l in range(2)]
        wv = [[sb(f"wv{l}{h}", [P, KT, D], F32R) for h in "hl"] for l in range(2)]
        bk, bv = sb("bk", [P, KT]), sb("bv", [P, D])
        x_in, x_f = sb("x_in", [P, KT, KV_TILE]), sb("x_f", [P, KT, KV_TILE])
        x_s = [sb(f"x_{h}", [P, KT, KV_TILE], F32R) for h in "hl"]
        k0f = sb("k0f", [P, KT, KV_TILE])
        k0s = [sb(f"k0{h}", [P, KT, KV_TILE], F32R) for h in "hl"]
        k1s = sb("k1s", [P, KT, KV_TILE])
        v_s = [sb(f"v{l}", [KV_TILE, D]) for l in range(2)]
        ps = ctx.enter_context(nc.psum_tensor("kv_ps", [P, 8, 512], F32))

        with ExitStack() as c2:
            w = Region(nc, c2, "kvw", 1, {"W": 0})
            for l in range(2):
                w.put("W", "sync", lambda e, b, l=l: e.dma_start(wv_raw[l][:], a[f"Wv{l}"].rearrange("(k p) n -> p k n", p=P)), dma=f"wv{l}")
                w.put("W", "scalar", lambda e, b, l=l: e.dma_start(wk[l][:], a[f"Wk{l}"].rearrange("(k p) n -> p k n", p=P)), dma=f"wk{l}")
            w.put("W", "sync", lambda e, b: e.dma_start(bk[:], tiles(a["bk0"]), allow_slow_non_contiguous=True), dma="bk")
            w.put("W", "sync", lambda e, b: e.dma_start(bv[:], spread(a["bv0"])), dma="bv")
            for l in range(2):
                w.put("W", "scalar", lambda e, b, l=l: e.activation(wv[l][0][:], wv_raw[l][:], ACT.Copy), after=[f"wv{l}"], done=f"wvh{l}")
                w.put("W", "vector", lambda e, b, l=l: e.tensor_tensor(wv[l][1][:], wv_raw[l][:], wv[l][0][:].bitcast(F32), ALU.subtract), after=[f"wvh{l}", f"wv{l}"], done=f"wvl{l}")
            w.emit()

        with ExitStack() as c2:
            r = Region(nc, c2, "kv", rows, {"T": 0})
            put = lambda *p, **k: r.put("T", *p, **k)
            put("sync", lambda e, b: e.dma_start(x_in[:], a["ctxT"].rearrange("(k p) t -> p k t", p=P)[:, :, row(b * KV_TILE, KV_TILE)]),
                after=[("xf", -1), ("xl", -1)], dma="x")
            put("scalar", lambda e, b: e.activation(x_s[0][:], x_in[:], ACT.Copy), after=["x", ("V1", -1)], done="xh")
            put("vector", lambda e, b: e.tensor_tensor(x_s[1][:], x_in[:], x_s[0][:].bitcast(F32), ALU.subtract), after=["xh"], done="xl")
            put("vector", lambda e, b: e.tensor_copy(x_f[:], x_in[:]), after=["x", ("K1", -1)], done="xf")
            for l in range(2):
                for k in range(KT):
                    put("tensor", lambda e, b, l=l, k=k: mm3(e, ps[0:KV_TILE, l, :], [x_s[0][:, k, :], x_s[1][:, k, :]],
                        [wv[l][0][:, k, :], wv[l][1][:, k, :]], k == 0, k == KT - 1),
                        after=["xl", (f"v{l}", -1)], done=f"V{l}" if k == KT - 1 else None)
            for l in range(2):
                for m in range(KT):
                    for k in range(KT):
                        put("tensor", lambda e, b, l=l, m=m, k=k: e.matmul(ps[:, 2 + l, m * KV_TILE:(m + 1) * KV_TILE],
                            wk[l][:, k, m * P:(m + 1) * P], x_f[:, k, :], start=(k == 0), stop=(k == KT - 1)),
                            after=["xf", (("k0f", "k1")[l], -1)], done=f"K{l}" if (m, k) == (KT - 1, KT - 1) else None)
            put("vector", lambda e, b: e.tensor_tensor(v_s[0][:], ps[0:KV_TILE, 0, :], bv[0:KV_TILE, :], ALU.add), after=["V0", ("v0_out", -1)], done="v0")
            put("scalar", lambda e, b: e.activation(v_s[1][:], ps[0:KV_TILE, 1, :], ACT.Copy), after=["V1", ("v1_out", -1)], done="v1")
            put("vector", lambda e, b: e.tensor_tensor(k0f[:], ps[:, 2, 0:KT * KV_TILE].rearrange("p (m t) -> p m t", m=KT),
                bk[:].unsqueeze(2).broadcast_to([P, KT, KV_TILE]), ALU.add), after=["K0", ("k0l", -1)], done="k0f")
            put("scalar", lambda e, b: e.activation(k0s[0][:], k0f[:], ACT.Copy), after=["k0f", ("k0h_out", -1)], done="k0h")
            put("vector", lambda e, b: e.tensor_tensor(k0s[1][:], k0f[:], k0s[0][:].bitcast(F32), ALU.subtract), after=["k0h", ("k0l_out", -1)], done="k0l")
            put("scalar", lambda e, b: e.activation(k1s[:], ps[:, 3, 0:KT * KV_TILE].rearrange("p (m t) -> p m t", m=KT), ACT.Copy), after=["K1", ("k1_out", -1)], done="k1")
            for l in range(2):
                put("sync", lambda e, b, l=l: e.dma_start(scratch[f"v{l}"][row(b * KV_TILE, KV_TILE), :], v_s[l][:]), after=[f"v{l}"], dma=f"v{l}_out")
            for n, t in (("k0h", k0s[0][:].bitcast(F32)), ("k0l", k0s[1][:].bitcast(F32)), ("k1", k1s[:])):
                put("sync", lambda e, b, n=n, t=t: e.dma_start(scratch[n].rearrange("m p t -> p m t")[:, :, row(b * KV_TILE, KV_TILE)], t),
                    after=[n], dma=f"{n}_out")
            r.emit()


def layer0(nc, a, scratch, rows):
    with ExitStack() as ctx:
        def sb(name, shape, dt=F32):
            return ctx.enter_context(nc.sbuf_tensor(f"l0_{name}", shape, dt))
        wq, wo = ([sb(f"{n}{h}", [P, KT, D], F32R) for h in "hl"] for n in ("wq", "wo"))
        bq, bo, gamma, beta = sb("bq", [P, KT]), sb("bo", [P, D]), sb("gamma", [P, D]), sb("beta", [P, D])
        ones = sb("ones", [C, HD0])
        x_in = sb("x_in", [P, KT, S])
        xs = [sb(f"x{h}", [P, KT, S], F32R) for h in "hl"]
        qs = [sb(f"q{h}", [P, KT, S], F32R) for h in "hl"]
        kp = [sb(f"k{h}", [P, H0, C], F32R) for h in "hl"]
        v = sb("v", [C, D])
        m_in, mf = sb("m_in", [C, S]), sb("mf", [C, S])
        sc = sb("sc", [C, 4, S])
        pt = sb("pt", [C, H0, S])
        lg, rd, nr = sb("lg", [P, S]), sb("rd", [P, S]), sb("nr", [P, S])
        cn = sb("cn", [P, S])
        cs = [sb(f"c{h}", [P, KT, S], F32R) for h in "hl"]
        xb = sb("xb", [P, TQ, D])
        y = sb("y", [P, TQ, D])
        sq = sb("sq", [P, D])
        st, mv = sb("st", [P, TQ, 6]), sb("mv", [P, TQ, 2])
        var, rstd, tmp = sb("var", [P, TQ]), sb("rstd", [P, TQ]), sb("tmp", [P, TQ])
        ms, rms, rinv, tmp2 = sb("ms", [P, TQ]), sb("rms", [P, TQ]), sb("rinv", [P, TQ]), sb("tmp2", [P, TQ])
        ps = ctx.enter_context(nc.psum_tensor("l0_ps", [P, 8, 512], F32))

        with ExitStack() as c2:
            w = Region(nc, c2, "l0w", 1, {"W": 0})
            put = lambda *p, **k: w.put("W", *p, **k)
            split_weights(w, [("wq", a["Wq0"].rearrange("(k p) n -> p k n", p=P), x_in, wq, HD0 ** -0.5, None),
                              ("wo", a["Wo0"].rearrange("(k p) n -> p k n", p=P), y, wo, 1.0, None)])
            put("sync", lambda e, b: e.dma_start(bq[:], tiles(a["bq0"]), allow_slow_non_contiguous=True), dma="bq")
            put("scalar", lambda e, b: e.dma_start(bo[:], spread(a["bo0"])), dma="bo")
            put("scalar", lambda e, b: e.dma_start(gamma[:], spread(a["gamma0"])), dma="gamma")
            put("scalar", lambda e, b: e.dma_start(beta[:], spread(a["beta0"])), dma="beta")
            put("gpsimd", lambda e, b: e.memset(ones[:], 1.0), done="ones")
            put("gpsimd", lambda e, b: e.memset(kp[0][:].bitcast(F32), 0.0), done="kz0")
            put("gpsimd", lambda e, b: e.memset(kp[1][:].bitcast(F32), 0.0), done="kz1")
            put("vector", lambda e, b: e.tensor_scalar(bq[:], bq[:], HD0 ** -0.5, None, ALU.mult), after=["bq"], done="bqs")
            w.emit()

        with ExitStack() as c2:
            r = Region(nc, c2, "l0", rows, {"X": 0, "A": 1, "B": 2}, "natural_log_exp_and_others")

            def load_split():
                put = lambda *p, **k: r.put("X", *p, **k)
                put("sync", lambda e, b: e.dma_start(x_in[:], a["xT"].rearrange("b (k p) t -> b p k t", p=P)[row(b)].rearrange("b p k t -> (b p) k t")),
                    after=[("xl3", -1)], dma="x_in")
                for k in range(KT):
                    put("scalar" if k % 2 else "vector",
                        (lambda e, b, k=k: e.activation(xs[0][:, k, :], x_in[:, k, :], ACT.Copy)) if k % 2 else
                        (lambda e, b, k=k: e.tensor_copy(xs[0][:, k, :], x_in[:, k, :])),
                        after=["x_in", ("q3", -1)], done=f"xh{k}")
                    put("gpsimd", lambda e, b, k=k: e.tensor_tensor(xs[1][:, k, :], x_in[:, k, :], xs[0][:, k, :].bitcast(F32), ALU.subtract),
                        after=[f"xh{k}", ("q3", -1)], done=f"xl{k}")
                yield

            def scores():
                put = lambda *p, **k: r.put("A", *p, **k)
                for n, s in enumerate(("k0h", "k0l")):
                    for j in range(HPT):
                        src = scratch[s].rearrange("m p t -> p m t")[j * HD0:(j + 1) * HD0]
                        dst = kp[n][j * HD0:(j + 1) * HD0, :, :].bitcast(F32).rearrange("p (m j) t -> p m j t", j=HPT)[:, :, j, :]
                        put("sync", lambda e, b, src=src, dst=dst: e.dma_start(dst, src[:, :, row(b * C, C)]),
                            after=[(f"S{H0 - 1}", -1)], dma=f"kp{n}{j}")
                put("sync", lambda e, b: e.dma_start(m_in[:], a["maskT"][row(b)].rearrange("b c t -> (b c) t")), after=[("mf", -1)], dma="m_in")
                put("vector", lambda e, b: e.tensor_scalar(mf[:], m_in[:], 0.5, 0.5, ALU.mult, ALU.add),
                    after=["m_in", (f"mul{H0 - 1}", -1)], done="mf")
                for m in range(KT):
                    for k in range(KT):
                        put("tensor", lambda e, b, m=m, k=k: mm3(e, ps[:, m, :], [w_[:, k, m * P:(m + 1) * P] for w_ in wq],
                            [x_[:, k, :] for x_ in xs], k == 0, k == KT - 1),
                            after=[f"xl{k}", f"xh{k}", (f"mul{12 + m}", -1)], done=f"q{m}" if k == KT - 1 else None)
                    put("scalar", lambda e, b, m=m: e.activation(qs[0][:, m, :], ps[:, m, :], ACT.Identity, bias=bq[:, m:m + 1]),
                        after=[f"q{m}", (f"S{4 * m + 3}", -1)], done=f"qh{m}")
                    put("vector", lambda e, b, m=m: e.scalar_tensor_tensor(out=qs[1][:, m, :], in0=ps[:, m, :], scalar=bq[:, m:m + 1],
                        in1=qs[0][:, m, :].bitcast(F32), op0=ALU.add, op1=ALU.subtract), after=[f"qh{m}"], done=f"ql{m}")
                    yield
                for h in range(H0):
                    m = h // HPT
                    free = f"ql{h}" if h < 4 else f"mul{h - 4}"
                    keys = [f"kp{n}{j}" for n in range(2) for j in range(HPT)] if h == 0 else []
                    put("tensor", lambda e, b, h=h, m=m: mm3(e, ps[0:C, h % 4, :], [k_[:, h, :] for k_ in kp], [q_[:, m, :] for q_ in qs]),
                        after=[f"ql{m}", free] + keys, done=f"S{h}")
                    put("vector", lambda e, b, h=h: e.tensor_tensor(sc[:, h % 4, :], ps[0:C, h % 4, :], mf[:], ALU.mult),
                        after=[f"S{h}", "mf", f"exp{h - 4}" if h >= 4 else (f"exp{12 + h}", -1)], done=f"mul{h}")
                    put("vector", lambda e, b, h=h: e.tensor_scalar(sc[:, h % 4, :], sc[:, h % 4, :], CLAMP, -CLAMP, ALU.min, ALU.max),
                        after=[f"mul{h}"], done=f"clip{h}")
                    put("scalar", lambda e, b, h=h: e.activation(pt[:, h, :], sc[:, h % 4, :], ACT.Exp),
                        after=[f"clip{h}", (f"pv{m}", -1)], done=f"exp{h}")
                    yield

            def values_out():
                put = lambda *p, **k: r.put("B", *p, **k)
                put("sync", lambda e, b: e.dma_start(v[:], scratch["v0"][row(b * C, C), :]), after=[("pv3", -1)], dma="v")
                put("sync", lambda e, b: e.dma_start(xb[:], a["x"].rearrange("b (q p) d -> b p q d", p=P)[row(b)].rearrange("b p q d -> (b p) q d")),
                    after=[("r3", -1)], dma="x_tok")
                for m in range(KT):
                    for j in range(HPT):
                        h = HPT * m + j
                        put("tensor", lambda e, b, j=j, h=h: e.matmul(ps[j * HD0:(j + 1) * HD0, 4, :], v[:, h * HD0:(h + 1) * HD0], pt[:, h, :], start=True, stop=True),
                            after=["v", f"exp{h}", f"cn{m - 1}" if m else ("cn3", -1)])
                    for j in range(HPT):
                        h = HPT * m + j
                        put("tensor", lambda e, b, j=j, h=h: e.matmul(ps[j * HD0:(j + 1) * HD0, 5, :], ones[:], pt[:, h, :], start=True, stop=True),
                            done=f"pv{m}" if j == HPT - 1 else None)
                    put("scalar", lambda e, b: e.activation(lg[:], ps[:, 5, :], ACT.Ln), after=[f"pv{m}"], done=f"lg{m}")
                    put("scalar", lambda e, b: e.activation(rd[:], lg[:], ACT.Exp, scale=-1.0),
                        after=[f"lg{m}", f"nr{m - 1}" if m else ("nr3", -1)], done=f"rd{m}")
                    yield
                    put("vector", lambda e, b: e.tensor_tensor(nr[:], ps[:, 5, :], rd[:], ALU.mult), after=[f"rd{m}"], done=f"sg{m}")
                    put("vector", lambda e, b: e.scalar_tensor_tensor(out=nr[:], in0=nr[:], scalar=2.0, in1=rd[:], op0=ALU.subtract, op1=ALU.mult),
                        after=[f"sg{m}"], done=f"nr{m}")
                    put("vector", lambda e, b: e.scalar_tensor_tensor(out=cn[:], in0=ps[:, 4, :], scalar=-1.0, in1=nr[:], op0=ALU.mult, op1=ALU.mult),
                        after=[f"nr{m}", f"cl{m - 1}" if m else ("cl3", -1)], done=f"cn{m}")
                    put("scalar", lambda e, b, m=m: e.activation(cs[0][:, m, :], cn[:], ACT.Copy), after=[f"cn{m}", ("o3", -1)], done=f"ch{m}")
                    put("gpsimd", lambda e, b, m=m: e.tensor_tensor(cs[1][:, m, :], cn[:], cs[0][:, m, :].bitcast(F32), ALU.subtract),
                        after=[f"ch{m}"], done=f"cl{m}")
                    put("gpsimd", lambda e, b, m=m: e.tensor_tensor(xb[:, m, :], xb[:, m, :], bo[:], ALU.add), after=["x_tok"], done=f"xb{m}")
                    yield
                for q in range(TQ):
                    for k in range(KT):
                        put("tensor", lambda e, b, q=q, k=k: mm3(e, ps[:, 6 + q % 2, :], [c_[:, k, q * P:(q + 1) * P] for c_ in cs],
                            [w_[:, k, :] for w_ in wo], k == 0, k == KT - 1),
                            after=["cl3", f"r{q - 2}" if q >= 2 else (f"r{q + 2}", -1)], done=f"o{q}" if k == KT - 1 else None)
                    put("vector", lambda e, b, q=q: e.tensor_tensor(y[:, q, :], ps[:, 6 + q % 2, :], xb[:, q, :], ALU.add),
                        after=[f"o{q}", f"xb{q}", ("y_out", -1), (f"sq{q}", -1)], done=f"r{q}")
                    put("vector", lambda e, b, q=q: e.bn_stats(st[:, q, :], y[:, q, :]), after=[f"r{q}"], done=f"st{q}")
                    put("vector", lambda e, b, q=q: e.bn_aggr(mv[:, q, :], st[:, q, :]), after=[f"st{q}"], done=f"mv{q}", apart=q)
                    yield
                put("vector", lambda e, b: e.tensor_scalar(var[:], mv[:, :, 1], EPS, None, ALU.add), after=["mv3"], done="var")
                root_guess(r, "B", var[:], rstd[:], ["var"], "rstd")
                yield
                root_refine(r, "B", var[:], rstd[:], tmp[:], "rstd")
                for q in range(TQ):
                    put("vector", lambda e, b, q=q: e.tensor_scalar(y[:, q, :], y[:, q, :], mv[:, q, 0:1], rstd[:, q:q + 1], ALU.subtract, ALU.mult),
                        after=["rstd"], done=f"n{q}")
                    put("gpsimd", lambda e, b, q=q: e.tensor_tensor(y[:, q, :], y[:, q, :], gamma[:], ALU.mult), after=[f"n{q}"], done=f"g{q}")
                    put("gpsimd", lambda e, b, q=q: e.tensor_tensor(y[:, q, :], y[:, q, :], beta[:], ALU.add), after=[f"g{q}"], done=f"y{q}")
                yield
                put("scalar", lambda e, b: e.dma_start(scratch["y"][row(b)].rearrange("b p q d -> (b p) q d"), y[:]), after=["y3"], dma="y_out")
                for q in range(TQ):
                    put("scalar", lambda e, b, q=q: e.activation(sq[:], y[:, q, :], ACT.Square, scale=D ** -0.5, accum_out=ms[:, q:q + 1]),
                        after=[f"y{q}", f"sq{q - 1}" if q else ("sq3", -1)] + ([("rms", -1)] if q == 0 else []), done=f"sq{q}")
                put("vector", lambda e, b: e.tensor_scalar(rms[:], ms[:], EPS, None, ALU.add), after=["sq3"], done="rms")
                root_guess(r, "B", rms[:], rinv[:], ["rms", ("rinv_out", -1)], "rinv")
                yield
                root_refine(r, "B", rms[:], rinv[:], tmp2[:], "rinv")
                put("scalar", lambda e, b: e.dma_start(scratch["rinv"][row(b)].rearrange("b p q -> (b p) q"), rinv[:]), after=["rinv"], dma="rinv_out")
                yield

            interleave("B AB AB AB AB BBB X AA B AA B AA B AA B AAA B A B AA B A B A", A=scores(), B=values_out(), X=load_split())
            r.emit()


def split_weights(w, items):
    for name, src, raw, (hi, lo), number, column in items:
        n = src.shape[2]
        w.put("W", "sync", lambda e, b, src=src, raw=raw, n=n: e.dma_start(raw[:, :, 0:n] if raw.shape[2] != n else raw[:], src), dma=name)
        for k in range(src.shape[1]):
            w.put("W", "vector", lambda e, b, k=k, raw=raw, n=n, number=number, column=column: e.tensor_scalar(
                raw[:, k, 0:n], raw[:, k, 0:n], number, None if column is None else column[:, k:k + 1],
                ALU.mult, ALU.bypass if column is None else ALU.mult),
                after=[name] + ([] if column is None else ["columns"]), done=f"{name}_s{k}")
            w.put("W", "scalar", lambda e, b, k=k, raw=raw, n=n, hi=hi: e.activation(hi[:, k, 0:n], raw[:, k, 0:n], ACT.Copy),
                  after=[f"{name}_s{k}"], done=f"{name}_h{k}")
            w.put("W", "vector", lambda e, b, k=k, raw=raw, n=n, hi=hi, lo=lo: e.tensor_tensor(
                lo[:, k, 0:n], raw[:, k, 0:n], hi[:, k, 0:n].bitcast(F32), ALU.subtract), after=[f"{name}_h{k}"], done=f"{name}_l{k}")


def mamba(nc, a, scratch, rows):
    XC, BC, CC, DC = DI, 2 * DI, 2 * DI + NS, 2 * DI + 2 * NS
    NCONV = CONVD // P
    with ExitStack() as ctx:
        def sb(name, shape, dt=F32):
            return ctx.enter_context(nc.sbuf_tensor(f"mb_{name}", shape, dt))
        wi = [sb(f"wi{h}", [P, KT, DC + P], F32R) for h in "hl"]
        wo = sb("wo", [P, MI, D])
        cw, cb, skip = sb("cw", [P, NCONV, TAPS]), sb("cb", [P, NCONV]), sb("skip", [P, MI])
        dtb, am = sb("dtb", [P, 1]), sb("am", [P, 1])
        eye, eyes = sb("eye", [P, P]), sb("eyes", [P, TQ, P])
        ones = sb("ones", [P, P])
        sel = sb("sel", [P, HM], F32R)
        selp = sb("selp", [P, MI, P], F32R)
        xp = sb("xp", [P, 2, TQ, 2 * P])
        d1 = sb("d1", [P, S])
        ps = ctx.enter_context(nc.psum_tensor("mb_ps", [P, 8, 512], F32))

        with ExitStack() as c2:
            raw = c2.enter_context(nc.sbuf_tensor("mb_raw", [P, KT, DC + HM], F32))
            nw, gw = c2.enter_context(nc.sbuf_tensor("mb_nw", [P, KT], F32)), c2.enter_context(nc.sbuf_tensor("mb_gw", [P, MI], F32))
            sel_f = c2.enter_context(nc.sbuf_tensor("mb_self", [P, HM], F32))
            w = Region(nc, c2, "mbw", 1, {"W": 0})
            put = lambda *p, **k: w.put("W", *p, **k)
            put("scalar", lambda e, b: e.dma_start(nw[:], tiles(a["norm1"]), allow_slow_non_contiguous=True), dma="columns")
            put("scalar", lambda e, b: e.dma_start(gw[:], tiles(a["gnorm1"]), allow_slow_non_contiguous=True), dma="gw")
            for n in range(2):
                put("vector", lambda e, b, n=n: e.memset(wi[n][:, :, DC:].bitcast(F32), 0.0), done=f"wz{n}")
            split_weights(w, [("wi", a["Win"].rearrange("(k p) n -> p k n", p=P), raw, wi, 1.0, nw)])
            for k in range(KT):
                again = slice(DC + 32, DC + 32 + HM)
                put("scalar", lambda e, b, k=k: e.activation(wi[0][:, k, again], raw[:, k, DC:DC + HM], ACT.Copy), after=[f"wi_s{k}", "wz1"], done=f"dh{k}")
                put("vector", lambda e, b, k=k: e.tensor_tensor(wi[1][:, k, again], raw[:, k, DC:DC + HM], wi[0][:, k, again].bitcast(F32), ALU.subtract),
                    after=[f"dh{k}"], done=f"dl{k}")
            put("sync", lambda e, b: e.dma_start(wo[:], a["Wout"].rearrange("(k p) n -> p k n", p=P)), dma="wo")
            for k in range(MI):
                put("gpsimd", lambda e, b, k=k: e.tensor_tensor(wo[:, k, :], wo[:, k, :], gw[:, k:k + 1].broadcast_to([P, D]), ALU.mult), after=["wo", "gw"])
            put("sync", lambda e, b: e.dma_start(cw[:], a["cw"].rearrange("(j p) k -> p j k", p=P)), dma="cw")
            put("scalar", lambda e, b: e.dma_start(cb[:], tiles(a["cb"]), allow_slow_non_contiguous=True), dma="cb")
            put("sync", lambda e, b: e.dma_start(eye[:], a["eye"]), dma="eye")
            for c in range(TQ):
                put("sync", lambda e, b, c=c: e.dma_start(eyes[:, c, :], a["eye"]), dma=f"eyes{c}")
            for j in range(2):
                put("scalar", lambda e, b, j=j: e.dma_start(skip[j * 64:(j + 1) * 64, :], a["skip"].rearrange("(m j) -> j m", j=2)[j:j + 1, :].broadcast_to([64, MI]),
                    allow_slow_non_contiguous=True), dma=f"skip{j}")
            put("vector", lambda e, b: e.memset(dtb[:], 0.0), done="z0")
            put("vector", lambda e, b: e.memset(am[:], 0.0), done="z1")
            put("vector", lambda e, b: e.memset(sel_f[:], 0.0), done="z2")
            put("vector", lambda e, b: e.memset(ones[:], 1.0))
            put("vector", lambda e, b: e.memset(d1[:], 0.0))
            put("gpsimd", lambda e, b: e.memset(xp[:], 0.0))
            for n, at in enumerate((0, 32)):
                put("sync", lambda e, b, at=at: e.dma_start(dtb[at:at + HM, :], a["dtb"].rearrange("(n a) -> n a", a=1)), after=["z0"], dma=f"dtb{n}")
                put("sync", lambda e, b, at=at: e.dma_start(am[at:at + HM, :], a["alog"].rearrange("(n a) -> n a", a=1)), after=["z1"], dma=f"am{n}")
                put("sync", lambda e, b, at=at: e.dma_start(sel_f[at:at + HM, :], a["eye"][0:HM, 0:HM]), after=["z2"], dma=f"sel{n}")
            put("scalar", lambda e, b: e.activation(sel[:], sel_f[:], ACT.Copy), after=["sel0", "sel1"])
            put("scalar", lambda e, b: e.activation(selp[:].rearrange("p m (j d) -> p (m j) d", j=2), sel_f[:].unsqueeze(2).broadcast_to([P, HM, 64]), ACT.Copy),
                after=["sel0", "sel1"])
            for n, at in enumerate((0, 32)):
                put("scalar", lambda e, b, at=at: e.activation(am[at:at + HM, :], am[at:at + HM, :], ACT.Exp), after=[f"am{n}"], done=f"ae{n}")
                put("vector", lambda e, b, at=at: e.tensor_scalar(am[at:at + HM, :], am[at:at + HM, :], -1.0, None, ALU.mult), after=[f"ae{n}"])
            w.emit()

        y = sb("y", [P, 2, D])
        ri = sb("ri", [P, TQ])
        yt = [sb(f"y{h}", [P, KT, S], F32R) for h in "hl"]
        cv, xs, sz = sb("cv", [P, 2, S]), sb("xs", [P, 2, S]), sb("sz", [P, 2, S])
        lm, gm = sb("lm", [P, 2, S]), sb("gm", [P, 2, 2, S])
        xw = sb("xw", [P, 2, TQ - 1, P])
        pb, hs, yw = sb("pb", [P, S]), sb("hs", [P, TQ - 1, P]), sb("yw", [P, S])
        u, sq, ssq = sb("u", [P, MI, S]), sb("sq", [P, S]), sb("ssq", [P, S])
        bt, ct, bk, g = sb("bt", [P, S]), sb("ct", [P, S]), sb("bk", [P, TQ, P]), sb("g", [P, S])
        v, ex, ul = sb("v", [P, S]), sb("ex", [P, S]), sb("ul", [P, S])
        dec2, pre2 = sb("dec2", [P, S], F32R), sb("pre2", [P, S], F32R)
        dtT, dg, dl = sb("dtT", [P, TQ, HM]), sb("dg", [HM, TQ, HM]), sb("dl", [P, TQ, HM])
        o, so = sb("o", [P, 2, D]), sb("so", [P, TQ])
        starts, ends = slice(0, S, P), slice(P - 1, S, P)

        with ExitStack() as c2:
            r = Region(nc, c2, "mb", rows, {"A": 0, "P": 1, "S": 1, "O": 1})

            def project(put, tag, bank, column, after):
                for k in range(KT):
                    put("tensor", lambda e, b, k=k: mm3(e, ps[:, bank, :], [w_[:, k, column:column + P] for w_ in wi],
                        [y_[:, k, :] for y_ in yt], k == 0, k == KT - 1), after=after, done=tag if k == KT - 1 else None)

            def convolve(put, tag, bank, j, ring, free):
                last = TAPS - 1
                put("scalar", lambda e, b: e.activation(cv[:, ring, :], ps[:, bank, :], ACT.Identity, bias=cb[:, j:j + 1], scale=cw[:, j, last:last + 1]),
                    after=[tag, free], done=f"{tag}_t{last}")
                for k in reversed(range(last)):
                    n = last - k
                    put("vector", lambda e, b, k=k, n=n: e.scalar_tensor_tensor(out=cv[:, ring, n:S], in0=ps[:, bank, 0:S - n], scalar=cw[:, j, k:k + 1],
                        in1=cv[:, ring, n:S], op0=ALU.mult, op1=ALU.add), after=[f"{tag}_t{k + 1}"], done=f"{tag}_t{k}")

            def prepare():
                put = lambda *p, **k: r.put("A", *p, **k)
                put("sync", lambda e, b: e.dma_start(ri[:], scratch["rinv"][row(b)].rearrange("b p q -> (b p) q")), after=[("ys3", -1)], dma="ri")
                for q in range(TQ):
                    put("sync", lambda e, b, q=q: e.dma_start(y[:, q % 2, :], scratch["y"][row(b), :, q, :].rearrange("b p d -> (b p) d")),
                        after=[f"yt{q - 2}" if q >= 2 else (f"yt{q + 2}", -1)], dma=f"y{q}")
                    put("vector", lambda e, b, q=q: e.tensor_scalar(y[:, q % 2, :], y[:, q % 2, :], ri[:, q:q + 1], None, ALU.mult), after=["ri", f"y{q}"], done=f"ys{q}")
                    for k in range(KT):
                        put("tensor", lambda e, b, q=q, k=k: e.transpose(ps[:, q % 2, k * P:(k + 1) * P], y[:, q % 2, k * P:(k + 1) * P], eye[:]),
                            after=[f"ys{q}"] + ([f"yl{q - 2}"] if q >= 2 else [("sz7", -1), ("x7_t0", -1)]),
                            done=f"yt{q}" if k == KT - 1 else None)
                    cols = slice(q * P, (q + 1) * P)
                    src = ps[:, q % 2, :].rearrange("p (k t) -> p k t", k=KT)
                    put("scalar", lambda e, b, cols=cols, src=src: e.activation(yt[0][:, :, cols], src, ACT.Copy), after=[f"yt{q}", ("z7", -1)], done=f"yh{q}")
                    put("vector", lambda e, b, cols=cols, src=src: e.tensor_tensor(yt[1][:, :, cols], src, yt[0][:, :, cols].bitcast(F32), ALU.subtract),
                        after=[f"yh{q}"], done=f"yl{q}")
                    if q % 2:
                        yield
                project(put, "dt", 2, DC, ["yl3", ("xp7", -1), ("dl", -1)])
                put("vector", lambda e, b: e.tensor_scalar(v[:], ps[:, 2, :], dtb[:, 0:1], None, ALU.add), after=["dt", ("dlm", -1)], done="v")
                put("vector", lambda e, b: e.scalar_tensor_tensor(out=ex[:], in0=v[:], scalar=-1.0, in1=v[:], op0=ALU.mult, op1=ALU.min), after=["v", ("dec", -1), ("d1", -1)], done="na")

                put("scalar", lambda e, b: e.activation(ex[:], ex[:], ACT.Exp), after=["na"], done="e",
                    first=lambda e: e.preload_act_table_set("natural_log_exp_and_others"))
                put("vector", lambda e, b: e.tensor_scalar(ul[:], ex[:], 1.0, None, ALU.add), after=["e"], done="1e")
                put("vector", lambda e, b: e.scalar_tensor_tensor(out=ex[:], in0=ul[:], scalar=1.0, in1=ex[:], op0=ALU.subtract, op1=ALU.subtract), after=["1e"], done="lost")
                put("scalar", lambda e, b: e.activation(ul[:], ul[:], ACT.Ln), after=["lost"], done="ln")
                put("vector", lambda e, b: e.tensor_tensor(ul[:], ul[:], ex[:], ALU.subtract), after=["ln"], done="l1")
                put("vector", lambda e, b: e.scalar_tensor_tensor(out=v[:], in0=v[:], scalar=0.0, in1=ul[:], op0=ALU.max, op1=ALU.add), after=["l1"], done="dtv")
                put("scalar", lambda e, b: e.activation(ex[:], v[:], ACT.Exp, scale=am[:, 0:1]), after=["dtv"], done="dec")
                yield
                for n, (tag, col, dst) in enumerate((("C", CC, ct), ("B", BC, bt))):
                    project(put, tag, n, col, ["yl2", "yl3"])
                    convolve(put, tag, n, (col - XC) // P, n, ("xs%d" % (6 + n), -1))
                    put("scalar", lambda e, b, n=n, dst=dst: e.activation(dst[:], cv[:, n, :], ACT.Silu),
                        after=[f"{tag}_t0", ("Yo7", -1), ("G", -1), ("bT", -1)], done=tag + "s")
                    yield
                put("vector", lambda e, b: e.tensor_copy(d1[:, starts], ex[:, starts]), after=["dec"], done="d1")
                put("vector", lambda e, b: e.memset(ex[:, starts], 0.0), after=["d1"], done="dec0")
                put("vector", lambda e, b: e.tensor_copy(dec2[:], ex[:]), after=["dec0", ("L15", -1)], done="dech")
                put("vector", lambda e, b: e.tensor_tensor(dec2[32:64, :], ex[32:64, :], dec2[32:64, :].bitcast(F32), ALU.subtract), after=["dech"], done="dec2")
                put("vector", lambda e, b: e.tensor_tensor_scan(ul[:], ex[:], d1[:], 0.0, ALU.mult, ALU.add), after=["dec0"], done="pre")
                put("vector", lambda e, b: e.tensor_copy(pre2[:], ul[:]), after=["pre", ("Pb7", -1)], done="preh")
                put("vector", lambda e, b: e.tensor_tensor(pre2[32:64, :], ul[32:64, :], pre2[32:64, :].bitcast(F32), ALU.subtract), after=["preh"], done="pre2")
                put("vector", lambda e, b: e.tensor_tensor(dg[:], eye[0:HM, 0:HM].unsqueeze(1).broadcast_to([HM, TQ, HM]),
                    ul[0:HM, ends].unsqueeze(2).broadcast_to([HM, TQ, HM]), ALU.mult), after=["pre", ("dlm", -1)], done="dg")
                put("tensor", lambda e, b: e.matmul(ps[:, 2, TQ * HM:2 * TQ * HM], ones[0:HM, :], dg[:], start=True, stop=True), after=["v", "dtv", "dg"])
                for c in range(TQ):
                    put("tensor", lambda e, b, c=c: e.transpose(ps[:, 2, c * HM:(c + 1) * HM], v[0:HM, c * P:(c + 1) * P], eye[0:HM, 0:HM]),
                        done="dlm" if c == TQ - 1 else None)
                put("vector", lambda e, b: e.tensor_copy(dtT[:], ps[:, 2, 0:TQ * HM].rearrange("p (c h) -> p c h", c=TQ)), after=["dlm", ("xp7", -1)], done="dtT")
                put("vector", lambda e, b: e.tensor_copy(dl[:], ps[:, 2, TQ * HM:2 * TQ * HM].rearrange("p (c h) -> p c h", c=TQ)), after=["dlm", ("H7", -1)], done="dl")
                for c in range(TQ):
                    put("tensor", lambda e, b, c=c: e.matmul(ps[:, 0, c * P:(c + 1) * P], bt[:, c * P:(c + 1) * P], ct[:, c * P:(c + 1) * P], start=True, stop=True),
                        after=["Cs", "Bs", "C_t0"], done="G" if c == TQ - 1 else None)
                for c in range(TQ):
                    put("tensor", lambda e, b, c=c: e.transpose(ps[:, 1, c * P:(c + 1) * P], bt[:, c * P:(c + 1) * P], eye[:]),
                        after=["Bs", "B_t0"], done="bT" if c == TQ - 1 else None)
                put("scalar", lambda e, b: e.activation(g[:], ps[:, 0, :], ACT.Copy), after=["G", ("gm15", -1)], done="g")
                put("scalar", lambda e, b: e.activation(bk[:], ps[:, 1, :].rearrange("p (c n) -> p c n", c=TQ), ACT.Copy), after=["bT", ("St7", -1)], done="bk")
                yield

            def inner():
                put = lambda *p, **k: r.put("P", *p, **k)
                for m in range(MI):
                    n = m % 2
                    project(put, f"x{m}", 0, XC + m * P, ["yl3", f"x{m - 1}_t0" if m else "g"])
                    convolve(put, f"x{m}", 0, m, n, f"xs{m - 2}" if m >= 2 else "Cs" if m == 0 else "Bs")
                    put("scalar", lambda e, b, n=n: e.activation(xs[:, n, :], cv[:, n, :], ACT.Silu),
                        after=[f"x{m}_t0", f"w{m - 2}" if m >= 2 else (f"w{m + 6}", -1)], done=f"xs{m}")
                    project(put, f"z{m}", 1, m * P, [f"sz{m - 1}" if m else "bk"])
                    put("scalar", lambda e, b, n=n: e.activation(sz[:, n, :], ps[:, 1, :], ACT.Silu),
                        after=[f"z{m}", f"u{m - 2}" if m >= 2 else (f"u{m + 6}", -1)], done=f"sz{m}")
                    yield

            def scan():
                put = lambda *p, **k: r.put("S", *p, **k)
                for m in range(MI):
                    n = m % 2
                    prev = lambda tag, d=1: f"{tag}{m - d}" if m >= d else (f"{tag}{m - d + MI}", -1)
                    for j in range(2):
                        h = 2 * m + j
                        put("tensor", lambda e, b, j=j, h=h: e.matmul(ps[:, 3 + j, :], sel[:, h:h + 1].broadcast_to([P, P]), dec2[:], start=True, stop=True),
                            after=["dec2", prev("pb") if j == 0 else (f"L{h - 2}" if h >= 2 else ("L15", -1))], done=f"De{h}")
                        put("vector", lambda e, b, j=j: e.tensor_tensor_scan(lm[:, j, :], ps[:, 3 + j, :], eyes[:].rearrange("p c t -> p (c t)"), 0.0, ALU.mult, ALU.add),
                            after=[f"De{h}", f"gm{h - 2}" if h >= 2 else (f"gm{h + 14}", -1), prev("xw")], done=f"L{h}")
                    for c in range(TQ):
                        put("tensor", lambda e, b, n=n, c=c: e.transpose(ps[:, 2, c * P:(c + 1) * P], xs[:, n, c * P:(c + 1) * P], eye[:]),
                            after=[f"xs{m}", prev("xp"), "dl", "dtT"], done=f"tx{m}" if c == TQ - 1 else None)
                    put("vector", lambda e, b, m=m, n=n: e.tensor_tensor(
                        xp[:, n, :, :].rearrange("p c (q d) -> p c q d", q=4)[:, :, 0::3, :],
                        ps[:, 2, :].rearrange("p (c j d) -> p c j d", c=TQ, j=2),
                        dtT[:, :, 2 * m:2 * m + 2].unsqueeze(3).broadcast_to([P, TQ, 2, 64]), ALU.mult),
                        after=[f"tx{m}", prev("Yi", 2)], done=f"xp{m}")
                    for j in range(2):
                        put("gpsimd", lambda e, b, j=j, n=n: e.tensor_tensor(xw[:, n, :, j * 64:(j + 1) * 64], xp[:, n, 0:TQ - 1, j * 192:j * 192 + 64],
                            lm[:, j, P - 1:(TQ - 1) * P:P].unsqueeze(2).broadcast_to([P, TQ - 1, 64]), ALU.mult),
                            after=[f"xp{m}", f"L{2 * m + j}", prev("St", 2)], done=f"xw{m}" if j else f"xw{m}_0")
                        put("gpsimd", lambda e, b, j=j, n=n: e.tensor_tensor(gm[:, n, j, :], lm[:, j, :], g[:], ALU.mult),
                            after=["g", prev("Yi", 2)], done=f"gm{2 * m + j}")
                    for c in range(TQ - 1):
                        put("tensor", lambda e, b, n=n, c=c: e.matmul(ps[:, 7, c * P:(c + 1) * P], bk[:, c, :], xw[:, n, c, :], start=True, stop=True),
                            after=["bk", f"xw{m}", prev("H")], done=f"St{m}" if c == TQ - 2 else None)
                    put("vector", lambda e, b: e.tensor_copy(hs[:, 0, :], ps[:, 7, 0:P]), after=[f"St{m}", prev("Yo")], done=f"H{m}_1")
                    for c in range(1, TQ - 1):
                        for j in range(2):
                            cols = slice(j * 64, (j + 1) * 64)
                            put("vector", lambda e, b, c=c, j=j, m=m, cols=cols: e.scalar_tensor_tensor(out=hs[:, c, cols], in0=hs[:, c - 1, cols],
                                scalar=dl[:, c, 2 * m + j:2 * m + j + 1], in1=ps[:, 7, c * P + j * 64:c * P + (j + 1) * 64], op0=ALU.mult, op1=ALU.add),
                                after=[f"H{m}_{c}", "dl"], done=None if j == 0 else f"H{m}_{c + 1}" if c < TQ - 2 else f"H{m}")
                    put("tensor", lambda e, b, m=m: e.matmul(ps[:, 3, :], selp[:, m, :], pre2[:], start=True, stop=True),
                        after=["pre2", f"L{2 * m}"], done=f"Pb{m}")
                    put("scalar", lambda e, b: e.activation(pb[:], ps[:, 3, :], ACT.Copy), after=[f"Pb{m}", prev("t")], done=f"pb{m}")
                    for c in range(TQ):
                        for j in range(2):
                            put("tensor", lambda e, b, c=c, j=j, n=n: e.matmul(ps[:, 5, c * P:(c + 1) * P], xp[:, n, c, j * P:(j + 1) * P],
                                gm[:, n, j, c * P:(c + 1) * P], start=(j == 0), stop=(j == 1)),
                                after=[f"xp{m}", f"gm{2 * m + 1}", prev("w")], done=f"Yi{m}" if (c, j) == (TQ - 1, 1) else None)
                    for c in range(1, TQ):
                        put("tensor", lambda e, b, c=c: e.matmul(ps[:, 6, c * P:(c + 1) * P], hs[:, c - 1, :], ct[:, c * P:(c + 1) * P], start=True, stop=True),
                            after=["Cs", f"H{m}", prev("t")], done=f"Yo{m}" if c == TQ - 1 else None)
                    late = slice(P, S)
                    put("vector", lambda e, b, n=n, m=m: e.scalar_tensor_tensor(out=yw[:, 0:P], in0=xs[:, n, 0:P], scalar=skip[:, m:m + 1],
                        in1=ps[:, 5, 0:P], op0=ALU.mult, op1=ALU.add), after=[f"Yi{m}", f"xs{m}", prev("u")], done=f"w{m}_0")
                    put("vector", lambda e, b: e.tensor_tensor(yw[:, late], ps[:, 6, late], pb[:, late], ALU.mult), after=[f"Yo{m}", f"pb{m}"], done=f"t{m}")
                    put("vector", lambda e, b: e.tensor_tensor(yw[:, late], yw[:, late], ps[:, 5, late], ALU.add), after=[f"t{m}"], done=f"ty{m}")
                    put("vector", lambda e, b, n=n, m=m: e.scalar_tensor_tensor(out=yw[:, late], in0=xs[:, n, late], scalar=skip[:, m:m + 1],
                        in1=yw[:, late], op0=ALU.mult, op1=ALU.add), after=[f"ty{m}"], done=f"w{m}")
                    put("gpsimd", lambda e, b, n=n, m=m: e.tensor_tensor(u[:, m, :], yw[:], sz[:, n, :], ALU.mult), after=[f"w{m}", f"sz{m}", ("o3", -1)], done=f"u{m}")
                    put("scalar", lambda e, b, m=m: e.activation(sq[:] if m else ssq[:], u[:, m, :], ACT.Square),
                        after=[f"u{m}", f"sa{m - 1}" if m > 1 else ("so_mm", -1)], done=f"sq{m}")
                    if m:
                        put("gpsimd", lambda e, b: e.tensor_tensor(ssq[:], ssq[:], sq[:], ALU.add), after=[f"sq{m}", f"sq{m - 1}" if m == 1 else f"sa{m - 1}"], done=f"sa{m}")
                    yield

            def out():
                put = lambda *p, **k: r.put("O", *p, **k)
                for q in range(TQ):
                    for k in range(MI):
                        put("tensor", lambda e, b, q=q, k=k: e.matmul(ps[:, 5 + q % 2, :], u[:, k, q * P:(q + 1) * P], wo[:, k, :], start=(k == 0), stop=(k == MI - 1)),
                            after=["u7", "w7", "t7", f"oc{q - 2}" if q >= 2 else "w7"], done=f"o{q}" if k == MI - 1 else None)
                    put("scalar", lambda e, b, q=q: e.activation(o[:, q % 2, :], ps[:, 5 + q % 2, :], ACT.Copy),
                        after=[f"o{q}", f"o_out{q - 2}" if q >= 2 else (f"o_out{q + 2}", -1)], done=f"oc{q}")
                    put("sync", lambda e, b, q=q: e.dma_start(scratch["o"][row(b), :, q, :].rearrange("b p d -> (b p) d"), o[:, q % 2, :]), after=[f"oc{q}"], dma=f"o_out{q}")
                    if q == 0:
                        for c in range(TQ):
                            put("tensor", lambda e, b, c=c: e.matmul(ps[:, 7, c:c + 1], ssq[:, c * P:(c + 1) * P], ones[:, 0:1], start=True, stop=True),
                                after=["sa7", "H7"], done="so_mm" if c == TQ - 1 else None)
                        put("vector", lambda e, b: e.tensor_copy(so[:], ps[:, 7, 0:TQ]), after=["so_mm", ("so_out", -1)], done="so")
                        put("sync", lambda e, b: e.dma_start(scratch["ssq"][row(b)].rearrange("b p q -> (b p) q"), so[:]), after=["so"], dma="so_out")
                    yield

            interleave("P PS PS PS PS PS PS PS S A O A A O A O A O A A", A=prepare(), P=inner(), S=scan(), O=out())
            r.emit()


def layer1(nc, a, scratch, out, rows):
    with ExitStack() as ctx:
        def sb(name, shape, dt=F32):
            return ctx.enter_context(nc.sbuf_tensor(f"l1_{name}", shape, dt))
        wq, wo = ([sb(f"{n}{h}", [P, KT, D], F32R) for h in "hl"] for n in ("wq", "wo"))
        qb = sb("qb", [P, KT])
        eye = sb("eye", [P, P])
        keep, neg = sb("keep", [P, C]), sb("neg", [P, C])
        o_in, y_in, ss = sb("o_in", [P, TQ, D]), sb("y_in", [P, TQ, D]), sb("ss", [P, TQ])
        ha, hb = sb("ha", [P, TQ, D]), sb("hb", [P, TQ, D])
        xn = sb("xn", [P, TQ, D])
        xt = [sb(f"x{h}", [P, KT, S], F32R) for h in "hl"]
        qt = sb("qt", [P, KT, S])
        kd, km = sb("kd", [P, KT, 2 * C]), sb("km", [P, KT, 2 * C])
        v = sb("v", [C, D])
        sc = sb("sc", [P, TQ, H1, C])
        mx, sm, rs = sb("mx", [P, TQ, H1]), sb("sm", [P, TQ, H1]), sb("rs", [P, TQ, H1])
        pt = sb("pt", [C, H1, S])
        cs = [sb(f"c{h}", [P, KT, S], F32R) for h in "hl"]
        ot = sb("ot", [P, TQ, D])
        vu, ru, t1 = sb("vu", [P, TQ]), sb("ru", [P, TQ]), sb("t1", [P, TQ])
        st, mv = sb("st", [P, TQ, 6]), sb("mv", [P, TQ, 2])
        var, rstd, t2 = sb("var", [P, TQ]), sb("rstd", [P, TQ]), sb("t2", [P, TQ])
        ps = ctx.enter_context(nc.psum_tensor("l1_ps", [P, 8, 512], F32))

        with ExitStack() as c2:
            mask = c2.enter_context(nc.sbuf_tensor("l1_mask", [P, C], U8))
            lw, lb = c2.enter_context(nc.sbuf_tensor("l1_lw", [P, KT], F32)), c2.enter_context(nc.sbuf_tensor("l1_lb", [P, KT], F32))
            w = Region(nc, c2, "l1w", 1, {"W": 0})
            put = lambda *p, **k: w.put("W", *p, **k)
            put("scalar", lambda e, b: e.dma_start(lw[:], tiles(a["lnw"]), allow_slow_non_contiguous=True), dma="lw")
            put("scalar", lambda e, b: e.dma_start(lb[:], tiles(a["lnb"]), allow_slow_non_contiguous=True), dma="lb")
            put("scalar", lambda e, b: e.dma_start(mask[:], a["kmask"].broadcast_to([P, C])), dma="mask")
            put("sync", lambda e, b: e.dma_start(xn[:], a["Wq1"].rearrange("(k p) n -> p k n", p=P)), dma="wq_raw")
            put("sync", lambda e, b: e.dma_start(eye[:], a["eye"]), dma="eye")
            for m in range(KT):
                for k in range(KT):
                    put("tensor", lambda e, b, m=m, k=k: e.matmul(ps[:, 0, m:m + 1], xn[:, k, m * P:(m + 1) * P], lb[:, k:k + 1], start=(k == 0), stop=(k == KT - 1)),
                        after=["wq_raw", "lb"], done="qb_mm" if (m, k) == (KT - 1, KT - 1) else None)
            put("vector", lambda e, b: e.tensor_scalar(qb[:], ps[:, 0, 0:KT], HD1 ** -0.5, None, ALU.mult), after=["qb_mm"], done="qb")
            put("vector", lambda e, b: e.tensor_scalar(lw[:], lw[:], 1.0, None, ALU.mult), after=["lw"], done="columns")
            split_weights(w, [("wq", a["Wq1"].rearrange("(k p) n -> p k n", p=P), ha, wq, HD1 ** -0.5, lw),
                              ("wo", a["Wo1"].rearrange("(k p) n -> p k n", p=P), hb, wo, 1.0, None)])
            put("vector", lambda e, b: e.tensor_copy(neg[:], mask[:]), after=["mask"], done="mf")
            put("vector", lambda e, b: e.tensor_scalar(keep[:], neg[:], -1.0, 1.0, ALU.mult, ALU.add), after=["mf"], done="keep")
            put("vector", lambda e, b: e.tensor_scalar(neg[:], neg[:], MASKED, None, ALU.mult), after=["keep"])
            put("gpsimd", lambda e, b: e.memset(kd[:], 0.0))
            w.emit()

        with ExitStack() as c2:
            r = Region(nc, c2, "l1", rows, {"A": 0, "B": 1}, "natural_log_exp_and_others")

            def attend():
                put = lambda *p, **k: r.put("A", *p, **k)
                rows_of = lambda t, b: t[row(b)].rearrange("b p q d -> (b p) q d")
                put("sync", lambda e, b: e.dma_start(ss[:], scratch["ssq"][row(b)].rearrange("b p q -> (b p) q")), after=[("vu", -1)], dma="ss")
                put("sync", lambda e, b: e.dma_start(o_in[:], rows_of(scratch["o"], b)), after=[("h3", -1)], dma="o_in")
                put("sync", lambda e, b: e.dma_start(y_in[:], rows_of(scratch["y"], b)), after=[("h3", -1)], dma="y_in")
                for j in range(2):
                    put("sync", lambda e, b, j=j: e.dma_start(kd[j * HD1:(j + 1) * HD1, :, j * C:(j + 1) * C],
                        scratch["k1"].rearrange("m p t -> p m t")[j * HD1:(j + 1) * HD1, :, row(b * C, C)]), after=[("km", -1)], dma=f"kd{j}")
                put("gpsimd", lambda e, b: e.tensor_tensor(km[:].rearrange("p m (j c) -> p (m j) c", j=2), kd[:].rearrange("p m (j c) -> p (m j) c", j=2),
                    keep[:].unsqueeze(1).broadcast_to([P, 2 * KT, C]), ALU.mult), after=["kd0", "kd1", (f"S{TQ - 1}", -1)], done="km")
                put("vector", lambda e, b: e.tensor_scalar(vu[:], ss[:], 1.0 / DI, EPS, ALU.mult, ALU.add), after=["ss", ("ru", -1)], done="vu")
                root_guess(r, "A", vu[:], ru[:], ["vu", ("h3", -1)], "ru")
                yield
                root_refine(r, "A", vu[:], ru[:], t1[:], "ru")
                for q in range(TQ):
                    put("vector", lambda e, b, q=q: e.scalar_tensor_tensor(out=ha[:, q, :], in0=o_in[:, q, :], scalar=ru[:, q:q + 1], in1=y_in[:, q, :],
                        op0=ALU.mult, op1=ALU.add), after=["ru", "o_in", "y_in", (f"hb{q}", -1)], done=f"h{q}")
                    put("vector", lambda e, b, q=q: e.bn_stats(st[:, q, :], ha[:, q, :]), after=[f"h{q}"], done=f"st{q}")
                for q in range(TQ):
                    put("vector", lambda e, b, q=q: e.bn_aggr(mv[:, q, :], st[:, q, :]), after=[f"st{q}"], done=f"mv{q}", apart=q)
                put("vector", lambda e, b: e.tensor_scalar(var[:], mv[:, :, 1], EPS, None, ALU.add), after=["mv3"], done="var")
                root_guess(r, "A", var[:], rstd[:], ["var"], "rstd")
                yield
                root_refine(r, "A", var[:], rstd[:], t2[:], "rstd")
                for q in range(TQ):
                    put("vector", lambda e, b, q=q: e.tensor_scalar(xn[:, q, :], ha[:, q, :], mv[:, q, 0:1], rstd[:, q:q + 1], ALU.subtract, ALU.mult),
                        after=["rstd", (f"tr{q}", -1)], done=f"n{q}")
                yield
                for q in range(TQ):
                    for k in range(KT):
                        put("tensor", lambda e, b, q=q, k=k: e.transpose(ps[:, q % 2, k * P:(k + 1) * P], xn[:, q, k * P:(k + 1) * P], eye[:]),
                            after=[f"n{q}", f"xl{q - 2}" if q >= 2 else (f"qt{q + 2}", -1)], done=f"tr{q}" if k == KT - 1 else None)
                    cols = slice(q * P, (q + 1) * P)
                    src = ps[:, q % 2, :].rearrange("p (k t) -> p k t", k=KT)
                    put("scalar", lambda e, b, cols=cols, src=src: e.activation(xt[0][:, :, cols], src, ACT.Copy), after=[f"tr{q}", ("q3", -1)], done=f"xh{q}")
                    put("vector", lambda e, b, cols=cols, src=src: e.tensor_tensor(xt[1][:, :, cols], src, xt[0][:, :, cols].bitcast(F32), ALU.subtract),
                        after=[f"xh{q}"], done=f"xl{q}")
                    if q % 2:
                        yield
                for m in range(KT):
                    for k in range(KT):
                        put("tensor", lambda e, b, m=m, k=k: mm3(e, ps[:, m % 2, :], [w_[:, k, m * P:(m + 1) * P] for w_ in wq],
                            [x_[:, k, :] for x_ in xt], k == 0, k == KT - 1),
                            after=["xl3", f"qt{m - 2}" if m >= 2 else "xl3"], done=f"q{m}" if k == KT - 1 else None)
                    put("scalar", lambda e, b, m=m: e.activation(qt[:, m, :], ps[:, m % 2, :], ACT.Identity, bias=qb[:, m:m + 1]),
                        after=[f"q{m}", (f"S{TQ - 1}", -1)], done=f"qt{m}")
                    yield

                for q in range(TQ):
                    put("scalar", lambda e, b, q=q: e.activation(hb[:, q, :], ha[:, q, :], ACT.Copy), after=[f"h{q}", (f"out{q}", -1)], done=f"hb{q}")

                def weigh(q):
                    for m in range(KT):
                        put("tensor", lambda e, b, m=m: e.matmul(ps[:, 2 + m // 2, (m % 2) * 2 * C:(m % 2 + 1) * 2 * C], qt[:, m, q * P:(q + 1) * P], km[:, m, :],
                            start=True, stop=True), after=["qt3", "km", f"add{q - 1}" if q else ("add3", -1)], done=f"S{q}" if m == KT - 1 else None)
                    put("vector", lambda e, b: e.tensor_tensor(sc[:, q, :, :].rearrange("p (a h) c -> p a h c", a=2),
                        ps[:, 2:4, 0:4 * C].rearrange("p a (h c) -> p a h c", h=4),
                        neg[:].unsqueeze(1).unsqueeze(1).broadcast_to([P, 2, 4, C]), ALU.add), after=[f"S{q}", (f"pt{q}", -1)], done=f"add{q}")
                    put("vector", lambda e, b: e.tensor_reduce(mx[:, q, :], sc[:, q, :, :], AX_X, ALU.max), after=[f"add{q}"], done=f"mx{q}")
                    put("vector", lambda e, b: e.tensor_tensor(sc[:, q, :, :], sc[:, q, :, :], mx[:, q, :].unsqueeze(2).broadcast_to([P, H1, C]), ALU.subtract),
                        after=[f"mx{q}"], done=f"sub{q}")
                    put("scalar", lambda e, b: e.activation(sc[:, q, :, :], sc[:, q, :, :], ACT.Exp), after=[f"sub{q}"], done=f"e{q}")

                def normalise(q):
                    put("vector", lambda e, b: e.tensor_reduce(sm[:, q, :], sc[:, q, :, :], AX_X, ALU.add), after=[f"e{q}"], done=f"sm{q}")
                    put("vector", lambda e, b: e.reciprocal(rs[:, q, :], sm[:, q, :]), after=[f"sm{q}", (f"nm{q}", -1)], done=f"rs{q}")
                    put("gpsimd", lambda e, b: e.tensor_tensor(sc[:, q, :, :], sc[:, q, :, :], rs[:, q, :].unsqueeze(2).broadcast_to([P, H1, C]), ALU.mult),
                        after=[f"rs{q}"], done=f"nm{q}")

                def turn(q):
                    for h in range(H1):
                        put("tensor", lambda e, b, h=h: e.transpose(ps[0:C, 4 + h // 4, (h % 4) * P:(h % 4 + 1) * P], sc[:, q, h, :], eye[:]),
                            after=[f"nm{q}", f"pc{q - 1}" if q else ("pc3", -1)], done=f"pt{q}" if h == H1 - 1 else None)
                    put("scalar", lambda e, b: e.activation(pt[:, :, q * P:(q + 1) * P], ps[0:C, 4:6, :].rearrange("c a (h t) -> c (a h) t", h=4), ACT.Copy),
                        after=[f"pt{q}", ("pv3", -1)], done=f"pc{q}")

                for step in ((weigh, 0), (weigh, 1), (normalise, 0), (weigh, 2), (normalise, 1), (turn, 0), (weigh, 3), (normalise, 2), (turn, 1),
                             (normalise, 3), (turn, 2), (turn, 3)):
                    step[0](step[1])
                    yield

            def finish():
                put = lambda *p, **k: r.put("B", *p, **k)
                put("sync", lambda e, b: e.dma_start(v[:], scratch["v1"][row(b * C, C), :]), after=[("pv3", -1)], dma="v")
                for m in range(KT):
                    for j in range(2):
                        h = 2 * m + j
                        put("tensor", lambda e, b, m=m, j=j, h=h: e.matmul(ps[j * HD1:(j + 1) * HD1, 6 + m % 2, :], v[:, h * HD1:(h + 1) * HD1], pt[:, h, :], start=True, stop=True),
                            after=["v", "pc3", f"cl{m - 2}" if m >= 2 else (f"out{m + 2}", -1)], done=f"pv{m}" if j else None)
                    put("scalar", lambda e, b, m=m: e.activation(cs[0][:, m, :], ps[:, 6 + m % 2, :], ACT.Copy), after=[f"pv{m}", ("O3", -1)], done=f"ch{m}")
                    put("vector", lambda e, b, m=m: e.tensor_tensor(cs[1][:, m, :], ps[:, 6 + m % 2, :], cs[0][:, m, :].bitcast(F32), ALU.subtract),
                        after=[f"ch{m}"], done=f"cl{m}")
                    yield
                for q in range(TQ):
                    for k in range(KT):
                        put("tensor", lambda e, b, q=q, k=k: mm3(e, ps[:, 6 + q % 2, :], [c_[:, k, q * P:(q + 1) * P] for c_ in cs],
                            [w_[:, k, :] for w_ in wo], k == 0, k == KT - 1),
                            after=["cl3", f"out{q - 2}" if q >= 2 else "cl3"], done=f"O{q}" if k == KT - 1 else None)
                    put("vector", lambda e, b, q=q: e.tensor_tensor(ot[:, q, :], ps[:, 6 + q % 2, :], hb[:, q, :], ALU.add),
                        after=[f"O{q}", f"hb{q}", (f"store{q}", -1)], done=f"out{q}")
                    put("sync", lambda e, b, q=q: e.dma_start(out[row(b), q * P:(q + 1) * P, :].rearrange("b p d -> (b p) d"), ot[:, q, :]), after=[f"out{q}"], dma=f"store{q}")
                    yield

            interleave("B B B A A B A A B A A B A A B A B AAAAAAAAAAAA A", A=attend(), B=finish())
            r.emit()


def build(nc, a, out):
    rows = a["x"].shape[0]
    tokens = a["ctxT"].shape[1]
    shapes = {"k0h": [KT, P, tokens], "k0l": [KT, P, tokens], "k1": [KT, P, tokens], "v0": [tokens, D], "v1": [tokens, D],
              "y": [rows, P, TQ, D], "o": [rows, P, TQ, D], "rinv": [rows, P, TQ], "ssq": [rows, P, TQ]}
    scratch = {n: nc.dram_tensor(f"scratch_{n}", s, F32).ap() for n, s in shapes.items()}
    keys_values(nc, a, scratch)
    layer0(nc, a, scratch, rows)
    mamba(nc, a, scratch, rows)
    layer1(nc, a, scratch, out, rows)


def kernel(**inputs):
    import numpy as np
    from concourse import bacc
    from concourse.bass_utils import run_bass_kernel_spmd

    get = lambda n: np.asarray(inputs[n])
    l0, l1 = (lambda n: get(f"L0_xattn_{n}")), (lambda n: get(f"L1_xattn_{n}"))
    ctx = get("ctx_1024")
    arrays = {
        "x": get("x"), "xT": get("x").transpose(0, 2, 1), "ctxT": ctx.transpose(2, 0, 1).reshape(ctx.shape[2], -1),
        "maskT": get("mask_Bx1xSxS2_fk0")[:, 0].transpose(0, 2, 1), "kmask": get("mask_1xS2_bf0"),
        "Wq0": l0("Wq"), "bq0": l0("bq"), "Wk0": l0("Wk"), "bk0": l0("bk"), "Wv0": l0("Wv"), "bv0": l0("bv"),
        "Wo0": l0("Wo"), "bo0": l0("bo"), "gamma0": l0("gamma"), "beta0": l0("beta"),
        "norm1": l1("m_norm_w"), "Win": l1("in_proj_w"), "cw": l1("conv_w"), "cb": l1("conv_b"), "dtb": l1("dt_bias"),
        "alog": l1("A_log"), "skip": l1("D_skip"), "gnorm1": l1("gnorm_w"), "Wout": l1("out_proj_w"),
        "lnw": l1("ca_ln_w"), "lnb": l1("ca_ln_b"), "Wq1": l1("Wq"), "Wk1": l1("Wk"), "Wv1": l1("Wv"), "Wo1": l1("Wo"),
        "eye": np.eye(P, dtype=np.float32),
    }
    nc = bacc.Bacc("TRN2", target_bir_lowering=False, num_devices=1)
    maps, args = {}, {}
    for name, array in arrays.items():
        maps[f"in_{name}"] = np.ascontiguousarray(array)
        args[name] = nc.dram_tensor(f"in_{name}", array.shape, mybir.dt.from_np(array.dtype), kind="ExternalInput").ap()
    out = nc.dram_tensor("out", get("x").shape, F32, kind="ExternalOutput").ap()
    build(nc, args, out)
    return run_bass_kernel_spmd(nc, [maps], core_ids=[0]).results[0]["out"]
```

```python
from contextlib import ExitStack

import concourse.bass as bass
from concourse import mybir

F32 = mybir.dt.float32
F32R = mybir.dt.float32r
U8 = mybir.dt.uint8
ALU = mybir.AluOpType
ACT = mybir.ActivationFunctionType
AX_X = mybir.AxisListType.X

P = 128
D = 512
KT = D // P
S = 512
TQ = S // P
C = 77
H0, HD0 = 16, 32
H1, HD1 = 8, 64
HPT = P // HD0
DI = 1024
MI = DI // P
HM = 16
NS = 128
CONVD = DI + 2 * NS
TAPS = 4
EPS = 1e-5
CLAMP = 50.0
MASKED = -1.0e9
KV_TILE = 112
DT_COLS = 64

ENGINES = ("tensor", "scalar", "vector", "gpsimd", "sync")


class Region:

    def __init__(self, nc, ctx, name, rows, lags, tables=None):
        self.tables = tables
        self.spare = ctx.enter_context(nc.sbuf_tensor(f"{name}_spare", [1, TQ], F32))
        self.nc, self.ctx, self.name, self.rows, self.lags = nc, ctx, name, rows, lags
        self.queue = {e: [] for e in ENGINES}
        self.count = {}
        self.step = {}
        self.named = {}
        self.placed = {}
        self.places = 0

    def put(self, stage, engine, build, after=(), done=None, dma=None, apart=None, first=None):
        raised = None
        self.places += 1
        if done or dma:
            raised = dma or f"{stage}_{engine}"
            self.count[raised] = self.count.get(raised, 0) + 1
            self.step[raised] = 16 if dma else 1
            for n in [done] if isinstance(done, str) else (done or []):
                assert n not in self.named, n
                self.named[n] = (raised, self.count[raised])
                self.placed[n] = (stage, self.places)
            if dma:
                self.placed[dma] = (stage, self.places)
                self.named[dma] = (raised, self.count[raised])
        self.queue[engine].append((stage, build, list(after), raised, apart, first, self.places))

    def emit(self):
        nc, last = self.nc, max(self.lags.values())
        for q in self.queue.values():
            for stage, _, after, _, _, _, at in q:
                for a in after:
                    n, shift = (a, 0) if isinstance(a, str) else a
                    turns = self.lags[self.placed[n][0]] + shift - self.lags[stage]
                    assert turns < 0 or (turns == 0 and self.placed[n][1] < at), (n, shift, stage)
        sem = {s: self.ctx.enter_context(nc.semaphore(f"{self.name}_{s}")) for s in self.count}
        per = {s: self.count[s] * self.step[s] for s in self.count}
        block = self.ctx.enter_context(nc.Block())

        def turn(eng, q, t, stages):
            waited, base = {}, {}
            for stage, build, after, raised, apart, first, _ in q:
                if stage not in stages:
                    continue
                b = t - self.lags[stage]
                if first:
                    first(eng)
                for a in after:
                    name, shift = (a, 0) if isinstance(a, str) else a
                    s, k = self.named[name]
                    if s not in base:
                        base[s] = t * per[s] if isinstance(t, int) else eng.snap(t * per[s])
                    ahead = (1 + shift - self.lags[stage]) * per[s] + k * self.step[s]
                    if waited.get(s, -10 ** 9) >= ahead:
                        continue
                    waited[s] = ahead
                    eng.wait_ge(sem[s], base[s] + ahead)
                if apart is not None:
                    eng.memset(self.spare[:, apart:apart + 1], 0.0)
                ins = build(eng, b)
                if raised:
                    ins.then_inc(sem[raised], self.step[raised])

        def program(name):
            def body(eng):
                q = self.queue[name]
                if name == "scalar" and self.tables:
                    eng.preload_act_table_set(self.tables)
                if name == "sync":
                    for s in per:
                        eng.sem_inc(sem[s], per[s])
                for t in range(last):
                    turn(eng, q, t, [s for s, lag in self.lags.items() if lag <= t])
                if self.rows > last:
                    if self.rows - last == 1:
                        turn(eng, q, last, list(self.lags))
                    elif q:
                        with eng.Fori(last, self.rows) as t:
                            turn(eng, q, t, list(self.lags))
                for t in range(self.rows, self.rows + last):
                    turn(eng, q, t, [s for s, lag in self.lags.items() if t - lag < self.rows])
                if name == "sync":
                    for s in per:
                        if self.step[s] == 16:
                            eng.wait_ge(sem[s], (self.rows + 1) * per[s])
            return body

        for name in ENGINES:
            if self.queue[name] or name == "sync":
                getattr_block = {"tensor": block.tensor, "scalar": block.scalar, "vector": block.vector,
                                 "gpsimd": block.gpsimd, "sync": block.sync}[name]
                getattr_block(program(name))


def interleave(order, **steps):
    for c in order.replace(" ", ""):
        next(steps[c], None)
    for c, g in steps.items():
        rest = sum(1 for _ in g)
        assert rest == 0, (c, rest)


def mm3(eng, out, w, x, start=True, stop=True):
    eng.matmul(out, w[0], x[0], start=start, stop=False)
    eng.matmul(out, w[0], x[1], start=False, stop=False)
    return eng.matmul(out, w[1], x[0], start=False, stop=stop)


def row(b, n=1):
    return slice(b, b + n) if isinstance(b, int) else bass.ds(b, n)


def tiles(vector, width=P):
    return vector.rearrange("(m p) -> p m", p=width)


def spread(vector, parts=P):
    return vector.rearrange("(a n) -> a n", a=1).broadcast_to([parts, vector.shape[0]])


def root_guess(r, stage, v, y, after, tag):
    r.put(stage, "scalar", lambda e, b: e.activation(y, v, ACT.Ln), after=after, done=f"{tag}_ln")
    r.put(stage, "scalar", lambda e, b: e.activation(y, y, ACT.Exp, scale=-0.5), after=[f"{tag}_ln"], done=f"{tag}_0")


def root_refine(r, stage, v, y, t, tag):
    steps = (lambda e, b: e.tensor_tensor(t, y, y, ALU.mult),
             lambda e, b: e.tensor_tensor(t, t, v, ALU.mult),
             lambda e, b: e.tensor_scalar(t, t, -0.5, 1.5, ALU.mult, ALU.add),
             lambda e, b: e.tensor_tensor(y, y, t, ALU.mult))
    for n, op in enumerate(steps):
        r.put(stage, "vector", op, after=[f"{tag}_{n}"], done=f"{tag}_{n + 1}" if n < 3 else tag)


def keys_values(nc, a, scratch):
    with ExitStack() as ctx:
        def sb(name, shape, dt=F32):
            return ctx.enter_context(nc.sbuf_tensor(f"kv_{name}", shape, dt))
        rows = a["ctxT"].shape[1] // KV_TILE
        wk = [sb(f"wk{l}", [P, KT, D]) for l in range(2)]
        wv_raw = [sb(f"wv{l}", [P, KT, D]) for l in range(2)]
        wv = [[sb(f"wv{l}{h}", [P, KT, D], F32R) for h in "hl"] for l in range(2)]
        bk, bv = sb("bk", [P, KT]), sb("bv", [P, D])
        x_in, x_f = sb("x_in", [P, KT, KV_TILE]), sb("x_f", [P, KT, KV_TILE])
        x_s = [sb(f"x_{h}", [P, KT, KV_TILE], F32R) for h in "hl"]
        k0f = sb("k0f", [P, KT, KV_TILE])
        k0s = [sb(f"k0{h}", [P, KT, KV_TILE], F32R) for h in "hl"]
        k1s = sb("k1s", [P, KT, KV_TILE])
        v_s = [sb(f"v{l}", [KV_TILE, D]) for l in range(2)]
        ps = ctx.enter_context(nc.psum_tensor("kv_ps", [P, 8, 512], F32))

        with ExitStack() as c2:
            w = Region(nc, c2, "kvw", 1, {"W": 0})
            for l in range(2):
                w.put("W", "sync", lambda e, b, l=l: e.dma_start(wv_raw[l][:], a[f"Wv{l}"].rearrange("(k p) n -> p k n", p=P)), dma=f"wv{l}")
                w.put("W", "scalar", lambda e, b, l=l: e.dma_start(wk[l][:], a[f"Wk{l}"].rearrange("(k p) n -> p k n", p=P)), dma=f"wk{l}")
            w.put("W", "sync", lambda e, b: e.dma_start(bk[:], tiles(a["bk0"]), allow_slow_non_contiguous=True), dma="bk")
            w.put("W", "sync", lambda e, b: e.dma_start(bv[:], spread(a["bv0"])), dma="bv")
            for l in range(2):
                w.put("W", "scalar", lambda e, b, l=l: e.activation(wv[l][0][:], wv_raw[l][:], ACT.Copy), after=[f"wv{l}"], done=f"wvh{l}")
                w.put("W", "vector", lambda e, b, l=l: e.tensor_tensor(wv[l][1][:], wv_raw[l][:], wv[l][0][:].bitcast(F32), ALU.subtract), after=[f"wvh{l}", f"wv{l}"], done=f"wvl{l}")
            w.emit()

        with ExitStack() as c2:
            r = Region(nc, c2, "kv", rows, {"T": 0})
            put = lambda *p, **k: r.put("T", *p, **k)
            put("sync", lambda e, b: e.dma_start(x_in[:], a["ctxT"].rearrange("(k p) t -> p k t", p=P)[:, :, row(b * KV_TILE, KV_TILE)]),
                after=[("xf", -1), ("xl", -1)], dma="x")
            put("scalar", lambda e, b: e.activation(x_s[0][:], x_in[:], ACT.Copy), after=["x", ("V1", -1)], done="xh")
            put("vector", lambda e, b: e.tensor_tensor(x_s[1][:], x_in[:], x_s[0][:].bitcast(F32), ALU.subtract), after=["xh"], done="xl")
            put("vector", lambda e, b: e.tensor_copy(x_f[:], x_in[:]), after=["x", ("K1", -1)], done="xf")
            for l in range(2):
                for k in range(KT):
                    put("tensor", lambda e, b, l=l, k=k: mm3(e, ps[0:KV_TILE, l, :], [x_s[0][:, k, :], x_s[1][:, k, :]],
                        [wv[l][0][:, k, :], wv[l][1][:, k, :]], k == 0, k == KT - 1),
                        after=["xl", (f"v{l}", -1)], done=f"V{l}" if k == KT - 1 else None)
            for l in range(2):
                for m in range(KT):
                    for k in range(KT):
                        put("tensor", lambda e, b, l=l, m=m, k=k: e.matmul(ps[:, 2 + l, m * KV_TILE:(m + 1) * KV_TILE],
                            wk[l][:, k, m * P:(m + 1) * P], x_f[:, k, :], start=(k == 0), stop=(k == KT - 1)),
                            after=["xf", (("k0f", "k1")[l], -1)], done=f"K{l}" if (m, k) == (KT - 1, KT - 1) else None)
            put("vector", lambda e, b: e.tensor_tensor(v_s[0][:], ps[0:KV_TILE, 0, :], bv[0:KV_TILE, :], ALU.add), after=["V0", ("v0_out", -1)], done="v0")
            put("scalar", lambda e, b: e.activation(v_s[1][:], ps[0:KV_TILE, 1, :], ACT.Copy), after=["V1", ("v1_out", -1)], done="v1")
            put("vector", lambda e, b: e.tensor_tensor(k0f[:], ps[:, 2, 0:KT * KV_TILE].rearrange("p (m t) -> p m t", m=KT),
                bk[:].unsqueeze(2).broadcast_to([P, KT, KV_TILE]), ALU.add), after=["K0", ("k0l", -1)], done="k0f")
            put("scalar", lambda e, b: e.activation(k0s[0][:], k0f[:], ACT.Copy), after=["k0f", ("k0h_out", -1)], done="k0h")
            put("vector", lambda e, b: e.tensor_tensor(k0s[1][:], k0f[:], k0s[0][:].bitcast(F32), ALU.subtract), after=["k0h", ("k0l_out", -1)], done="k0l")
            put("scalar", lambda e, b: e.activation(k1s[:], ps[:, 3, 0:KT * KV_TILE].rearrange("p (m t) -> p m t", m=KT), ACT.Copy), after=["K1", ("k1_out", -1)], done="k1")
            for l in range(2):
                put("sync", lambda e, b, l=l: e.dma_start(scratch[f"v{l}"][row(b * KV_TILE, KV_TILE), :], v_s[l][:]), after=[f"v{l}"], dma=f"v{l}_out")
            for n, t in (("k0h", k0s[0][:].bitcast(F32)), ("k0l", k0s[1][:].bitcast(F32)), ("k1", k1s[:])):
                put("sync", lambda e, b, n=n, t=t: e.dma_start(scratch[n].rearrange("m p t -> p m t")[:, :, row(b * KV_TILE, KV_TILE)], t),
                    after=[n], dma=f"{n}_out")
            r.emit()


def layer0(nc, a, scratch, rows):
    with ExitStack() as ctx:
        def sb(name, shape, dt=F32):
            return ctx.enter_context(nc.sbuf_tensor(f"l0_{name}", shape, dt))
        wq, wo = ([sb(f"{n}{h}", [P, KT, D], F32R) for h in "hl"] for n in ("wq", "wo"))
        bq, bo, gamma, beta = sb("bq", [P, KT]), sb("bo", [P, D]), sb("gamma", [P, D]), sb("beta", [P, D])
        ones = sb("ones", [C, HD0])
        x_in = sb("x_in", [P, KT, S])
        xs = [sb(f"x{h}", [P, KT, S], F32R) for h in "hl"]
        qs = [sb(f"q{h}", [P, KT, S], F32R) for h in "hl"]
        kp = [sb(f"k{h}", [P, H0, C], F32R) for h in "hl"]
        v = sb("v", [C, D])
        m_in, mf = sb("m_in", [C, S]), sb("mf", [C, S])
        sc = sb("sc", [C, 4, S])
        pt = sb("pt", [C, H0, S])
        lg, rd, nr = sb("lg", [P, 2, S]), sb("rd", [P, 2, S]), sb("nr", [P, 2, S])
        cn = sb("cn", [P, 2, S])
        cs = [sb(f"c{h}", [P, KT, S], F32R) for h in "hl"]
        xb = sb("xb", [P, TQ, D])
        res = sb("res", [P, TQ, D])
        y = sb("y", [P, TQ, D])
        sq = sb("sq", [P, D])
        st, mv = sb("st", [P, TQ, 6]), sb("mv", [P, TQ, 2])
        var, rstd, tmp = sb("var", [P, TQ]), sb("rstd", [P, TQ]), sb("tmp", [P, TQ])
        ms, rms, rinv, tmp2 = sb("ms", [P, TQ]), sb("rms", [P, TQ]), sb("rinv", [P, TQ]), sb("tmp2", [P, TQ])
        ps = ctx.enter_context(nc.psum_tensor("l0_ps", [P, 8, 512], F32))

        with ExitStack() as c2:
            w = Region(nc, c2, "l0w", 1, {"W": 0})
            put = lambda *p, **k: w.put("W", *p, **k)
            split_weights(w, [("wq", a["Wq0"].rearrange("(k p) n -> p k n", p=P), x_in, wq, HD0 ** -0.5, None),
                              ("wo", a["Wo0"].rearrange("(k p) n -> p k n", p=P), y, wo, 1.0, None)])
            put("sync", lambda e, b: e.dma_start(bq[:], tiles(a["bq0"]), allow_slow_non_contiguous=True), dma="bq")
            put("scalar", lambda e, b: e.dma_start(bo[:], spread(a["bo0"])), dma="bo")
            put("scalar", lambda e, b: e.dma_start(gamma[:], spread(a["gamma0"])), dma="gamma")
            put("scalar", lambda e, b: e.dma_start(beta[:], spread(a["beta0"])), dma="beta")
            put("gpsimd", lambda e, b: e.memset(ones[:], 1.0), done="ones")
            put("gpsimd", lambda e, b: e.memset(kp[0][:].bitcast(F32), 0.0), done="kz0")
            put("gpsimd", lambda e, b: e.memset(kp[1][:].bitcast(F32), 0.0), done="kz1")
            put("vector", lambda e, b: e.tensor_scalar(bq[:], bq[:], HD0 ** -0.5, None, ALU.mult), after=["bq"], done="bqs")
            w.emit()

        with ExitStack() as c2:
            r = Region(nc, c2, "l0", rows, {"X": 0, "K": 0, "V": 1, "A": 1, "B": 2, "C": 3, "R": 4}, "natural_log_exp_and_others")

            def load_split():
                put = lambda *p, **k: r.put("X", *p, **k)
                put("sync", lambda e, b: e.dma_start(x_in[:], a["xT"].rearrange("b (k p) t -> b p k t", p=P)[row(b)].rearrange("b p k t -> (b p) k t")),
                    after=[("xl3", -1)], dma="x_in")
                for k in range(KT):
                    put("scalar" if k % 2 else "vector",
                        (lambda e, b, k=k: e.activation(xs[0][:, k, :], x_in[:, k, :], ACT.Copy)) if k % 2 else
                        (lambda e, b, k=k: e.tensor_copy(xs[0][:, k, :], x_in[:, k, :])),
                        after=["x_in", ("q3", -1)], done=f"xh{k}")
                    put("gpsimd", lambda e, b, k=k: e.tensor_tensor(xs[1][:, k, :], x_in[:, k, :], xs[0][:, k, :].bitcast(F32), ALU.subtract),
                        after=[f"xh{k}", ("q3", -1)], done=f"xl{k}")
                yield

            def load_keys():
                put = lambda *p, **k: r.put("K", *p, **k)
                for n, s in enumerate(("k0h", "k0l")):
                    for j in range(HPT):
                        src = scratch[s].rearrange("m p t -> p m t")[j * HD0:(j + 1) * HD0]
                        dst = kp[n][j * HD0:(j + 1) * HD0, :, :].bitcast(F32).rearrange("p (m j) t -> p m j t", j=HPT)[:, :, j, :]
                        put("sync", lambda e, b, src=src, dst=dst: e.dma_start(dst, src[:, :, row(b * C, C)]),
                            after=[(f"S{H0 - 1}", -1)], dma=f"kp{n}{j}")
                put("sync", lambda e, b: e.dma_start(m_in[:], a["maskT"][row(b)].rearrange("b c t -> (b c) t")), after=[("mf", -1)], dma="m_in")
                yield

            def load_values():
                put = lambda *p, **k: r.put("V", *p, **k)
                put("sync", lambda e, b: e.dma_start(v[:], scratch["v0"][row(b * C, C), :]), after=[("pv3", -1)], dma="v")
                yield
                put("sync", lambda e, b: e.dma_start(xb[:], a["x"].rearrange("b (q p) d -> b p q d", p=P)[row(b)].rearrange("b p q d -> (b p) q d")),
                    after=[("r3", -1)], dma="x_tok")
                yield

            def scores():
                put = lambda *p, **k: r.put("A", *p, **k)
                put("vector", lambda e, b: e.tensor_scalar(mf[:], m_in[:], 0.5, 0.5, ALU.mult, ALU.add),
                    after=["m_in", (f"mul{H0 - 1}", -1)], done="mf")
                for m in range(KT):
                    for k in range(KT):
                        put("tensor", lambda e, b, m=m, k=k: mm3(e, ps[:, m, :], [w_[:, k, m * P:(m + 1) * P] for w_ in wq],
                            [x_[:, k, :] for x_ in xs], k == 0, k == KT - 1),
                            after=[f"xl{k}", f"xh{k}", (f"mul{12 + m}", -1)], done=f"q{m}" if k == KT - 1 else None)
                    put("scalar", lambda e, b, m=m: e.activation(qs[0][:, m, :], ps[:, m, :], ACT.Identity, bias=bq[:, m:m + 1]),
                        after=[f"q{m}", (f"S{4 * m + 3}", -1)], done=f"qh{m}")
                    put("vector", lambda e, b, m=m: e.scalar_tensor_tensor(out=qs[1][:, m, :], in0=ps[:, m, :], scalar=bq[:, m:m + 1],
                        in1=qs[0][:, m, :].bitcast(F32), op0=ALU.add, op1=ALU.subtract), after=[f"qh{m}"], done=f"ql{m}")
                    yield
                for h in range(H0):
                    m = h // HPT
                    free = f"ql{h}" if h < 4 else f"mul{h - 4}"
                    keys = [f"kp{n}{j}" for n in range(2) for j in range(HPT)] if h == 0 else []
                    put("tensor", lambda e, b, h=h, m=m: mm3(e, ps[0:C, h % 4, :], [k_[:, h, :] for k_ in kp], [q_[:, m, :] for q_ in qs]),
                        after=[f"ql{m}", free] + keys, done=f"S{h}")
                    put("vector", lambda e, b, h=h: e.tensor_tensor(sc[:, h % 4, :], ps[0:C, h % 4, :], mf[:], ALU.mult),
                        after=[f"S{h}", "mf", f"exp{h - 4}" if h >= 4 else (f"exp{12 + h}", -1)], done=f"mul{h}")
                    put("vector", lambda e, b, h=h: e.tensor_scalar(sc[:, h % 4, :], sc[:, h % 4, :], CLAMP, -CLAMP, ALU.min, ALU.max),
                        after=[f"mul{h}"], done=f"clip{h}")
                    put("scalar", lambda e, b, h=h: e.activation(pt[:, h, :], sc[:, h % 4, :], ACT.Exp),
                        after=[f"clip{h}", (f"pv{m}", -1)], done=f"exp{h}")
                    yield

            def values_out():
                put = lambda *p, **k: r.put("B", *p, **k)

                def banks(m):
                    return 4 + 2 * (m % 2)

                def weigh_values(m):
                    free = [f"cn{m - 2}"] if m >= 2 else [("r2", -1), ("r3", -1), (f"cn{m + 2}", -1)]
                    for j in range(HPT):
                        h = HPT * m + j
                        put("tensor", lambda e, b, j=j, h=h: e.matmul(ps[j * HD0:(j + 1) * HD0, banks(m), :], v[:, h * HD0:(h + 1) * HD0], pt[:, h, :], start=True, stop=True),
                            after=["v", f"exp{h}"] + free)
                    for j in range(HPT):
                        h = HPT * m + j
                        put("tensor", lambda e, b, j=j, h=h: e.matmul(ps[j * HD0:(j + 1) * HD0, banks(m) + 1, :], ones[:], pt[:, h, :], start=True, stop=True),
                            done=f"pv{m}" if j == HPT - 1 else None)
                    put("scalar", lambda e, b: e.activation(lg[:, m % 2, :], ps[:, banks(m) + 1, :], ACT.Ln), after=[f"pv{m}"], done=f"lg{m}")
                    put("scalar", lambda e, b: e.activation(rd[:, m % 2, :], lg[:, m % 2, :], ACT.Exp, scale=-1.0),
                        after=[f"lg{m}", f"nr{m - 2}" if m >= 2 else (f"nr{m + 2}", -1)], done=f"rd{m}")

                def divide(m):
                    put("vector", lambda e, b: e.tensor_tensor(nr[:, m % 2, :], ps[:, banks(m) + 1, :], rd[:, m % 2, :], ALU.mult), after=[f"rd{m}", f"cn{m - 2}" if m >= 2 else (f"cn{m + 2}", -1)], done=f"sg{m}")
                    put("vector", lambda e, b: e.scalar_tensor_tensor(out=nr[:, m % 2, :], in0=nr[:, m % 2, :], scalar=2.0, in1=rd[:, m % 2, :], op0=ALU.subtract, op1=ALU.mult),
                        after=[f"sg{m}"], done=f"nr{m}")
                    put("vector", lambda e, b: e.scalar_tensor_tensor(out=cn[:, m % 2, :], in0=ps[:, banks(m), :], scalar=-1.0, in1=nr[:, m % 2, :], op0=ALU.mult, op1=ALU.mult),
                        after=[f"nr{m}", f"cl{m - 2}" if m >= 2 else (f"cl{m + 2}", -1)], done=f"cn{m}")
                    put("scalar", lambda e, b: e.activation(cs[0][:, m, :], cn[:, m % 2, :], ACT.Copy), after=[f"cn{m}", ("o3", -1)], done=f"ch{m}")
                    put("gpsimd", lambda e, b: e.tensor_tensor(cs[1][:, m, :], cn[:, m % 2, :], cs[0][:, m, :].bitcast(F32), ALU.subtract),
                        after=[f"ch{m}"], done=f"cl{m}")
                    put("gpsimd", lambda e, b: e.tensor_tensor(xb[:, m, :], xb[:, m, :], bo[:], ALU.add), after=["x_tok"], done=f"xb{m}")

                for step in ((weigh_values, 0), (weigh_values, 1), (divide, 0), (weigh_values, 2), (divide, 1), (weigh_values, 3), (divide, 2), (divide, 3)):
                    step[0](step[1])
                    yield
                for q in range(TQ):
                    for k in range(KT):
                        put("tensor", lambda e, b, q=q, k=k: mm3(e, ps[:, 6 + q % 2, :], [c_[:, k, q * P:(q + 1) * P] for c_ in cs],
                            [w_[:, k, :] for w_ in wo], k == 0, k == KT - 1),
                            after=[f"ch{k}", f"cl{k}", f"r{q - 2}" if q >= 2 else "cn3"], done=f"o{q}" if k == KT - 1 else None)
                    put("vector", lambda e, b, q=q: e.tensor_tensor(res[:, q, :], ps[:, 6 + q % 2, :], xb[:, q, :], ALU.add),
                        after=[f"o{q}", f"xb{q}", (f"n{q}", -1)], done=f"r{q}")
                    put("vector", lambda e, b, q=q: e.bn_stats(st[:, q, :], res[:, q, :]), after=[f"r{q}"], done=f"st{q}")
                    put("vector", lambda e, b, q=q: e.bn_aggr(mv[:, q, :], st[:, q, :]), after=[f"st{q}"], done=f"mv{q}", apart=q)
                    yield
                put("vector", lambda e, b: e.tensor_scalar(var[:], mv[:, :, 1], EPS, None, ALU.add), after=["mv3"], done="var")
                root_guess(r, "B", var[:], rstd[:], ["var"], "rstd")
                yield

            def normalise():
                put = lambda *p, **k: r.put("C", *p, **k)
                root_refine(r, "C", var[:], rstd[:], tmp[:], "rstd")
                for q in range(TQ):
                    put("vector", lambda e, b, q=q: e.tensor_scalar(y[:, q, :], res[:, q, :], mv[:, q, 0:1], rstd[:, q:q + 1], ALU.subtract, ALU.mult),
                        after=["rstd", ("y_out", -1), (f"sq{q}", -1)], done=f"n{q}")
                    put("gpsimd", lambda e, b, q=q: e.tensor_tensor(y[:, q, :], y[:, q, :], gamma[:], ALU.mult), after=[f"n{q}"], done=f"g{q}")
                    put("gpsimd", lambda e, b, q=q: e.tensor_tensor(y[:, q, :], y[:, q, :], beta[:], ALU.add), after=[f"g{q}"], done=f"y{q}")
                put("sync", lambda e, b: e.dma_start(scratch["y"][row(b)].rearrange("b p q d -> (b p) q d"), y[:]), after=["y3"], dma="y_out")
                yield
                for q in range(TQ):
                    put("scalar", lambda e, b, q=q: e.activation(sq[:], y[:, q, :], ACT.Square, scale=D ** -0.5, accum_out=ms[:, q:q + 1]),
                        after=[f"y{q}", f"sq{q - 1}" if q else ("sq3", -1)] + ([("rms", -1)] if q == 0 else []), done=f"sq{q}")
                yield
                put("vector", lambda e, b: e.tensor_scalar(rms[:], ms[:], EPS, None, ALU.add), after=["sq3", ("rinv", -1)], done="rms")
                root_guess(r, "C", rms[:], rinv[:], ["rms", ("rinv_out", -1)], "rinv")
                yield

            def store_rms():
                root_refine(r, "R", rms[:], rinv[:], tmp2[:], "rinv")
                r.put("R", "sync", lambda e, b: e.dma_start(scratch["rinv"][row(b)].rearrange("b p q -> (b p) q"), rinv[:]), after=["rinv"], dma="rinv_out")
                yield

            interleave("BC A BB A BB A BB A BX V AA B AA R B AAA C B AAA B V AA C AAAA B K",
                       A=scores(), B=values_out(), C=normalise(), X=load_split(), K=load_keys(), V=load_values(), R=store_rms())
            r.emit()


def split_weights(w, items):
    for name, src, raw, (hi, lo), number, column in items:
        n = src.shape[2]
        w.put("W", "sync", lambda e, b, src=src, raw=raw, n=n: e.dma_start(raw[:, :, 0:n] if raw.shape[2] != n else raw[:], src), dma=name)
        for k in range(src.shape[1]):
            w.put("W", "vector", lambda e, b, k=k, raw=raw, n=n, number=number, column=column: e.tensor_scalar(
                raw[:, k, 0:n], raw[:, k, 0:n], number, None if column is None else column[:, k:k + 1],
                ALU.mult, ALU.bypass if column is None else ALU.mult),
                after=[name] + ([] if column is None else ["columns"]), done=f"{name}_s{k}")
            w.put("W", "scalar", lambda e, b, k=k, raw=raw, n=n, hi=hi: e.activation(hi[:, k, 0:n], raw[:, k, 0:n], ACT.Copy),
                  after=[f"{name}_s{k}"], done=f"{name}_h{k}")
            w.put("W", "vector", lambda e, b, k=k, raw=raw, n=n, hi=hi, lo=lo: e.tensor_tensor(
                lo[:, k, 0:n], raw[:, k, 0:n], hi[:, k, 0:n].bitcast(F32), ALU.subtract), after=[f"{name}_h{k}"], done=f"{name}_l{k}")


def mamba(nc, a, scratch, rows):
    XC, BC, CC, DC = DI, 2 * DI, 2 * DI + NS, 2 * DI + 2 * NS
    NCONV = CONVD // P
    with ExitStack() as ctx:
        def sb(name, shape, dt=F32):
            return ctx.enter_context(nc.sbuf_tensor(f"mb_{name}", shape, dt))
        wi = [sb(f"wi{h}", [P, KT, DC + P], F32R) for h in "hl"]
        wo = sb("wo", [P, MI, D])
        cw, cb, skip = sb("cw", [P, NCONV, TAPS]), sb("cb", [P, NCONV]), sb("skip", [P, MI])
        dtb, am = sb("dtb", [P, 1]), sb("am", [P, 1])
        eyes = sb("eyes", [P, TQ, P])
        eye = eyes[:, 0, :]
        ones = sb("ones", [P, 1])
        sel = sb("sel", [P, HM], F32R)
        selp = sb("selp", [P, MI, P], F32R)
        d1 = sb("d1", [P, S])
        ps = ctx.enter_context(nc.psum_tensor("mb_ps", [P, 8, 512], F32))

        with ExitStack() as c2:
            raw = c2.enter_context(nc.sbuf_tensor("mb_raw", [P, KT, DC + HM], F32))
            nw, gw = c2.enter_context(nc.sbuf_tensor("mb_nw", [P, KT], F32)), c2.enter_context(nc.sbuf_tensor("mb_gw", [P, MI], F32))
            sel_f = c2.enter_context(nc.sbuf_tensor("mb_self", [P, HM], F32))
            w = Region(nc, c2, "mbw", 1, {"W": 0})
            put = lambda *p, **k: w.put("W", *p, **k)
            put("scalar", lambda e, b: e.dma_start(nw[:], tiles(a["norm1"]), allow_slow_non_contiguous=True), dma="columns")
            put("scalar", lambda e, b: e.dma_start(gw[:], tiles(a["gnorm1"]), allow_slow_non_contiguous=True), dma="gw")
            for n in range(2):
                put("vector", lambda e, b, n=n: e.memset(wi[n][:, :, DC:].bitcast(F32), 0.0), done=f"wz{n}")
            split_weights(w, [("wi", a["Win"].rearrange("(k p) n -> p k n", p=P), raw, wi, 1.0, nw)])
            for k in range(KT):
                again = slice(DC + 32, DC + 32 + HM)
                put("scalar", lambda e, b, k=k: e.activation(wi[0][:, k, again], raw[:, k, DC:DC + HM], ACT.Copy), after=[f"wi_s{k}", "wz1"], done=f"dh{k}")
                put("vector", lambda e, b, k=k: e.tensor_tensor(wi[1][:, k, again], raw[:, k, DC:DC + HM], wi[0][:, k, again].bitcast(F32), ALU.subtract),
                    after=[f"dh{k}"], done=f"dl{k}")
            put("sync", lambda e, b: e.dma_start(wo[:], a["Wout"].rearrange("(k p) n -> p k n", p=P)), dma="wo")
            for k in range(MI):
                put("gpsimd", lambda e, b, k=k: e.tensor_tensor(wo[:, k, :], wo[:, k, :], gw[:, k:k + 1].broadcast_to([P, D]), ALU.mult), after=["wo", "gw"])
            put("sync", lambda e, b: e.dma_start(cw[:], a["cw"].rearrange("(j p) k -> p j k", p=P)), dma="cw")
            put("scalar", lambda e, b: e.dma_start(cb[:], tiles(a["cb"]), allow_slow_non_contiguous=True), dma="cb")
            for c in range(TQ):
                put("sync", lambda e, b, c=c: e.dma_start(eyes[:, c, :], a["eye"]), dma=f"eyes{c}")
            for j in range(2):
                put("scalar", lambda e, b, j=j: e.dma_start(skip[j * 64:(j + 1) * 64, :], a["skip"].rearrange("(m j) -> j m", j=2)[j:j + 1, :].broadcast_to([64, MI]),
                    allow_slow_non_contiguous=True), dma=f"skip{j}")
            put("vector", lambda e, b: e.memset(dtb[:], 0.0), done="z0")
            put("vector", lambda e, b: e.memset(am[:], 0.0), done="z1")
            put("vector", lambda e, b: e.memset(sel_f[:], 0.0), done="z2")
            put("vector", lambda e, b: e.memset(ones[:], 1.0))
            put("vector", lambda e, b: e.memset(d1[:], 0.0))
            for n, at in enumerate((0, 32)):
                put("sync", lambda e, b, at=at: e.dma_start(dtb[at:at + HM, :], a["dtb"].rearrange("(n a) -> n a", a=1)), after=["z0"], dma=f"dtb{n}")
                put("sync", lambda e, b, at=at: e.dma_start(am[at:at + HM, :], a["alog"].rearrange("(n a) -> n a", a=1)), after=["z1"], dma=f"am{n}")
                put("sync", lambda e, b, at=at: e.dma_start(sel_f[at:at + HM, :], a["eye"][0:HM, 0:HM]), after=["z2"], dma=f"sel{n}")
            put("scalar", lambda e, b: e.activation(sel[:], sel_f[:], ACT.Copy), after=["sel0", "sel1"])
            put("scalar", lambda e, b: e.activation(selp[:].rearrange("p m (j d) -> p (m j) d", j=2), sel_f[:].unsqueeze(2).broadcast_to([P, HM, 64]), ACT.Copy),
                after=["sel0", "sel1"])
            for n, at in enumerate((0, 32)):
                put("scalar", lambda e, b, at=at: e.activation(am[at:at + HM, :], am[at:at + HM, :], ACT.Exp), after=[f"am{n}"], done=f"ae{n}")
                put("vector", lambda e, b, at=at: e.tensor_scalar(am[at:at + HM, :], am[at:at + HM, :], -1.0, None, ALU.mult), after=[f"ae{n}"])
            w.emit()

        y = sb("y", [P, 2, D])
        ri = sb("ri", [P, TQ])
        yt = [sb(f"y{h}", [P, KT, S], F32R) for h in "hl"]
        cv, xs, sz = sb("cv", [P, 2, S]), sb("xs", [P, 3, S]), sb("sz", [P, 3, S])
        lm, gm = sb("lm", [P, 2, S]), sb("gm", [P, 2, 2, S])
        xp = sb("xp", [P, 2, TQ, P])
        xw = sb("xw", [P, 2, TQ - 1, P])
        pb, hs, yw = sb("pb", [P, S]), sb("hs", [P, TQ - 1, P]), sb("yw", [P, S])
        u, sq, ssq = sb("u", [P, MI, S]), sb("sq", [P, S]), sb("ssq", [P, S])
        bt, ct, bk, g = sb("bt", [P, S]), sb("ct", [P, S]), sb("bk", [P, TQ, P]), sb("g", [P, S])
        v, ex, ul = sb("v", [P, S]), sb("ex", [P, S]), sb("ul", [P, S])
        dec2, pre2 = sb("dec2", [P, S], F32R), sb("pre2", [P, S], F32R)
        dtT, dg, dl = sb("dtT", [P, TQ, HM]), sb("dg", [HM, TQ, HM]), sb("dl", [P, TQ, HM])
        o, so = sb("o", [P, 2, D]), sb("so", [P, TQ])
        starts, ends = slice(0, S, P), slice(P - 1, S, P)

        with ExitStack() as c2:
            r = Region(nc, c2, "mb", rows, {"A": 0, "F": 0, "P": 1, "S": 1, "O": 1})

            def project(put, tag, bank, column, after):
                for k in range(KT):
                    put("tensor", lambda e, b, k=k: mm3(e, ps[:, bank, :], [w_[:, k, column:column + P] for w_ in wi],
                        [y_[:, k, :] for y_ in yt], k == 0, k == KT - 1), after=after, done=tag if k == KT - 1 else None)

            def convolve(put, tag, bank, j, ring, free):
                last = TAPS - 1
                put("scalar", lambda e, b: e.activation(cv[:, ring, :], ps[:, bank, :], ACT.Identity, bias=cb[:, j:j + 1], scale=cw[:, j, last:last + 1]),
                    after=[tag, free], done=f"{tag}_t{last}")
                for k in reversed(range(last)):
                    n = last - k
                    put("vector", lambda e, b, k=k, n=n: e.scalar_tensor_tensor(out=cv[:, ring, n:S], in0=ps[:, bank, 0:S - n], scalar=cw[:, j, k:k + 1],
                        in1=cv[:, ring, n:S], op0=ALU.mult, op1=ALU.add), after=[f"{tag}_t{k + 1}"], done=f"{tag}_t{k}")

            def prepare():
                put = lambda *p, **k: r.put("A", *p, **k)

                def load(q):
                    put("sync", lambda e, b: e.dma_start(y[:, q % 2, :], scratch["y"][row(b), :, q, :].rearrange("b p d -> (b p) d")),
                        after=[f"yt{q - 2}" if q >= 2 else (f"yt{q + 2}", -1)], dma=f"y{q}")

                def scale(q):
                    put("vector", lambda e, b: e.tensor_scalar(y[:, q % 2, :], y[:, q % 2, :], ri[:, q:q + 1], None, ALU.mult), after=["ri", f"y{q}"], done=f"ys{q}")

                put("sync", lambda e, b: e.dma_start(ri[:], scratch["rinv"][row(b)].rearrange("b p q -> (b p) q")), after=[("ys3", -1)], dma="ri")
                load(0)
                load(1)
                yield
                scale(0)
                scale(1)
                yield
                for q in range(TQ):
                    if q == 2:
                        scale(2)
                        scale(3)
                        yield
                    for k in range(KT):
                        put("tensor", lambda e, b, q=q, k=k: e.transpose(ps[:, q % 2, k * P:(k + 1) * P], y[:, q % 2, k * P:(k + 1) * P], eye),
                            after=[f"ys{q}"] + ([f"yl{q - 2}"] if q >= 2 else [("sz7", -1), ("x7_t0", -1)]),
                            done=f"yt{q}" if k == KT - 1 else None)
                    cols = slice(q * P, (q + 1) * P)
                    src = ps[:, q % 2, :].rearrange("p (k t) -> p k t", k=KT)
                    put("scalar", lambda e, b, cols=cols, src=src: e.activation(yt[0][:, :, cols], src, ACT.Copy), after=[f"yt{q}", ("z7", -1)], done=f"yh{q}")
                    put("vector", lambda e, b, cols=cols, src=src: e.tensor_tensor(yt[1][:, :, cols], src, yt[0][:, :, cols].bitcast(F32), ALU.subtract),
                        after=[f"yh{q}"], done=f"yl{q}")
                    if q < 2:
                        load(q + 2)
                    yield
                project(put, "dt", 2, DC, ["yl3", ("xp7", -1), ("dl", -1)])
                put("vector", lambda e, b: e.tensor_scalar(v[:], ps[:, 2, :], dtb[:, 0:1], None, ALU.add), after=["dt", ("dlm", -1)], done="v")
                put("vector", lambda e, b: e.scalar_tensor_tensor(out=ex[:], in0=v[:], scalar=-1.0, in1=v[:], op0=ALU.mult, op1=ALU.min), after=["v", ("dec", -1), ("d1", -1)], done="na")

                put("scalar", lambda e, b: e.activation(ex[:], ex[:], ACT.Exp), after=["na"], done="e",
                    first=lambda e: e.preload_act_table_set("natural_log_exp_and_others"))
                put("vector", lambda e, b: e.tensor_scalar(ul[:], ex[:], 1.0, None, ALU.add), after=["e"], done="1e")
                put("vector", lambda e, b: e.scalar_tensor_tensor(out=ex[:], in0=ul[:], scalar=1.0, in1=ex[:], op0=ALU.subtract, op1=ALU.subtract), after=["1e"], done="lost")
                put("scalar", lambda e, b: e.activation(ul[:], ul[:], ACT.Ln), after=["lost"], done="ln")
                put("vector", lambda e, b: e.tensor_tensor(ul[:], ul[:], ex[:], ALU.subtract), after=["ln"], done="l1")
                put("vector", lambda e, b: e.scalar_tensor_tensor(out=v[:], in0=v[:], scalar=0.0, in1=ul[:], op0=ALU.max, op1=ALU.add), after=["l1"], done="dtv")
                put("scalar", lambda e, b: e.activation(ex[:], v[:], ACT.Exp, scale=am[:, 0:1]), after=["dtv"], done="dec")
                yield
                for n, (tag, col, dst) in enumerate((("C", CC, ct), ("B", BC, bt))):
                    project(put, tag, n, col, ["yl2", "yl3"])
                    convolve(put, tag, n, (col - XC) // P, n, ("xs%d" % (6 + n), -1))
                    put("scalar", lambda e, b, n=n, dst=dst: e.activation(dst[:], cv[:, n, :], ACT.Silu),
                        after=[f"{tag}_t0", ("Yo7", -1), ("G", -1), ("bT", -1)], done=tag + "s")
                    yield
                put("vector", lambda e, b: e.tensor_copy(d1[:, starts], ex[:, starts]), after=["dec"], done="d1")
                put("vector", lambda e, b: e.memset(ex[:, starts], 0.0), after=["d1"], done="dec0")
                put("vector", lambda e, b: e.tensor_copy(dec2[:], ex[:]), after=["dec0", ("L15", -1)], done="dech")
                put("vector", lambda e, b: e.tensor_tensor(dec2[32:64, :], ex[32:64, :], dec2[32:64, :].bitcast(F32), ALU.subtract), after=["dech"], done="dec2")
                put("vector", lambda e, b: e.tensor_tensor_scan(ul[:], ex[:], d1[:], 0.0, ALU.mult, ALU.add), after=["dec0"], done="pre")
                put("vector", lambda e, b: e.tensor_copy(pre2[:], ul[:]), after=["pre", ("Pb7", -1)], done="preh")
                put("vector", lambda e, b: e.tensor_tensor(pre2[32:64, :], ul[32:64, :], pre2[32:64, :].bitcast(F32), ALU.subtract), after=["preh"], done="pre2")
                put("vector", lambda e, b: e.tensor_tensor(dg[:], eye[0:HM, 0:HM].unsqueeze(1).broadcast_to([HM, TQ, HM]),
                    ul[0:HM, ends].unsqueeze(2).broadcast_to([HM, TQ, HM]), ALU.mult), after=["pre", ("dlm", -1)], done="dg")
                put("tensor", lambda e, b: e.matmul(ps[:, 2, TQ * HM:2 * TQ * HM], ones[0:HM, :].broadcast_to([HM, P]), dg[:], start=True, stop=True), after=["v", "dtv", "dg"])
                for c in range(TQ):
                    put("tensor", lambda e, b, c=c: e.transpose(ps[:, 2, c * HM:(c + 1) * HM], v[0:HM, c * P:(c + 1) * P], eye[0:HM, 0:HM]),
                        done="dlm" if c == TQ - 1 else None)
                put("vector", lambda e, b: e.tensor_copy(dtT[:], ps[:, 2, 0:TQ * HM].rearrange("p (c h) -> p c h", c=TQ)), after=["dlm", ("xp7", -1)], done="dtT")
                put("vector", lambda e, b: e.tensor_copy(dl[:], ps[:, 2, TQ * HM:2 * TQ * HM].rearrange("p (c h) -> p c h", c=TQ)), after=["dlm", ("H7", -1)], done="dl")
                for c in range(TQ):
                    put("tensor", lambda e, b, c=c: e.matmul(ps[:, 0, c * P:(c + 1) * P], bt[:, c * P:(c + 1) * P], ct[:, c * P:(c + 1) * P], start=True, stop=True),
                        after=["Cs", "Bs", "C_t0"], done="G" if c == TQ - 1 else None)
                for c in range(TQ):
                    put("tensor", lambda e, b, c=c: e.transpose(ps[:, 1, c * P:(c + 1) * P], bt[:, c * P:(c + 1) * P], eye),
                        after=["Bs", "B_t0"], done="bT" if c == TQ - 1 else None)
                put("scalar", lambda e, b: e.activation(g[:], ps[:, 0, :], ACT.Copy), after=["G", ("gm15", -1)], done="g")
                put("scalar", lambda e, b: e.activation(bk[:], ps[:, 1, :].rearrange("p (c n) -> p c n", c=TQ), ACT.Copy), after=["bT", ("St7", -1)], done="bk")
                yield

            def inner(stage, tiles_m):
                put = lambda *p, **k: r.put(stage, *p, **k)
                for m in tiles_m:
                    n, f = m % 2, m % 3
                    project(put, f"x{m}", 0, XC + m * P, ["yl3", f"x{m - 1}_t0" if m else "g"])
                    convolve(put, f"x{m}", 0, m, n, f"xs{m - 2}" if m >= 2 else "Cs" if m == 0 else "Bs")
                    put("scalar", lambda e, b, n=n, f=f: e.activation(xs[:, f, :], cv[:, n, :], ACT.Silu),
                        after=[f"x{m}_t0"] + [f"w{m - 3}" if m >= 3 else (f"w{(6, 7, 5)[m]}", -1)], done=f"xs{m}")
                    yield
                    project(put, f"z{m}", 1, m * P, [f"sz{m - 1}" if m else "bk"])
                    put("scalar", lambda e, b, f=f: e.activation(sz[:, f, :], ps[:, 1, :], ACT.Silu),
                        after=[f"z{m}"] + [f"u{m - 3}" if m >= 3 else (f"u{(6, 7, 5)[m]}", -1)], done=f"sz{m}")
                    yield

            def scan():
                put = lambda *p, **k: r.put("S", *p, **k)

                def prev(m, tag, d=1):
                    return f"{tag}{m - d}" if m >= d else (f"{tag}{m - d + MI}", -1)

                def weights(m):
                    n, f = m % 2, m % 3
                    for j in range(2):
                        h = 2 * m + j
                        put("tensor", lambda e, b, j=j, h=h: e.matmul(ps[:, 3 + j, :], sel[:, h:h + 1].broadcast_to([P, P]), dec2[:], start=True, stop=True),
                            after=["dec2", f"pb{m - 2}" if m >= 2 else ("pb7", -1), f"L{h - 2}" if h >= 2 else (f"L{h + 14}", -1)], done=f"De{h}")
                        put("vector", lambda e, b, j=j: e.tensor_tensor_scan(lm[:, j, :], ps[:, 3 + j, :], eyes[:].rearrange("p c t -> p (c t)"), 0.0, ALU.mult, ALU.add),
                            after=[f"De{h}", f"gm{h - 2}" if h >= 2 else (f"gm{h + 14}", -1), prev(m, "xw")], done=f"L{h}")
                    for c in range(TQ):
                        put("tensor", lambda e, b, c=c: e.transpose(ps[:, 2, c * P:(c + 1) * P], xs[:, f, c * P:(c + 1) * P], eye),
                            after=[f"xs{m}", prev(m, "xp"), "dl", "dtT"], done=f"tx{m}" if c == TQ - 1 else None)
                    put("vector", lambda e, b, m=m, n=n: e.tensor_tensor(xp[:, n, :, :].rearrange("p c (j d) -> p c j d", j=2),
                        ps[:, 2, :].rearrange("p (c j d) -> p c j d", c=TQ, j=2),
                        dtT[:, :, 2 * m:2 * m + 2].unsqueeze(3).broadcast_to([P, TQ, 2, 64]), ALU.mult),
                        after=[f"tx{m}", prev(m, "Yi", 2)], done=f"xp{m}")
                    for j in range(2):
                        put("gpsimd", lambda e, b, j=j, n=n: e.tensor_tensor(xw[:, n, :, j * 64:(j + 1) * 64], xp[:, n, 0:TQ - 1, j * 64:(j + 1) * 64],
                            lm[:, j, P - 1:(TQ - 1) * P:P].unsqueeze(2).broadcast_to([P, TQ - 1, 64]), ALU.mult),
                            after=[f"xp{m}", f"L{2 * m + j}", prev(m, "St", 2)], done=f"xw{m}" if j else f"xw{m}_0")
                        put("gpsimd", lambda e, b, j=j, n=n: e.tensor_tensor(gm[:, n, j, :], lm[:, j, :], g[:], ALU.mult),
                            after=["g", prev(m, "Yi", 2)], done=f"gm{2 * m + j}")

                def states(m):
                    n = m % 2
                    for c in range(TQ - 1):
                        put("tensor", lambda e, b, n=n, c=c: e.matmul(ps[:, 7, c * P:(c + 1) * P], bk[:, c, :], xw[:, n, c, :], start=True, stop=True),
                            after=["bk", f"xw{m}", prev(m, "H")], done=f"St{m}" if c == TQ - 2 else None)
                    put("vector", lambda e, b: e.tensor_copy(hs[:, 0, :], ps[:, 7, 0:P]), after=[f"St{m}", prev(m, "Yo")], done=f"H{m}_1")
                    for c in range(1, TQ - 1):
                        for j in range(2):
                            cols = slice(j * 64, (j + 1) * 64)
                            put("vector", lambda e, b, c=c, j=j, m=m, cols=cols: e.scalar_tensor_tensor(out=hs[:, c, cols], in0=hs[:, c - 1, cols],
                                scalar=dl[:, c, 2 * m + j:2 * m + j + 1], in1=ps[:, 7, c * P + j * 64:c * P + (j + 1) * 64], op0=ALU.mult, op1=ALU.add),
                                after=[f"H{m}_{c}", "dl"], done=None if j == 0 else f"H{m}_{c + 1}" if c < TQ - 2 else f"H{m}")

                def outputs(m):
                    n, f = m % 2, m % 3
                    for c in range(TQ):
                        for j in range(2):
                            rows_j = slice(j * 64, (j + 1) * 64)
                            put("tensor", lambda e, b, c=c, j=j, n=n, rows_j=rows_j: e.matmul(ps[rows_j, 5, c * P:(c + 1) * P], xp[:, n, c, rows_j],
                                gm[:, n, j, c * P:(c + 1) * P], start=True, stop=True),
                                after=[f"xp{m}", f"gm{2 * m + 1}", prev(m, "w")], done=f"Yi{m}" if (c, j) == (TQ - 1, 1) else None)
                    put("tensor", lambda e, b, m=m: e.matmul(ps[:, 3, :], selp[:, m, :], pre2[:], start=True, stop=True),
                        after=["pre2", f"L{min(2 * m + 2, HM - 2)}", prev(m, "pb")], done=f"Pb{m}")
                    put("scalar", lambda e, b: e.activation(pb[:], ps[:, 3, :], ACT.Copy), after=[f"Pb{m}", prev(m, "t")], done=f"pb{m}")
                    for c in range(1, TQ):
                        put("tensor", lambda e, b, c=c: e.matmul(ps[:, 6, c * P:(c + 1) * P], hs[:, c - 1, :], ct[:, c * P:(c + 1) * P], start=True, stop=True),
                            after=["Cs", f"H{m}", prev(m, "t")], done=f"Yo{m}" if c == TQ - 1 else None)
                    late = slice(P, S)
                    put("vector", lambda e, b: e.scalar_tensor_tensor(out=yw[:, 0:P], in0=xs[:, f, 0:P], scalar=skip[:, m:m + 1],
                        in1=ps[:, 5, 0:P], op0=ALU.mult, op1=ALU.add), after=[f"Yi{m}", f"xs{m}", prev(m, "u")], done=f"w{m}_0")
                    put("vector", lambda e, b: e.tensor_tensor(yw[:, late], ps[:, 6, late], pb[:, late], ALU.mult), after=[f"Yo{m}", f"pb{m}"], done=f"t{m}")
                    put("vector", lambda e, b: e.tensor_tensor(yw[:, late], yw[:, late], ps[:, 5, late], ALU.add), after=[f"t{m}"], done=f"ty{m}")
                    put("vector", lambda e, b: e.scalar_tensor_tensor(out=yw[:, late], in0=xs[:, f, late], scalar=skip[:, m:m + 1],
                        in1=yw[:, late], op0=ALU.mult, op1=ALU.add), after=[f"ty{m}"], done=f"w{m}")
                    put("gpsimd", lambda e, b: e.tensor_tensor(u[:, m, :], yw[:], sz[:, f, :], ALU.mult), after=[f"w{m}", f"sz{m}", ("o3", -1)], done=f"u{m}")
                    put("scalar", lambda e, b, m=m: e.activation(sq[:] if m else ssq[:], u[:, m, :], ACT.Square),
                        after=[f"u{m}", f"sa{m - 1}" if m > 1 else ("so_mm", -1)], done=f"sq{m}")
                    if m:
                        put("gpsimd", lambda e, b: e.tensor_tensor(ssq[:], ssq[:], sq[:], ALU.add), after=[f"sq{m}", f"sq{m - 1}" if m == 1 else f"sa{m - 1}"], done=f"sa{m}")

                for m in range(MI + 1):
                    if m < MI:
                        weights(m)
                    if m:
                        states(m - 1)
                    if m < MI:
                        yield
                    if m:
                        outputs(m - 1)
                        yield


            def out():
                put = lambda *p, **k: r.put("O", *p, **k)
                for q in range(TQ):
                    for k in range(MI):
                        put("tensor", lambda e, b, q=q, k=k: e.matmul(ps[:, 5 + q % 2, :], u[:, k, q * P:(q + 1) * P], wo[:, k, :], start=(k == 0), stop=(k == MI - 1)),
                            after=["u7", "w7", "t7", f"oc{q - 2}" if q >= 2 else "w7"], done=f"o{q}" if k == MI - 1 else None)
                    put("scalar", lambda e, b, q=q: e.activation(o[:, q % 2, :], ps[:, 5 + q % 2, :], ACT.Copy),
                        after=[f"o{q}", f"o_out{q - 2}" if q >= 2 else (f"o_out{q + 2}", -1)], done=f"oc{q}")
                    put("sync", lambda e, b, q=q: e.dma_start(scratch["o"][row(b), :, q, :].rearrange("b p d -> (b p) d"), o[:, q % 2, :]), after=[f"oc{q}"], dma=f"o_out{q}")
                    if q == 0:
                        for c in range(TQ):
                            put("tensor", lambda e, b, c=c: e.matmul(ps[:, 7, c:c + 1], ssq[:, c * P:(c + 1) * P], ones[:], start=True, stop=True),
                                after=["sa7", "H7"], done="so_mm" if c == TQ - 1 else None)
                        put("vector", lambda e, b: e.tensor_copy(so[:], ps[:, 7, 0:TQ]), after=["so_mm", ("so_out", -1)], done="so")
                        put("sync", lambda e, b: e.dma_start(scratch["ssq"][row(b)].rearrange("b p q -> (b p) q"), so[:]), after=["so"], dma="so_out")
                    yield

            interleave("P" "S" "PSPS" "PSPS" "PSPS" "PSPS" "A" "PSPS" "A" "PSPS" "P" "S" "S" "AAA" "S" "AA" "A A A O O A FF O O",
                       A=prepare(), F=inner("F", [0]), P=inner("P", range(1, MI)), S=scan(), O=out())
            r.emit()


def layer1(nc, a, scratch, out, rows):
    with ExitStack() as ctx:
        def sb(name, shape, dt=F32):
            return ctx.enter_context(nc.sbuf_tensor(f"l1_{name}", shape, dt))
        wq, wo = ([sb(f"{n}{h}", [P, KT, D], F32R) for h in "hl"] for n in ("wq", "wo"))
        qb = sb("qb", [P, KT])
        eye = sb("eye", [P, P])
        keep, neg = sb("keep", [P, C]), sb("neg", [P, C])
        o_in, y_in, ss = sb("o_in", [P, TQ, D]), sb("y_in", [P, TQ, D]), sb("ss", [P, TQ])
        ha, hb = sb("ha", [P, TQ, D]), sb("hb", [P, TQ, D])
        xn = sb("xn", [P, TQ, D])
        xt = [sb(f"x{h}", [P, KT, S], F32R) for h in "hl"]
        qt = sb("qt", [P, KT, S])
        kd, km = sb("kd", [P, KT, 2 * C]), sb("km", [P, KT, 2 * C])
        v = sb("v", [C, D])
        sc = sb("sc", [P, TQ, H1, C])
        mx, sm, rs = sb("mx", [P, TQ, H1]), sb("sm", [P, TQ, H1]), sb("rs", [P, TQ, H1])
        pt = sb("pt", [C, H1, S])
        cs = [sb(f"c{h}", [P, KT, S], F32R) for h in "hl"]
        ot = sb("ot", [P, TQ, D])
        vu, ru, t1 = sb("vu", [P, TQ]), sb("ru", [P, TQ]), sb("t1", [P, TQ])
        st, mv = sb("st", [P, TQ, 6]), sb("mv", [P, TQ, 2])
        var, rstd, t2 = sb("var", [P, TQ]), sb("rstd", [P, TQ]), sb("t2", [P, TQ])
        ps = ctx.enter_context(nc.psum_tensor("l1_ps", [P, 8, 512], F32))

        with ExitStack() as c2:
            mask = c2.enter_context(nc.sbuf_tensor("l1_mask", [P, C], U8))
            lw, lb = c2.enter_context(nc.sbuf_tensor("l1_lw", [P, KT], F32)), c2.enter_context(nc.sbuf_tensor("l1_lb", [P, KT], F32))
            w = Region(nc, c2, "l1w", 1, {"W": 0})
            put = lambda *p, **k: w.put("W", *p, **k)
            put("scalar", lambda e, b: e.dma_start(lw[:], tiles(a["lnw"]), allow_slow_non_contiguous=True), dma="lw")
            put("scalar", lambda e, b: e.dma_start(lb[:], tiles(a["lnb"]), allow_slow_non_contiguous=True), dma="lb")
            put("scalar", lambda e, b: e.dma_start(mask[:], a["kmask"].broadcast_to([P, C])), dma="mask")
            put("sync", lambda e, b: e.dma_start(xn[:], a["Wq1"].rearrange("(k p) n -> p k n", p=P)), dma="wq_raw")
            put("sync", lambda e, b: e.dma_start(eye[:], a["eye"]), dma="eye")
            for m in range(KT):
                for k in range(KT):
                    put("tensor", lambda e, b, m=m, k=k: e.matmul(ps[:, 0, m:m + 1], xn[:, k, m * P:(m + 1) * P], lb[:, k:k + 1], start=(k == 0), stop=(k == KT - 1)),
                        after=["wq_raw", "lb"], done="qb_mm" if (m, k) == (KT - 1, KT - 1) else None)
            put("vector", lambda e, b: e.tensor_scalar(qb[:], ps[:, 0, 0:KT], HD1 ** -0.5, None, ALU.mult), after=["qb_mm"], done="qb")
            put("vector", lambda e, b: e.tensor_scalar(lw[:], lw[:], 1.0, None, ALU.mult), after=["lw"], done="columns")
            split_weights(w, [("wq", a["Wq1"].rearrange("(k p) n -> p k n", p=P), ha, wq, HD1 ** -0.5, lw),
                              ("wo", a["Wo1"].rearrange("(k p) n -> p k n", p=P), hb, wo, 1.0, None)])
            put("vector", lambda e, b: e.tensor_copy(neg[:], mask[:]), after=["mask"], done="mf")
            put("vector", lambda e, b: e.tensor_scalar(keep[:], neg[:], -1.0, 1.0, ALU.mult, ALU.add), after=["mf"], done="keep")
            put("vector", lambda e, b: e.tensor_scalar(neg[:], neg[:], MASKED, None, ALU.mult), after=["keep"])
            put("gpsimd", lambda e, b: e.memset(kd[:], 0.0))
            w.emit()

        with ExitStack() as c2:
            r = Region(nc, c2, "l1", rows, {"A": 0, "B": 1}, "natural_log_exp_and_others")

            def attend():
                put = lambda *p, **k: r.put("A", *p, **k)
                rows_of = lambda t, b: t[row(b)].rearrange("b p q d -> (b p) q d")
                put("sync", lambda e, b: e.dma_start(ss[:], scratch["ssq"][row(b)].rearrange("b p q -> (b p) q")), after=[("vu", -1)], dma="ss")
                put("sync", lambda e, b: e.dma_start(o_in[:], rows_of(scratch["o"], b)), after=[("h3", -1)], dma="o_in")
                put("sync", lambda e, b: e.dma_start(y_in[:], rows_of(scratch["y"], b)), after=[("h3", -1)], dma="y_in")
                for j in range(2):
                    put("sync", lambda e, b, j=j: e.dma_start(kd[j * HD1:(j + 1) * HD1, :, j * C:(j + 1) * C],
                        scratch["k1"].rearrange("m p t -> p m t")[j * HD1:(j + 1) * HD1, :, row(b * C, C)]), after=[("km", -1)], dma=f"kd{j}")
                put("gpsimd", lambda e, b: e.tensor_tensor(km[:].rearrange("p m (j c) -> p (m j) c", j=2), kd[:].rearrange("p m (j c) -> p (m j) c", j=2),
                    keep[:].unsqueeze(1).broadcast_to([P, 2 * KT, C]), ALU.mult), after=["kd0", "kd1", (f"S{TQ - 1}", -1)], done="km")
                put("vector", lambda e, b: e.tensor_scalar(vu[:], ss[:], 1.0 / DI, EPS, ALU.mult, ALU.add), after=["ss", ("ru", -1)], done="vu")
                root_guess(r, "A", vu[:], ru[:], ["vu", ("h3", -1)], "ru")
                yield
                root_refine(r, "A", vu[:], ru[:], t1[:], "ru")
                for q in range(TQ):
                    put("vector", lambda e, b, q=q: e.scalar_tensor_tensor(out=ha[:, q, :], in0=o_in[:, q, :], scalar=ru[:, q:q + 1], in1=y_in[:, q, :],
                        op0=ALU.mult, op1=ALU.add), after=["ru", "o_in", "y_in", (f"hb{q}", -1)], done=f"h{q}")
                    put("vector", lambda e, b, q=q: e.bn_stats(st[:, q, :], ha[:, q, :]), after=[f"h{q}"], done=f"st{q}")
                for q in range(TQ):
                    put("vector", lambda e, b, q=q: e.bn_aggr(mv[:, q, :], st[:, q, :]), after=[f"st{q}"], done=f"mv{q}", apart=q)
                put("vector", lambda e, b: e.tensor_scalar(var[:], mv[:, :, 1], EPS, None, ALU.add), after=["mv3"], done="var")
                root_guess(r, "A", var[:], rstd[:], ["var"], "rstd")
                yield
                root_refine(r, "A", var[:], rstd[:], t2[:], "rstd")
                for q in range(TQ):
                    put("vector", lambda e, b, q=q: e.tensor_scalar(xn[:, q, :], ha[:, q, :], mv[:, q, 0:1], rstd[:, q:q + 1], ALU.subtract, ALU.mult),
                        after=["rstd", (f"tr{q}", -1)], done=f"n{q}")
                yield
                for q in range(TQ):
                    for k in range(KT):
                        put("tensor", lambda e, b, q=q, k=k: e.transpose(ps[:, q % 2, k * P:(k + 1) * P], xn[:, q, k * P:(k + 1) * P], eye[:]),
                            after=[f"n{q}", f"xl{q - 2}" if q >= 2 else (f"qt{q + 2}", -1)], done=f"tr{q}" if k == KT - 1 else None)
                    cols = slice(q * P, (q + 1) * P)
                    src = ps[:, q % 2, :].rearrange("p (k t) -> p k t", k=KT)
                    put("scalar", lambda e, b, cols=cols, src=src: e.activation(xt[0][:, :, cols], src, ACT.Copy), after=[f"tr{q}", ("q3", -1)], done=f"xh{q}")
                    put("vector", lambda e, b, cols=cols, src=src: e.tensor_tensor(xt[1][:, :, cols], src, xt[0][:, :, cols].bitcast(F32), ALU.subtract),
                        after=[f"xh{q}"], done=f"xl{q}")
                    if q % 2:
                        yield
                for m in range(KT):
                    for k in range(KT):
                        put("tensor", lambda e, b, m=m, k=k: mm3(e, ps[:, m % 2, :], [w_[:, k, m * P:(m + 1) * P] for w_ in wq],
                            [x_[:, k, :] for x_ in xt], k == 0, k == KT - 1),
                            after=["xl3", f"qt{m - 2}" if m >= 2 else "xl3"], done=f"q{m}" if k == KT - 1 else None)
                    put("scalar", lambda e, b, m=m: e.activation(qt[:, m, :], ps[:, m % 2, :], ACT.Identity, bias=qb[:, m:m + 1]),
                        after=[f"q{m}", (f"S{TQ - 1}", -1)], done=f"qt{m}")
                    yield

                for q in range(TQ):
                    put("scalar", lambda e, b, q=q: e.activation(hb[:, q, :], ha[:, q, :], ACT.Copy), after=[f"h{q}", (f"out{q}", -1)], done=f"hb{q}")

                def weigh(q):
                    for m in range(KT):
                        put("tensor", lambda e, b, m=m: e.matmul(ps[:, 2 + m // 2, (m % 2) * 2 * C:(m % 2 + 1) * 2 * C], qt[:, m, q * P:(q + 1) * P], km[:, m, :],
                            start=True, stop=True), after=["qt3", "km", f"add{q - 1}" if q else ("add3", -1)], done=f"S{q}" if m == KT - 1 else None)
                    put("vector", lambda e, b: e.tensor_tensor(sc[:, q, :, :].rearrange("p (a h) c -> p a h c", a=2),
                        ps[:, 2:4, 0:4 * C].rearrange("p a (h c) -> p a h c", h=4),
                        neg[:].unsqueeze(1).unsqueeze(1).broadcast_to([P, 2, 4, C]), ALU.add), after=[f"S{q}", (f"pt{q}", -1)], done=f"add{q}")
                    put("vector", lambda e, b: e.tensor_reduce(mx[:, q, :], sc[:, q, :, :], AX_X, ALU.max), after=[f"add{q}"], done=f"mx{q}")
                    put("vector", lambda e, b: e.tensor_tensor(sc[:, q, :, :], sc[:, q, :, :], mx[:, q, :].unsqueeze(2).broadcast_to([P, H1, C]), ALU.subtract),
                        after=[f"mx{q}"], done=f"sub{q}")
                    put("scalar", lambda e, b: e.activation(sc[:, q, :, :], sc[:, q, :, :], ACT.Exp), after=[f"sub{q}"], done=f"e{q}")

                def normalise(q):
                    put("vector", lambda e, b: e.tensor_reduce(sm[:, q, :], sc[:, q, :, :], AX_X, ALU.add), after=[f"e{q}"], done=f"sm{q}")
                    put("vector", lambda e, b: e.reciprocal(rs[:, q, :], sm[:, q, :]), after=[f"sm{q}", (f"nm{q}", -1)], done=f"rs{q}")
                    put("gpsimd", lambda e, b: e.tensor_tensor(sc[:, q, :, :], sc[:, q, :, :], rs[:, q, :].unsqueeze(2).broadcast_to([P, H1, C]), ALU.mult),
                        after=[f"rs{q}"], done=f"nm{q}")

                def turn(q):
                    for h in range(H1):
                        put("tensor", lambda e, b, h=h: e.transpose(ps[0:C, 4 + h // 4, (h % 4) * P:(h % 4 + 1) * P], sc[:, q, h, :], eye[:]),
                            after=[f"nm{q}", f"pc{q - 1}" if q else ("pc3", -1)], done=f"pt{q}" if h == H1 - 1 else None)
                    put("scalar", lambda e, b: e.activation(pt[:, :, q * P:(q + 1) * P], ps[0:C, 4:6, :].rearrange("c a (h t) -> c (a h) t", h=4), ACT.Copy),
                        after=[f"pt{q}", ("pv3", -1)], done=f"pc{q}")

                for step in ((weigh, 0), (weigh, 1), (normalise, 0), (weigh, 2), (normalise, 1), (turn, 0), (weigh, 3), (normalise, 2), (turn, 1),
                             (normalise, 3), (turn, 2), (turn, 3)):
                    step[0](step[1])
                    yield

            def finish():
                put = lambda *p, **k: r.put("B", *p, **k)
                put("sync", lambda e, b: e.dma_start(v[:], scratch["v1"][row(b * C, C), :]), after=[("pv3", -1)], dma="v")
                for m in range(KT):
                    for j in range(2):
                        h = 2 * m + j
                        put("tensor", lambda e, b, m=m, j=j, h=h: e.matmul(ps[j * HD1:(j + 1) * HD1, 6 + m % 2, :], v[:, h * HD1:(h + 1) * HD1], pt[:, h, :], start=True, stop=True),
                            after=["v", "pc3", f"cl{m - 2}" if m >= 2 else (f"out{m + 2}", -1)], done=f"pv{m}" if j else None)
                    put("scalar", lambda e, b, m=m: e.activation(cs[0][:, m, :], ps[:, 6 + m % 2, :], ACT.Copy), after=[f"pv{m}", ("O3", -1)], done=f"ch{m}")
                    put("vector", lambda e, b, m=m: e.tensor_tensor(cs[1][:, m, :], ps[:, 6 + m % 2, :], cs[0][:, m, :].bitcast(F32), ALU.subtract),
                        after=[f"ch{m}"], done=f"cl{m}")
                    yield
                for q in range(TQ):
                    for k in range(KT):
                        put("tensor", lambda e, b, q=q, k=k: mm3(e, ps[:, 6 + q % 2, :], [c_[:, k, q * P:(q + 1) * P] for c_ in cs],
                            [w_[:, k, :] for w_ in wo], k == 0, k == KT - 1),
                            after=["cl3", f"out{q - 2}" if q >= 2 else "cl3"], done=f"O{q}" if k == KT - 1 else None)
                    put("vector", lambda e, b, q=q: e.tensor_tensor(ot[:, q, :], ps[:, 6 + q % 2, :], hb[:, q, :], ALU.add),
                        after=[f"O{q}", f"hb{q}", (f"store{q}", -1)], done=f"out{q}")
                    put("sync", lambda e, b, q=q: e.dma_start(out[row(b), q * P:(q + 1) * P, :].rearrange("b p d -> (b p) d"), ot[:, q, :]), after=[f"out{q}"], dma=f"store{q}")
                    yield

            interleave("B B B A A B A A B A A B A A B A B AAAAAAAAAAAA A", A=attend(), B=finish())
            r.emit()


def build(nc, a, out):
    rows = a["x"].shape[0]
    tokens = a["ctxT"].shape[1]
    shapes = {"k0h": [KT, P, tokens], "k0l": [KT, P, tokens], "k1": [KT, P, tokens], "v0": [tokens, D], "v1": [tokens, D],
              "y": [rows, P, TQ, D], "o": [rows, P, TQ, D], "rinv": [rows, P, TQ], "ssq": [rows, P, TQ]}
    scratch = {n: nc.dram_tensor(f"scratch_{n}", s, F32).ap() for n, s in shapes.items()}
    keys_values(nc, a, scratch)
    layer0(nc, a, scratch, rows)
    mamba(nc, a, scratch, rows)
    layer1(nc, a, scratch, out, rows)


def kernel(**inputs):
    import numpy as np
    from concourse import bacc
    from concourse.bass_utils import run_bass_kernel_spmd

    get = lambda n: np.asarray(inputs[n])
    l0, l1 = (lambda n: get(f"L0_xattn_{n}")), (lambda n: get(f"L1_xattn_{n}"))
    ctx = get("ctx_1024")
    arrays = {
        "x": get("x"), "xT": get("x").transpose(0, 2, 1), "ctxT": ctx.transpose(2, 0, 1).reshape(ctx.shape[2], -1),
        "maskT": get("mask_Bx1xSxS2_fk0")[:, 0].transpose(0, 2, 1), "kmask": get("mask_1xS2_bf0"),
        "Wq0": l0("Wq"), "bq0": l0("bq"), "Wk0": l0("Wk"), "bk0": l0("bk"), "Wv0": l0("Wv"), "bv0": l0("bv"),
        "Wo0": l0("Wo"), "bo0": l0("bo"), "gamma0": l0("gamma"), "beta0": l0("beta"),
        "norm1": l1("m_norm_w"), "Win": l1("in_proj_w"), "cw": l1("conv_w"), "cb": l1("conv_b"), "dtb": l1("dt_bias"),
        "alog": l1("A_log"), "skip": l1("D_skip"), "gnorm1": l1("gnorm_w"), "Wout": l1("out_proj_w"),
        "lnw": l1("ca_ln_w"), "lnb": l1("ca_ln_b"), "Wq1": l1("Wq"), "Wk1": l1("Wk"), "Wv1": l1("Wv"), "Wo1": l1("Wo"),
        "eye": np.eye(P, dtype=np.float32),
    }
    nc = bacc.Bacc("TRN2", target_bir_lowering=False, num_devices=1)
    maps, args = {}, {}
    for name, array in arrays.items():
        maps[f"in_{name}"] = np.ascontiguousarray(array)
        args[name] = nc.dram_tensor(f"in_{name}", array.shape, mybir.dt.from_np(array.dtype), kind="ExternalInput").ap()
    out = nc.dram_tensor("out", get("x").shape, F32, kind="ExternalOutput").ap()
    build(nc, args, out)
    return run_bass_kernel_spmd(nc, [maps], core_ids=[0]).results[0]["out"]
```

```python
from contextlib import ExitStack

import concourse.bass as bass
from concourse import mybir

F32 = mybir.dt.float32
F32R = mybir.dt.float32r
U8 = mybir.dt.uint8
ALU = mybir.AluOpType
ACT = mybir.ActivationFunctionType
AX_X = mybir.AxisListType.X

P = 128
D = 512
KT = D // P
S = 512
TQ = S // P
C = 77
H0, HD0 = 16, 32
H1, HD1 = 8, 64
HPT = P // HD0
DI = 1024
MI = DI // P
HM = 16
NS = 128
CONVD = DI + 2 * NS
TAPS = 4
EPS = 1e-5
CLAMP = 50.0
MASKED = -1.0e9
KV_TILE = 112

ENGINES = ("tensor", "scalar", "vector", "gpsimd", "sync")


class Region:

    def __init__(self, nc, ctx, name, rows, lags, tables=None):
        self.tables = tables
        self.spare = ctx.enter_context(nc.sbuf_tensor(f"{name}_spare", [1, TQ], F32))
        self.nc, self.ctx, self.name, self.rows, self.lags = nc, ctx, name, rows, lags
        self.queue = {e: [] for e in ENGINES}
        self.count = {}
        self.step = {}
        self.named = {}
        self.placed = {}
        self.places = 0

    def put(self, stage, engine, build, after=(), done=None, dma=None, apart=None, first=None, unit=1):
        raised = None
        self.places += 1
        if done or dma:
            raised = dma or f"{stage}_{engine}"
            self.count[raised] = self.count.get(raised, 0) + 1
            self.step[raised] = 16 if dma else 1
            for n in [done] if isinstance(done, str) else (done or []):
                assert n not in self.named, n
                self.named[n] = (raised, self.count[raised])
                self.placed[n] = (stage, self.places)
            if dma:
                self.placed[dma] = (stage, self.places)
                self.named[dma] = (raised, self.count[raised])
        self.queue[engine].append((stage, build, list(after), raised, apart, first, unit, self.places))

    def emit(self):
        nc, last = self.nc, max(self.lags.values())
        for q in self.queue.values():
            for stage, _, after, _, _, _, _, at in q:
                for a in after:
                    n, shift = (a, 0) if isinstance(a, str) else a
                    if self.placed[n][0] == "W":
                        assert shift == 0 and (self.lags[stage] > 0 or self.placed[n][1] < at), (n, stage)
                        continue
                    turns = self.lags[self.placed[n][0]] + shift - self.lags[stage]
                    assert turns < 0 or (turns == 0 and self.placed[n][1] < at), (n, shift, stage)
        sem = {s: self.ctx.enter_context(nc.semaphore(f"{self.name}_{s}")) for s in self.count}
        per = {s: self.count[s] * self.step[s] for s in self.count}
        once = {self.named[n][0] for n, (stage, _) in self.placed.items() if stage == "W"}
        block = self.ctx.enter_context(nc.Block())

        def turn(eng, q, t, stages):
            waited, base = {}, {}
            for stage, build, after, raised, apart, first, unit, _ in q:
                if stage not in stages:
                    continue
                b = t - self.lags[stage]
                if unit != 1:
                    b = b * unit
                    if not isinstance(t, int):
                        if (stage, unit) not in base:
                            base[stage, unit] = eng.snap(b)
                        b = base[stage, unit]
                if first:
                    first(eng)
                for a in after:
                    s = self.named[a if isinstance(a, str) else a[0]][0]
                    if s not in base and s not in once:
                        base[s] = t * per[s] if isinstance(t, int) else eng.snap(t * per[s])
                for a in after:
                    name, shift = (a, 0) if isinstance(a, str) else a
                    s, k = self.named[name]
                    if s in once:
                        if isinstance(t, int) and t == 0 and waited.get(s, 0) < k:
                            waited[s] = k
                            eng.wait_ge(sem[s], k * self.step[s])
                        continue
                    ahead = (1 + shift - self.lags[stage]) * per[s] + k * self.step[s]
                    if waited.get(s, -10 ** 9) >= ahead:
                        continue
                    waited[s] = ahead
                    eng.wait_ge(sem[s], base[s] + ahead)
                if apart is not None:
                    eng.memset(self.spare[:, apart:apart + 1], 0.0)
                ins = build(eng, b)
                if raised:
                    ins.then_inc(sem[raised], self.step[raised])

        def program(name):
            def body(eng):
                q = self.queue[name]
                if name == "scalar" and self.tables:
                    eng.preload_act_table_set(self.tables)
                if name == "sync":
                    for s in per:
                        if s not in once:
                            eng.sem_inc(sem[s], per[s])
                for t in range(last):
                    turn(eng, q, t, [s for s, lag in self.lags.items() if lag <= t and (s != "W" or t == 0)])
                    if t == 0:
                        need = {}
                        for stage, _, after, _, _, _, _, _ in q:
                            for n in after if stage != "W" else []:
                                if isinstance(n, str) and self.named[n][0] in once:
                                    s, k = self.named[n]
                                    need[s] = max(need.get(s, 0), k)
                        for s, k in need.items():
                            eng.wait_ge(sem[s], k * self.step[s])
                if self.rows > last:
                    if self.rows - last == 1:
                        turn(eng, q, last, [s for s in self.lags if s != "W" or last == 0])
                    elif q:
                        with eng.Fori(last, self.rows) as t:
                            turn(eng, q, t, [s for s in self.lags if s != "W"])
                for t in range(self.rows, self.rows + last):
                    turn(eng, q, t, [s for s, lag in self.lags.items() if t - lag < self.rows and s != "W"])
                if name == "sync":
                    for s in per:
                        if self.step[s] == 16:
                            eng.wait_ge(sem[s], (1 if s in once else self.rows + 1) * per[s])
            return body

        for name in ENGINES:
            if self.queue[name] or name == "sync":
                run_on = {"tensor": block.tensor, "scalar": block.scalar, "vector": block.vector,
                          "gpsimd": block.gpsimd, "sync": block.sync}[name]
                run_on(program(name))


def interleave(order, **steps):
    for c in order.replace(" ", ""):
        next(steps[c], None)
    for c, g in steps.items():
        rest = sum(1 for _ in g)
        assert rest == 0, (c, rest)


def mm3(eng, out, w, x, start=True, stop=True):
    eng.matmul(out, w[0], x[0], start=start, stop=False)
    eng.matmul(out, w[0], x[1], start=False, stop=False)
    return eng.matmul(out, w[1], x[0], start=False, stop=stop)


def row(b, n=1):
    return slice(b, b + n) if isinstance(b, int) else bass.ds(b, n)


def tiles(vector, width=P):
    return vector.rearrange("(m p) -> p m", p=width)


def spread(vector, parts=P):
    return vector.rearrange("(a n) -> a n", a=1).broadcast_to([parts, vector.shape[0]])


def root_guess(r, stage, v, y, after, tag):
    r.put(stage, "scalar", lambda e, b: e.activation(y, v, ACT.Ln), after=after, done=f"{tag}_ln")
    r.put(stage, "scalar", lambda e, b: e.activation(y, y, ACT.Exp, scale=-0.5), after=[f"{tag}_ln"], done=f"{tag}_0")


def root_refine(r, stage, v, y, t, tag):
    steps = (lambda e, b: e.tensor_tensor(t, y, y, ALU.mult),
             lambda e, b: e.tensor_tensor(t, t, v, ALU.mult),
             lambda e, b: e.tensor_scalar(t, t, -0.5, 1.5, ALU.mult, ALU.add),
             lambda e, b: e.tensor_tensor(y, y, t, ALU.mult))
    for n, op in enumerate(steps):
        r.put(stage, "vector", op, after=[f"{tag}_{n}"], done=f"{tag}_{n + 1}" if n < 3 else tag)


def keys_values(nc, a, scratch):
    with ExitStack() as ctx:
        def sb(name, shape, dt=F32):
            return ctx.enter_context(nc.sbuf_tensor(f"kv_{name}", shape, dt))
        rows = a["ctxT"].shape[1] // KV_TILE
        wk = [sb(f"wk{l}", [P, KT, D]) for l in range(2)]
        wv_raw = [sb(f"wv{l}", [P, KT, D]) for l in range(2)]
        wv = [[sb(f"wv{l}{h}", [P, KT, D], F32R) for h in "hl"] for l in range(2)]
        bk, bv = sb("bk", [P, KT]), sb("bv", [P, D])
        x_in, x_f = sb("x_in", [P, KT, KV_TILE]), sb("x_f", [P, KT, KV_TILE])
        x_s = [sb(f"x_{h}", [P, KT, KV_TILE], F32R) for h in "hl"]
        k0f = sb("k0f", [P, KT, KV_TILE])
        k0s = [sb(f"k0{h}", [P, KT, KV_TILE], F32R) for h in "hl"]
        k1s = sb("k1s", [P, KT, KV_TILE])
        v_s = [sb(f"v{l}", [KV_TILE, D]) for l in range(2)]
        ps = ctx.enter_context(nc.psum_tensor("kv_ps", [P, 8, 512], F32))

        with ExitStack() as c2:
            r = Region(nc, c2, "kv", rows, {"W": 0, "L": 0, "T": 1})
            w = lambda l, n: a[f"W{n}{l}"].rearrange("(k p) n -> p k n", p=P)
            load = lambda *p, **k: r.put("L", *p, **k)
            load("sync", lambda e, b: e.dma_start(x_in[:], a["ctxT"].rearrange("(k p) t -> p k t", p=P)[:, :, row(b, KV_TILE)]),
                after=[("xf", -1), ("xl", -1)], dma="x", unit=KV_TILE)
            split_weights(r, [(f"wv{l}", w(l, "v"), wv_raw[l], wv[l], 1.0) for l in range(2)])
            for l in range(2):
                r.put("W", "sync", lambda e, b, l=l: e.dma_start(wk[l][:], w(l, "k")), dma=f"wk{l}")
            r.put("W", "sync", lambda e, b: e.dma_start(bk[:], tiles(a["bk0"]), allow_slow_non_contiguous=True), dma="bk")
            r.put("W", "sync", lambda e, b: e.dma_start(bv[:], spread(a["bv0"])), dma="bv")
            put = lambda *p, **k: r.put("T", *p, **k)
            for l in range(2):
                for k in range(KT):
                    put("tensor", lambda e, b, l=l, k=k: mm3(e, ps[0:KV_TILE, l, :], [x_s[0][:, k, :], x_s[1][:, k, :]],
                        [wv[l][0][:, k, :], wv[l][1][:, k, :]], k == 0, k == KT - 1),
                        after=["xl", f"wv{l}_l{k}", (f"v{l}", -1)], done=f"V{l}" if k == KT - 1 else None)
            load("scalar", lambda e, b: e.activation(x_s[0][:], x_in[:], ACT.Copy), after=["x", ("V1", -1)], done="xh")
            load("vector", lambda e, b: e.tensor_tensor(x_s[1][:], x_in[:], x_s[0][:].bitcast(F32), ALU.subtract), after=["xh"], done="xl")
            put("vector", lambda e, b: e.tensor_tensor(v_s[0][:], ps[0:KV_TILE, 0, :], bv[0:KV_TILE, :], ALU.add), after=["V0", "bv", ("v0_out", -1)], done="v0")
            put("scalar", lambda e, b: e.activation(v_s[1][:], ps[0:KV_TILE, 1, :], ACT.Copy), after=["V1", ("v1_out", -1)], done="v1")
            for l in range(2):
                for m in range(KT):
                    for k in range(KT):
                        put("tensor", lambda e, b, l=l, m=m, k=k: e.matmul(ps[:, 2 + l, m * KV_TILE:(m + 1) * KV_TILE],
                            wk[l][:, k, m * P:(m + 1) * P], x_f[:, k, :], start=(k == 0), stop=(k == KT - 1)),
                            after=["xf", f"wk{l}", (("k0f", "k1")[l], -1)], done=f"K{l}" if (m, k) == (KT - 1, KT - 1) else None)
            put("vector", lambda e, b: e.tensor_tensor(k0f[:], ps[:, 2, 0:KT * KV_TILE].rearrange("p (m t) -> p m t", m=KT),
                bk[:].unsqueeze(2).broadcast_to([P, KT, KV_TILE]), ALU.add), after=["K0", "bk", ("k0l", -1)], done="k0f")
            put("scalar", lambda e, b: e.activation(k0s[0][:], k0f[:], ACT.Copy), after=["k0f", ("k0h_out", -1)], done="k0h")
            put("vector", lambda e, b: e.tensor_tensor(k0s[1][:], k0f[:], k0s[0][:].bitcast(F32), ALU.subtract), after=["k0h", ("k0l_out", -1)], done="k0l")
            load("vector", lambda e, b: e.tensor_copy(x_f[:], x_in[:]), after=["x", ("K1", -1)], done="xf")
            put("scalar", lambda e, b: e.activation(k1s[:], ps[:, 3, 0:KT * KV_TILE].rearrange("p (m t) -> p m t", m=KT), ACT.Copy), after=["K1", ("k1_out", -1)], done="k1")
            for n, t in (("k0h", k0s[0][:].bitcast(F32)), ("k0l", k0s[1][:].bitcast(F32)), ("k1", k1s[:])):
                put("sync", lambda e, b, n=n, t=t: e.dma_start(scratch[n].rearrange("m p t -> p m t")[:, :, row(b, KV_TILE)], t),
                    after=[n], dma=f"{n}_out", unit=KV_TILE)
            for l in range(2):
                put("sync", lambda e, b, l=l: e.dma_start(scratch[f"v{l}"][row(b, KV_TILE), :], v_s[l][:]), after=[f"v{l}"], dma=f"v{l}_out", unit=KV_TILE)
            r.emit()


def layer0(nc, a, scratch, rows):
    with ExitStack() as ctx:
        def sb(name, shape, dt=F32):
            return ctx.enter_context(nc.sbuf_tensor(f"l0_{name}", shape, dt))
        wq, wo = ([sb(f"{n}{h}", [P, KT, D], F32R) for h in "hl"] for n in ("wq", "wo"))
        bq, bo, gamma, beta = sb("bq", [P, KT]), sb("bo", [P, D]), sb("gamma", [P, D]), sb("beta", [P, D])
        ones = sb("ones", [C, HD0])
        x_in = sb("x_in", [P, KT, S])
        xs = [sb(f"x{h}", [P, KT, S], F32R) for h in "hl"]
        qs = [sb(f"q{h}", [P, KT, S], F32R) for h in "hl"]
        kp = [sb(f"k{h}", [P, H0, C], F32R) for h in "hl"]
        v = sb("v", [C, D])
        m_in, mf = sb("m_in", [C, S]), sb("mf", [C, S])
        sc = sb("sc", [C, 4, S])
        pt = sb("pt", [C, H0, S])
        lg, rd, nr = sb("lg", [P, 2, S]), sb("rd", [P, 2, S]), sb("nr", [P, 2, S])
        cn = sb("cn", [P, 2, S])
        cs = [sb(f"c{h}", [P, KT, S], F32R) for h in "hl"]
        xb = sb("xb", [P, TQ, D])
        res = sb("res", [P, TQ, D])
        y = sb("y", [P, TQ, D])
        sq = sb("sq", [P, D])
        st, mv = sb("st", [P, TQ, 6]), sb("mv", [P, TQ, 2])
        var, rstd, tmp = sb("var", [P, TQ]), sb("rstd", [P, TQ]), sb("tmp", [P, TQ])
        ms, rms, rinv, tmp2 = sb("ms", [P, TQ]), sb("rms", [P, TQ]), sb("rinv", [P, TQ]), sb("tmp2", [P, TQ])
        ps = ctx.enter_context(nc.psum_tensor("l0_ps", [P, 8, 512], F32))

        with ExitStack() as c2:
            r = Region(nc, c2, "l0", rows, {"W": 0, "X": 0, "K": 0, "V": 1, "A": 1, "B": 2, "C": 3, "R": 4}, "natural_log_exp_and_others")
            put = lambda *p, **k: r.put("W", *p, **k)
            split_weights(r, [("wq", a["Wq0"].rearrange("(k p) n -> p k n", p=P), res, wq, HD0 ** -0.5),
                              ("wo", a["Wo0"].rearrange("(k p) n -> p k n", p=P), y, wo, 1.0)])
            put("sync", lambda e, b: e.dma_start(bq[:], tiles(a["bq0"]), allow_slow_non_contiguous=True), dma="bq")
            put("scalar", lambda e, b: e.dma_start(bo[:], spread(a["bo0"])), dma="bo")
            put("scalar", lambda e, b: e.dma_start(gamma[:], spread(a["gamma0"])), dma="gamma")
            put("scalar", lambda e, b: e.dma_start(beta[:], spread(a["beta0"])), dma="beta")
            put("gpsimd", lambda e, b: e.memset(ones[:], 1.0), done="ones")
            put("gpsimd", lambda e, b: e.memset(kp[0][:].bitcast(F32), 0.0), done="kz0")
            put("gpsimd", lambda e, b: e.memset(kp[1][:].bitcast(F32), 0.0), done="kz1")
            put("vector", lambda e, b: e.tensor_scalar(bq[:], bq[:], HD0 ** -0.5, None, ALU.mult), after=["bq"], done="bqs")

            def load_split():
                put = lambda *p, **k: r.put("X", *p, **k)
                put("sync", lambda e, b: e.dma_start(x_in[:], a["xT"].rearrange("b (k p) t -> b p k t", p=P)[row(b)].rearrange("b p k t -> (b p) k t")),
                    after=[("xl3", -1)], dma="x_in")
                for k in range(KT):
                    put("scalar" if k % 2 else "vector",
                        (lambda e, b, k=k: e.activation(xs[0][:, k, :], x_in[:, k, :], ACT.Copy)) if k % 2 else
                        (lambda e, b, k=k: e.tensor_copy(xs[0][:, k, :], x_in[:, k, :])),
                        after=["x_in", ("q3", -1)], done=f"xh{k}")
                    put("gpsimd", lambda e, b, k=k: e.tensor_tensor(xs[1][:, k, :], x_in[:, k, :], xs[0][:, k, :].bitcast(F32), ALU.subtract),
                        after=[f"xh{k}", ("q3", -1)], done=f"xl{k}")
                yield

            def load_keys():
                put = lambda *p, **k: r.put("K", *p, **k)
                for n, s in enumerate(("k0h", "k0l")):
                    for j in range(HPT):
                        src = scratch[s].rearrange("m p t -> p m t")[j * HD0:(j + 1) * HD0]
                        dst = kp[n][j * HD0:(j + 1) * HD0, :, :].bitcast(F32).rearrange("p (m j) t -> p m j t", j=HPT)[:, :, j, :]
                        put("sync", lambda e, b, src=src, dst=dst: e.dma_start(dst, src[:, :, row(b, C)]),
                            after=[f"kz{n}", (f"S{H0 - 1}", -1)], dma="kp", unit=C)
                put("sync", lambda e, b: e.dma_start(m_in[:], a["maskT"][row(b)].rearrange("b c t -> (b c) t")), after=[("mf", -1)], dma="m_in")
                yield

            def load_values():
                put = lambda *p, **k: r.put("V", *p, **k)
                put("sync", lambda e, b: e.dma_start(v[:], scratch["v0"][row(b, C), :]), after=[("pv3", -1)], dma="v", unit=C)
                yield
                put("sync", lambda e, b: e.dma_start(xb[:], a["x"].rearrange("b (q p) d -> b p q d", p=P)[row(b)].rearrange("b p q d -> (b p) q d")),
                    after=[("r3", -1)], dma="x_tok")
                yield

            def scores():
                put = lambda *p, **k: r.put("A", *p, **k)
                put("vector", lambda e, b: e.tensor_scalar(mf[:], m_in[:], 0.5, 0.5, ALU.mult, ALU.add),
                    after=["m_in", (f"mul{H0 - 1}", -1)], done="mf")
                for m in range(KT):
                    for k in range(KT):
                        put("tensor", lambda e, b, m=m, k=k: mm3(e, ps[:, m, :], [w_[:, k, m * P:(m + 1) * P] for w_ in wq],
                            [x_[:, k, :] for x_ in xs], k == 0, k == KT - 1),
                            after=[f"xl{k}", f"xh{k}", f"wq_l{k}", (f"mul{12 + m}", -1)], done=f"q{m}" if k == KT - 1 else None)
                    yield
                    put("scalar", lambda e, b, m=m: e.activation(qs[0][:, m, :], ps[:, m, :], ACT.Identity, bias=bq[:, m:m + 1]),
                        after=[f"q{m}", "bqs", (f"S{4 * m + 3}", -1)], done=f"qh{m}")
                    put("vector", lambda e, b, m=m: e.scalar_tensor_tensor(out=qs[1][:, m, :], in0=ps[:, m, :], scalar=bq[:, m:m + 1],
                        in1=qs[0][:, m, :].bitcast(F32), op0=ALU.add, op1=ALU.subtract), after=[f"qh{m}"], done=f"ql{m}")
                    yield
                for h in range(H0):
                    m = h // HPT
                    free = f"ql{h}" if h < 4 else f"mul{h - 4}"
                    keys = ["kp"] if h == 0 else []
                    put("tensor", lambda e, b, h=h, m=m: mm3(e, ps[0:C, h % 4, :], [k_[:, h, :] for k_ in kp], [q_[:, m, :] for q_ in qs]),
                        after=[f"ql{m}", free] + keys, done=f"S{h}")
                    yield
                    put("vector", lambda e, b, h=h: e.tensor_tensor(sc[:, h % 4, :], ps[0:C, h % 4, :], mf[:], ALU.mult),
                        after=[f"S{h}", "mf", f"exp{h - 4}" if h >= 4 else (f"exp{12 + h}", -1)], done=f"mul{h}")
                    put("vector", lambda e, b, h=h: e.tensor_scalar(sc[:, h % 4, :], sc[:, h % 4, :], CLAMP, -CLAMP, ALU.min, ALU.max),
                        after=[f"mul{h}"], done=f"clip{h}")
                    put("scalar", lambda e, b, h=h: e.activation(pt[:, h, :], sc[:, h % 4, :], ACT.Exp),
                        after=[f"clip{h}", (f"pv{m}", -1)], done=f"exp{h}")
                    yield

            def values_out():
                put = lambda *p, **k: r.put("B", *p, **k)

                def banks(m):
                    return 4 + 2 * (m % 2)

                def weigh_values(m):
                    free = [f"cn{m - 2}"] if m >= 2 else [("r2", -1), ("r3", -1), (f"cn{m + 2}", -1)]
                    for j in range(HPT):
                        h = HPT * m + j
                        put("tensor", lambda e, b, j=j, h=h: e.matmul(ps[j * HD0:(j + 1) * HD0, banks(m), :], v[:, h * HD0:(h + 1) * HD0], pt[:, h, :], start=True, stop=True),
                            after=["v", f"exp{h}"] + free)
                    for j in range(HPT):
                        h = HPT * m + j
                        put("tensor", lambda e, b, j=j, h=h: e.matmul(ps[j * HD0:(j + 1) * HD0, banks(m) + 1, :], ones[:], pt[:, h, :], start=True, stop=True),
                            after=["ones"], done=f"pv{m}" if j == HPT - 1 else None)
                    yield
                    put("scalar", lambda e, b: e.activation(lg[:, m % 2, :], ps[:, banks(m) + 1, :], ACT.Ln), after=[f"pv{m}"], done=f"lg{m}")
                    put("scalar", lambda e, b: e.activation(rd[:, m % 2, :], lg[:, m % 2, :], ACT.Exp, scale=-1.0),
                        after=[f"lg{m}", f"nr{m - 2}" if m >= 2 else (f"nr{m + 2}", -1)], done=f"rd{m}")

                def divide(m):
                    put("vector", lambda e, b: e.tensor_tensor(nr[:, m % 2, :], ps[:, banks(m) + 1, :], rd[:, m % 2, :], ALU.mult), after=[f"rd{m}", f"cn{m - 2}" if m >= 2 else (f"cn{m + 2}", -1)], done=f"sg{m}")
                    put("vector", lambda e, b: e.scalar_tensor_tensor(out=nr[:, m % 2, :], in0=nr[:, m % 2, :], scalar=2.0, in1=rd[:, m % 2, :], op0=ALU.subtract, op1=ALU.mult),
                        after=[f"sg{m}"], done=f"nr{m}")
                    put("vector", lambda e, b: e.scalar_tensor_tensor(out=cn[:, m % 2, :], in0=ps[:, banks(m), :], scalar=-1.0, in1=nr[:, m % 2, :], op0=ALU.mult, op1=ALU.mult),
                        after=[f"nr{m}", f"cl{m - 2}" if m >= 2 else (f"cl{m + 2}", -1)], done=f"cn{m}")
                    put("scalar", lambda e, b: e.activation(cs[0][:, m, :], cn[:, m % 2, :], ACT.Copy), after=[f"cn{m}", ("o3", -1)], done=f"ch{m}")
                    put("gpsimd", lambda e, b: e.tensor_tensor(cs[1][:, m, :], cn[:, m % 2, :], cs[0][:, m, :].bitcast(F32), ALU.subtract),
                        after=[f"ch{m}"], done=f"cl{m}")
                    put("gpsimd", lambda e, b: e.tensor_tensor(xb[:, m, :], xb[:, m, :], bo[:], ALU.add), after=["x_tok", "bo"], done=f"xb{m}")

                for step in ((weigh_values, 0), (weigh_values, 1), (divide, 0), (weigh_values, 2), (divide, 1), (weigh_values, 3), (divide, 2), (divide, 3)):
                    yield from step[0](step[1]) or ()
                    yield
                for q in range(TQ):
                    for k in range(KT):
                        put("tensor", lambda e, b, q=q, k=k: mm3(e, ps[:, 6 + q % 2, :], [c_[:, k, q * P:(q + 1) * P] for c_ in cs],
                            [w_[:, k, :] for w_ in wo], k == 0, k == KT - 1),
                            after=[f"ch{k}", f"cl{k}", f"wo_l{k}", f"r{q - 2}" if q >= 2 else "cn3"], done=f"o{q}" if k == KT - 1 else None)
                    yield
                    put("vector", lambda e, b, q=q: e.tensor_tensor(res[:, q, :], ps[:, 6 + q % 2, :], xb[:, q, :], ALU.add),
                        after=[f"o{q}", f"xb{q}", "wq_l3", (f"n{q}", -1)], done=f"r{q}")
                    put("vector", lambda e, b, q=q: e.bn_stats(st[:, q, :], res[:, q, :]), after=[f"r{q}"], done=f"st{q}")
                    put("vector", lambda e, b, q=q: e.bn_aggr(mv[:, q, :], st[:, q, :]), after=[f"st{q}"], done=f"mv{q}", apart=q)
                    yield
                put("vector", lambda e, b: e.tensor_scalar(var[:], mv[:, :, 1], EPS, None, ALU.add), after=["mv3"], done="var")
                root_guess(r, "B", var[:], rstd[:], ["var"], "rstd")
                yield

            def normalise():
                put = lambda *p, **k: r.put("C", *p, **k)
                root_refine(r, "C", var[:], rstd[:], tmp[:], "rstd")
                for q in range(TQ):
                    put("vector", lambda e, b, q=q: e.tensor_scalar(y[:, q, :], res[:, q, :], mv[:, q, 0:1], rstd[:, q:q + 1], ALU.subtract, ALU.mult),
                        after=["rstd", "wo_l3", ("y_out", -1), (f"sq{q}", -1)], done=f"n{q}")
                    put("gpsimd", lambda e, b, q=q: e.tensor_tensor(y[:, q, :], y[:, q, :], gamma[:], ALU.mult), after=[f"n{q}", "gamma", "beta"], done=f"g{q}")
                    put("gpsimd", lambda e, b, q=q: e.tensor_tensor(y[:, q, :], y[:, q, :], beta[:], ALU.add), after=[f"g{q}"], done=f"y{q}")
                put("sync", lambda e, b: e.dma_start(scratch["y"][row(b)].rearrange("b p q d -> (b p) q d"), y[:]), after=["y3"], dma="y_out")
                yield
                for q in range(TQ):
                    put("scalar", lambda e, b, q=q: e.activation(sq[:], y[:, q, :], ACT.Square, scale=D ** -0.5, accum_out=ms[:, q:q + 1]),
                        after=[f"y{q}", f"sq{q - 1}" if q else ("sq3", -1)] + ([("rms", -1)] if q == 0 else []), done=f"sq{q}")
                yield
                put("vector", lambda e, b: e.tensor_scalar(rms[:], ms[:], EPS, None, ALU.add), after=["sq3", ("rinv", -1)], done="rms")
                root_guess(r, "C", rms[:], rinv[:], ["rms", ("rinv_out", -1)], "rinv")
                yield

            def store_rms():
                root_refine(r, "R", rms[:], rinv[:], tmp2[:], "rinv")
                r.put("R", "sync", lambda e, b: e.dma_start(scratch["rinv"][row(b)].rearrange("b p q -> (b p) q"), rinv[:]), after=["rinv"], dma="rinv_out")
                yield

            interleave("BBCBBBAAAABBBAARAAABBBABAAAXVAAAAABBAAAAAABBAAAACBBBBAVAAAABCAAAAAAAK",
                       A=scores(), B=values_out(), C=normalise(), X=load_split(), K=load_keys(), V=load_values(), R=store_rms())
            r.emit()


def split_weights(w, items):
    for name, src, raw, _, _ in items:
        for k in range(src.shape[1]):
            w.put("W", "sync", lambda e, b, k=k, src=src, raw=raw: e.dma_start(raw[:, k, 0:src.shape[2]], src[:, k, :]), dma=f"{name}{k}")
    for name, src, raw, (hi, lo), scale in items:
        n = src.shape[2]
        for k in range(src.shape[1]):
            by = scale if isinstance(scale, float) else scale[:, k:k + 1]
            w.put("W", "scalar", lambda e, b, k=k, raw=raw, n=n, hi=hi, by=by: e.activation(hi[:, k, 0:n], raw[:, k, 0:n], ACT.Copy, scale=by),
                  after=[f"{name}{k}"] + ([] if isinstance(scale, float) else ["columns"]), done=f"{name}_h{k}")
            w.put("W", "vector", lambda e, b, k=k, raw=raw, n=n, hi=hi, lo=lo, by=by: e.scalar_tensor_tensor(
                out=lo[:, k, 0:n], in0=raw[:, k, 0:n], scalar=by, in1=hi[:, k, 0:n].bitcast(F32), op0=ALU.mult, op1=ALU.subtract),
                after=[f"{name}_h{k}", f"{name}{k}"], done=f"{name}_l{k}")


def mamba(nc, a, scratch, rows):
    XC, BC, CC, DC = DI, 2 * DI, 2 * DI + NS, 2 * DI + 2 * NS
    NCONV = CONVD // P
    with ExitStack() as ctx:
        def sb(name, shape, dt=F32):
            return ctx.enter_context(nc.sbuf_tensor(f"mb_{name}", shape, dt))
        wi = [sb(f"wi{h}", [P, KT, DC + P], F32R) for h in "hl"]
        wo, gw = sb("wo", [P, MI, D]), sb("gw", [P, MI])
        cw, cb, skip = sb("cw", [P, NCONV, TAPS]), sb("cb", [P, NCONV]), sb("skip", [P, MI])
        dtb, am = sb("dtb", [P, 1]), sb("am", [P, 1])
        eyes = sb("eyes", [P, TQ, P])
        eye = eyes[:, 0, :]
        ones = sb("ones", [P, 1])
        sel = sb("sel", [P, HM], F32R)
        selp = sb("selp", [P, MI, P], F32R)
        d1 = sb("d1", [P, S])
        ps = ctx.enter_context(nc.psum_tensor("mb_ps", [P, 8, 512], F32))

        with ExitStack() as c2:
            raw = c2.enter_context(nc.sbuf_tensor("mb_raw", [P, KT, DC + HM], F32))
            nw = c2.enter_context(nc.sbuf_tensor("mb_nw", [P, KT], F32))
            sel_f = c2.enter_context(nc.sbuf_tensor("mb_self", [P, HM], F32))
            w = Region(nc, c2, "mbw", 1, {"W": 0})
            put = lambda *p, **k: w.put("W", *p, **k)
            put("vector", lambda e, b: e.memset(dtb[:], 0.0), done="z0")
            put("vector", lambda e, b: e.memset(am[:], 0.0), done="z1")
            put("vector", lambda e, b: e.memset(sel_f[:], 0.0), done="z2")
            put("vector", lambda e, b: e.memset(ones[:], 1.0))
            put("vector", lambda e, b: e.memset(d1[:], 0.0))
            put("scalar", lambda e, b: e.dma_start(nw[:], tiles(a["norm1"]), allow_slow_non_contiguous=True), dma="columns")
            put("scalar", lambda e, b: e.dma_start(gw[:], tiles(a["gnorm1"]), allow_slow_non_contiguous=True), dma="gw")
            for n in range(2):
                for unused in (slice(DC + HM, DC + 32), slice(DC + 32 + HM, DC + P)):
                    put("vector", lambda e, b, n=n, unused=unused: e.memset(wi[n][:, :, unused].bitcast(F32), 0.0))
            split_weights(w, [("wi", a["Win"].rearrange("(k p) n -> p k n", p=P), raw, wi, nw)])
            for k in range(KT):
                again = slice(DC + 32, DC + 32 + HM)
                put("scalar", lambda e, b, k=k: e.activation(wi[0][:, k, again], raw[:, k, DC:DC + HM], ACT.Copy, scale=nw[:, k:k + 1]),
                    after=[f"wi{k}", "columns"], done=f"dh{k}")
                put("vector", lambda e, b, k=k: e.scalar_tensor_tensor(out=wi[1][:, k, again], in0=raw[:, k, DC:DC + HM], scalar=nw[:, k:k + 1],
                    in1=wi[0][:, k, again].bitcast(F32), op0=ALU.mult, op1=ALU.subtract), after=[f"dh{k}"], done=f"dl{k}")
            put("sync", lambda e, b: e.dma_start(cw[:], a["cw"].rearrange("(j p) k -> p j k", p=P)), dma="cw")
            put("scalar", lambda e, b: e.dma_start(cb[:], tiles(a["cb"]), allow_slow_non_contiguous=True), dma="cb")
            for c in range(TQ):
                put("sync", lambda e, b, c=c: e.dma_start(eyes[:, c, :], a["eye"]), dma="eyes")
            for j in range(2):
                put("scalar", lambda e, b, j=j: e.dma_start(skip[j * 64:(j + 1) * 64, :], a["skip"].rearrange("(m j) -> j m", j=2)[j:j + 1, :].broadcast_to([64, MI]),
                    allow_slow_non_contiguous=True), dma="skip")
            for n, at in enumerate((0, 32)):
                put("sync", lambda e, b, at=at: e.dma_start(dtb[at:at + HM, :], a["dtb"].rearrange("(n a) -> n a", a=1)), after=["z0"], dma="dtb")
                put("sync", lambda e, b, at=at: e.dma_start(am[at:at + HM, :], a["alog"].rearrange("(n a) -> n a", a=1)), after=["z1"], dma="am")
                put("sync", lambda e, b, at=at: e.dma_start(sel_f[at:at + HM, :], a["eye"][0:HM, 0:HM]), after=["z2"], dma="sel")
            put("scalar", lambda e, b: e.activation(sel[:], sel_f[:], ACT.Copy), after=["sel"])
            put("scalar", lambda e, b: e.activation(selp[:].rearrange("p m (j d) -> p (m j) d", j=2), sel_f[:].unsqueeze(2).broadcast_to([P, HM, 64]), ACT.Copy),
                after=["sel"])
            for n, at in enumerate((0, 32)):
                put("scalar", lambda e, b, at=at: e.activation(am[at:at + HM, :], am[at:at + HM, :], ACT.Exp), after=["am"], done=f"ae{n}")
                put("vector", lambda e, b, at=at: e.tensor_scalar(am[at:at + HM, :], am[at:at + HM, :], -1.0, None, ALU.mult), after=[f"ae{n}"])
            w.emit()

        y = sb("y", [P, 2, D])
        ri = sb("ri", [P, TQ])
        yt = [sb(f"y{h}", [P, KT, S], F32R) for h in "hl"]
        cv, xs, sz = sb("cv", [P, 2, S]), sb("xs", [P, 3, S]), sb("sz", [P, 3, S])
        lm, gm = sb("lm", [P, 2, S]), sb("gm", [P, 2, 2, S])
        xp = sb("xp", [P, 2, TQ, P])
        xw = sb("xw", [P, 2, TQ - 1, P])
        pb, hs, yw = sb("pb", [P, S]), sb("hs", [P, TQ - 1, P]), sb("yw", [P, S])
        u, sq, ssq = sb("u", [P, MI, S]), sb("sq", [P, S]), sb("ssq", [P, S])
        bt, ct, bk, g = sb("bt", [P, S]), sb("ct", [P, S]), sb("bk", [P, TQ, P]), sb("g", [P, S])
        v, ex, ul = sb("v", [P, S]), sb("ex", [P, S]), sb("ul", [P, S])
        dec2, pre2 = sb("dec2", [P, S], F32R), sb("pre2", [P, S], F32R)
        dtT, dg, dl = sb("dtT", [P, TQ, HM]), sb("dg", [HM, TQ, HM]), sb("dl", [P, TQ, HM])
        o, so = sb("o", [P, 2, D]), sb("so", [P, TQ])
        starts, ends = slice(0, S, P), slice(P - 1, S, P)

        with ExitStack() as c2:
            r = Region(nc, c2, "mb", rows, {"W": 0, "A": 0, "F": 0, "P": 1, "S": 1, "O": 1})

            def project(put, tag, bank, column, after):
                for k in range(KT):
                    put("tensor", lambda e, b, k=k: mm3(e, ps[:, bank, :], [w_[:, k, column:column + P] for w_ in wi],
                        [y_[:, k, :] for y_ in yt], k == 0, k == KT - 1), after=after, done=tag if k == KT - 1 else None)

            def convolve(put, tag, bank, j, ring, free):
                last = TAPS - 1
                put("scalar", lambda e, b: e.activation(cv[:, ring, :], ps[:, bank, :], ACT.Identity, bias=cb[:, j:j + 1], scale=cw[:, j, last:last + 1]),
                    after=[tag, free], done=f"{tag}_t{last}")
                for k in reversed(range(last)):
                    n = last - k
                    put("vector", lambda e, b, k=k, n=n: e.scalar_tensor_tensor(out=cv[:, ring, n:S], in0=ps[:, bank, 0:S - n], scalar=cw[:, j, k:k + 1],
                        in1=cv[:, ring, n:S], op0=ALU.mult, op1=ALU.add), after=[f"{tag}_t{k + 1}"], done=f"{tag}_t{k}")

            def prepare():
                put = lambda *p, **k: r.put("A", *p, **k)

                def load(q):
                    put("sync", lambda e, b: e.dma_start(y[:, q % 2, :], scratch["y"][row(b), :, q, :].rearrange("b p d -> (b p) d")),
                        after=[f"yt{q - 2}" if q >= 2 else (f"yt{q + 2}", -1)], dma=f"y{q}")

                def scale(q):
                    put("vector", lambda e, b: e.tensor_scalar(y[:, q % 2, :], y[:, q % 2, :], ri[:, q:q + 1], None, ALU.mult), after=["ri", f"y{q}"], done=f"ys{q}")

                put("sync", lambda e, b: e.dma_start(ri[:], scratch["rinv"][row(b)].rearrange("b p q -> (b p) q")), after=[("ys3", -1)], dma="ri")
                load(0)
                load(1)
                yield
                scale(0)
                scale(1)
                yield
                for q in range(TQ):
                    if q == 2:
                        scale(2)
                        scale(3)
                        yield
                    for k in range(KT):
                        put("tensor", lambda e, b, q=q, k=k: e.transpose(ps[:, q % 2, k * P:(k + 1) * P], y[:, q % 2, k * P:(k + 1) * P], eye),
                            after=[f"ys{q}"] + ([f"yl{q - 2}"] if q >= 2 else [("sz7", -1), ("x7_t0", -1)]),
                            done=f"yt{q}" if k == KT - 1 else None)
                    cols = slice(q * P, (q + 1) * P)
                    src = ps[:, q % 2, :].rearrange("p (k t) -> p k t", k=KT)
                    put("scalar", lambda e, b, cols=cols, src=src: e.activation(yt[0][:, :, cols], src, ACT.Copy), after=[f"yt{q}", ("z7", -1)], done=f"yh{q}")
                    put("vector", lambda e, b, cols=cols, src=src: e.tensor_tensor(yt[1][:, :, cols], src, yt[0][:, :, cols].bitcast(F32), ALU.subtract),
                        after=[f"yh{q}"], done=f"yl{q}")
                    if q < 2:
                        load(q + 2)
                    yield
                project(put, "dt", 2, DC, ["yl3", ("xp7", -1), ("dl", -1)])
                yield
                put("vector", lambda e, b: e.tensor_scalar(v[:], ps[:, 2, :], dtb[:, 0:1], None, ALU.add), after=["dt", ("dlm", -1)], done="v")
                put("vector", lambda e, b: e.scalar_tensor_tensor(out=ex[:], in0=v[:], scalar=-1.0, in1=v[:], op0=ALU.mult, op1=ALU.min), after=["v", ("dec", -1), ("d1", -1)], done="na")

                put("scalar", lambda e, b: e.activation(ex[:], ex[:], ACT.Exp), after=["na"], done="e",
                    first=lambda e: e.preload_act_table_set("natural_log_exp_and_others"))
                put("vector", lambda e, b: e.tensor_scalar(ul[:], ex[:], 1.0, None, ALU.add), after=["e"], done="1e")
                put("vector", lambda e, b: e.scalar_tensor_tensor(out=ex[:], in0=ul[:], scalar=1.0, in1=ex[:], op0=ALU.subtract, op1=ALU.subtract), after=["1e"], done="lost")
                put("scalar", lambda e, b: e.activation(ul[:], ul[:], ACT.Ln), after=["lost"], done="ln")
                put("vector", lambda e, b: e.tensor_tensor(ul[:], ul[:], ex[:], ALU.subtract), after=["ln"], done="l1")
                put("vector", lambda e, b: e.scalar_tensor_tensor(out=v[:], in0=v[:], scalar=0.0, in1=ul[:], op0=ALU.max, op1=ALU.add), after=["l1"], done="dtv")
                put("scalar", lambda e, b: e.activation(ex[:], v[:], ACT.Exp, scale=am[:, 0:1]), after=["dtv"], done="dec")
                yield
                for n, (tag, col, dst) in enumerate((("C", CC, ct), ("B", BC, bt))):
                    project(put, tag, n, col, ["yl2", "yl3"])
                    yield
                    convolve(put, tag, n, (col - XC) // P, n, ("xs%d" % (6 + n), -1))
                    put("scalar", lambda e, b, n=n, dst=dst: e.activation(dst[:], cv[:, n, :], ACT.Silu),
                        after=[f"{tag}_t0", ("Yo7", -1), ("G", -1), ("bT", -1)], done=tag + "s")
                    yield
                put("vector", lambda e, b: e.tensor_copy(d1[:, starts], ex[:, starts]), after=["dec"], done="d1")
                put("vector", lambda e, b: e.memset(ex[:, starts], 0.0), after=["d1"], done="dec0")
                put("vector", lambda e, b: e.tensor_copy(dec2[:], ex[:]), after=["dec0", ("L15", -1)], done="dech")
                put("vector", lambda e, b: e.tensor_tensor(dec2[32:64, :], ex[32:64, :], dec2[32:64, :].bitcast(F32), ALU.subtract), after=["dech"], done="dec2")
                put("vector", lambda e, b: e.tensor_tensor_scan(ul[:], ex[:], d1[:], 0.0, ALU.mult, ALU.add), after=["dec0"], done="pre")
                put("vector", lambda e, b: e.tensor_copy(pre2[:], ul[:]), after=["pre", ("Pb7", -1)], done="preh")
                put("vector", lambda e, b: e.tensor_tensor(pre2[32:64, :], ul[32:64, :], pre2[32:64, :].bitcast(F32), ALU.subtract), after=["preh"], done="pre2")
                yield
                put("vector", lambda e, b: e.tensor_tensor(dg[:], eye[0:HM, 0:HM].unsqueeze(1).broadcast_to([HM, TQ, HM]),
                    ul[0:HM, ends].unsqueeze(2).broadcast_to([HM, TQ, HM]), ALU.mult), after=["pre", ("dlm", -1)], done="dg")
                put("tensor", lambda e, b: e.matmul(ps[:, 2, TQ * HM:2 * TQ * HM], ones[0:HM, :].broadcast_to([HM, P]), dg[:], start=True, stop=True), after=["v", "dtv", "dg"])
                for c in range(TQ):
                    put("tensor", lambda e, b, c=c: e.transpose(ps[:, 2, c * HM:(c + 1) * HM], v[0:HM, c * P:(c + 1) * P], eye[0:HM, 0:HM]),
                        done="dlm" if c == TQ - 1 else None)
                put("vector", lambda e, b: e.tensor_copy(dtT[:], ps[:, 2, 0:TQ * HM].rearrange("p (c h) -> p c h", c=TQ)), after=["dlm", ("xp7", -1)], done="dtT")
                put("vector", lambda e, b: e.tensor_copy(dl[:], ps[:, 2, TQ * HM:2 * TQ * HM].rearrange("p (c h) -> p c h", c=TQ)), after=["dlm", ("H7", -1)], done="dl")
                yield
                for c in range(TQ):
                    put("tensor", lambda e, b, c=c: e.matmul(ps[:, 0, c * P:(c + 1) * P], bt[:, c * P:(c + 1) * P], ct[:, c * P:(c + 1) * P], start=True, stop=True),
                        after=["Cs", "Bs", "C_t0"], done="G" if c == TQ - 1 else None)
                for c in range(TQ):
                    put("tensor", lambda e, b, c=c: e.transpose(ps[:, 1, c * P:(c + 1) * P], bt[:, c * P:(c + 1) * P], eye),
                        after=["Bs", "B_t0"], done="bT" if c == TQ - 1 else None)
                put("scalar", lambda e, b: e.activation(g[:], ps[:, 0, :], ACT.Copy), after=["G", ("gm15", -1)], done="g")
                put("scalar", lambda e, b: e.activation(bk[:], ps[:, 1, :].rearrange("p (c n) -> p c n", c=TQ), ACT.Copy), after=["bT", ("St7", -1)], done="bk")
                yield

            def inner(stage, tiles_m):
                put = lambda *p, **k: r.put(stage, *p, **k)
                for m in tiles_m:
                    n, f = m % 2, m % 3
                    project(put, f"x{m}", 0, XC + m * P, ["yl3", f"x{m - 1}_t0" if m else "g"])
                    yield
                    convolve(put, f"x{m}", 0, m, n, f"xs{m - 2}" if m >= 2 else "Cs" if m == 0 else "Bs")
                    put("scalar", lambda e, b, n=n, f=f: e.activation(xs[:, f, :], cv[:, n, :], ACT.Silu),
                        after=[f"x{m}_t0"] + [f"w{m - 3}" if m >= 3 else (f"w{(6, 7, 5)[m]}", -1)], done=f"xs{m}")
                    yield
                    project(put, f"z{m}", 1, m * P, [f"sz{m - 1}" if m else "bk"])
                    put("scalar", lambda e, b, f=f: e.activation(sz[:, f, :], ps[:, 1, :], ACT.Silu),
                        after=[f"z{m}"] + [f"u{m - 3}" if m >= 3 else (f"u{(6, 7, 5)[m]}", -1)], done=f"sz{m}")
                    yield

            def scan():
                put = lambda *p, **k: r.put("S", *p, **k)

                def prev(m, tag, d=1):
                    return f"{tag}{m - d}" if m >= d else (f"{tag}{m - d + MI}", -1)

                def weights(m):
                    n, f = m % 2, m % 3
                    for j in range(2):
                        h = 2 * m + j
                        put("tensor", lambda e, b, j=j, h=h: e.matmul(ps[:, 3 + j, :], sel[:, h:h + 1].broadcast_to([P, P]), dec2[:], start=True, stop=True),
                            after=["dec2", f"pb{m - 2}" if m >= 2 else ("pb7", -1), f"L{h - 2}" if h >= 2 else (f"L{h + 14}", -1)], done=f"De{h}")
                        put("vector", lambda e, b, j=j: e.tensor_tensor_scan(lm[:, j, :], ps[:, 3 + j, :], eyes[:].rearrange("p c t -> p (c t)"), 0.0, ALU.mult, ALU.add),
                            after=[f"De{h}", f"gm{h - 2}" if h >= 2 else (f"gm{h + 14}", -1), prev(m, "xw")], done=f"L{h}")
                    yield
                    for c in range(TQ):
                        put("tensor", lambda e, b, c=c: e.transpose(ps[:, 2, c * P:(c + 1) * P], xs[:, f, c * P:(c + 1) * P], eye),
                            after=[f"xs{m}", prev(m, "xp"), "dl", "dtT"], done=f"tx{m}" if c == TQ - 1 else None)
                    put("vector", lambda e, b, m=m, n=n: e.tensor_tensor(xp[:, n, :, :].rearrange("p c (j d) -> p c j d", j=2),
                        ps[:, 2, :].rearrange("p (c j d) -> p c j d", c=TQ, j=2),
                        dtT[:, :, 2 * m:2 * m + 2].unsqueeze(3).broadcast_to([P, TQ, 2, 64]), ALU.mult),
                        after=[f"tx{m}", prev(m, "Yi", 2)], done=f"xp{m}")
                    for j in range(2):
                        put("gpsimd", lambda e, b, j=j, n=n: e.tensor_tensor(xw[:, n, :, j * 64:(j + 1) * 64], xp[:, n, 0:TQ - 1, j * 64:(j + 1) * 64],
                            lm[:, j, P - 1:(TQ - 1) * P:P].unsqueeze(2).broadcast_to([P, TQ - 1, 64]), ALU.mult),
                            after=[f"xp{m}", f"L{2 * m + j}", prev(m, "St", 2)], done=f"xw{m}" if j else f"xw{m}_0")
                        put("gpsimd", lambda e, b, j=j, n=n: e.tensor_tensor(gm[:, n, j, :], lm[:, j, :], g[:], ALU.mult),
                            after=["g", prev(m, "Yi", 2)], done=f"gm{2 * m + j}")

                def states(m):
                    n = m % 2
                    for c in range(TQ - 1):
                        put("tensor", lambda e, b, n=n, c=c: e.matmul(ps[:, 7, c * P:(c + 1) * P], bk[:, c, :], xw[:, n, c, :], start=True, stop=True),
                            after=["bk", f"xw{m}", prev(m, "H")], done=f"St{m}" if c == TQ - 2 else None)
                    put("vector", lambda e, b: e.tensor_copy(hs[:, 0, :], ps[:, 7, 0:P]), after=[f"St{m}", prev(m, "Yo")], done=f"H{m}_1")
                    for c in range(1, TQ - 1):
                        for j in range(2):
                            cols = slice(j * 64, (j + 1) * 64)
                            put("vector", lambda e, b, c=c, j=j, m=m, cols=cols: e.scalar_tensor_tensor(out=hs[:, c, cols], in0=hs[:, c - 1, cols],
                                scalar=dl[:, c, 2 * m + j:2 * m + j + 1], in1=ps[:, 7, c * P + j * 64:c * P + (j + 1) * 64], op0=ALU.mult, op1=ALU.add),
                                after=[f"H{m}_{c}", "dl"], done=None if j == 0 else f"H{m}_{c + 1}" if c < TQ - 2 else f"H{m}")

                def outputs(m):
                    n, f = m % 2, m % 3
                    for c in range(TQ):
                        for j in range(2):
                            rows_j = slice(j * 64, (j + 1) * 64)
                            put("tensor", lambda e, b, c=c, j=j, n=n, rows_j=rows_j: e.matmul(ps[rows_j, 5, c * P:(c + 1) * P], xp[:, n, c, rows_j],
                                gm[:, n, j, c * P:(c + 1) * P], start=True, stop=True),
                                after=[f"xp{m}", f"gm{2 * m + 1}", prev(m, "w")], done=f"Yi{m}" if (c, j) == (TQ - 1, 1) else None)
                    yield
                    put("tensor", lambda e, b, m=m: e.matmul(ps[:, 3, :], selp[:, m, :], pre2[:], start=True, stop=True),
                        after=["pre2", f"L{min(2 * m + 2, HM - 2)}", prev(m, "pb")], done=f"Pb{m}")
                    put("scalar", lambda e, b: e.activation(pb[:], ps[:, 3, :], ACT.Copy), after=[f"Pb{m}", prev(m, "t")], done=f"pb{m}")
                    for c in range(1, TQ):
                        put("tensor", lambda e, b, c=c: e.matmul(ps[:, 6, c * P:(c + 1) * P], hs[:, c - 1, :], ct[:, c * P:(c + 1) * P], start=True, stop=True),
                            after=["Cs", f"H{m}", prev(m, "t")], done=f"Yo{m}" if c == TQ - 1 else None)
                    late = slice(P, S)
                    put("vector", lambda e, b: e.scalar_tensor_tensor(out=yw[:, 0:P], in0=xs[:, f, 0:P], scalar=skip[:, m:m + 1],
                        in1=ps[:, 5, 0:P], op0=ALU.mult, op1=ALU.add), after=[f"Yi{m}", f"xs{m}", prev(m, "u")], done=f"w{m}_0")
                    put("vector", lambda e, b: e.tensor_tensor(yw[:, late], ps[:, 6, late], pb[:, late], ALU.mult), after=[f"Yo{m}", f"pb{m}"], done=f"t{m}")
                    put("vector", lambda e, b: e.tensor_tensor(yw[:, late], yw[:, late], ps[:, 5, late], ALU.add), after=[f"t{m}"], done=f"ty{m}")
                    put("vector", lambda e, b: e.scalar_tensor_tensor(out=yw[:, late], in0=xs[:, f, late], scalar=skip[:, m:m + 1],
                        in1=yw[:, late], op0=ALU.mult, op1=ALU.add), after=[f"ty{m}"], done=f"w{m}")
                    put("gpsimd", lambda e, b: e.tensor_tensor(u[:, m, :], yw[:], sz[:, f, :], ALU.mult), after=[f"w{m}", f"sz{m}", ("o3", -1)], done=f"u{m}")
                    put("scalar", lambda e, b, m=m: e.activation(sq[:] if m else ssq[:], u[:, m, :], ACT.Square),
                        after=[f"u{m}", f"sa{m - 1}" if m > 1 else ("so_mm", -1)], done=f"sq{m}")
                    if m:
                        put("gpsimd", lambda e, b: e.tensor_tensor(ssq[:], ssq[:], sq[:], ALU.add), after=[f"sq{m}", f"sq{m - 1}" if m == 1 else f"sa{m - 1}"], done=f"sa{m}")

                for m in range(MI + 1):
                    if m < MI:
                        yield from weights(m)
                        yield
                    if m:
                        states(m - 1)
                        yield
                        yield from outputs(m - 1)
                        yield


            def out():
                put = lambda *p, **k: r.put("O", *p, **k)
                for q in range(TQ):
                    for k in range(MI):
                        put("tensor", lambda e, b, q=q, k=k: e.matmul(ps[:, 5 + q % 2, :], u[:, k, q * P:(q + 1) * P], wo[:, k, :], start=(k == 0), stop=(k == MI - 1)),
                            after=["wos", "u7", "w7", "t7", f"oc{q - 2}" if q >= 2 else "w7"], done=f"o{q}" if k == MI - 1 else None)
                    put("scalar", lambda e, b, q=q: e.activation(o[:, q % 2, :], ps[:, 5 + q % 2, :], ACT.Copy),
                        after=[f"o{q}", f"o_out{q - 2}" if q >= 2 else (f"o_out{q + 2}", -1)], done=f"oc{q}")
                    put("sync", lambda e, b, q=q: e.dma_start(scratch["o"][row(b), :, q, :].rearrange("b p d -> (b p) d"), o[:, q % 2, :]), after=[f"oc{q}"], dma=f"o_out{q}")
                    if q == 0:
                        for c in range(TQ):
                            put("tensor", lambda e, b, c=c: e.matmul(ps[:, 7, c:c + 1], ssq[:, c * P:(c + 1) * P], ones[:], start=True, stop=True),
                                after=["sa7", "H7"], done="so_mm" if c == TQ - 1 else None)
                        put("vector", lambda e, b: e.tensor_copy(so[:], ps[:, 7, 0:TQ]), after=["so_mm", ("so_out", -1)], done="so")
                        put("sync", lambda e, b: e.dma_start(scratch["ssq"][row(b)].rearrange("b p q -> (b p) q"), so[:]), after=["so"], dma="so_out")
                    yield

            interleave("SPSPPSPPSSPSSSSSPPSSPSSSPPSSPSSSPPSSPSSASPPSSPSASSPPSPSSSSAASSASAASSAAAAAAOOAAAFFOFO",
                       A=prepare(), F=inner("F", [0]), P=inner("P", range(1, MI)), S=scan(), O=out())
            put = lambda *p, **k: r.put("W", *p, **k)
            put("sync", lambda e, b: e.dma_start(wo[:], a["Wout"].rearrange("(k p) n -> p k n", p=P)), dma="wo")
            for k in range(MI):
                put("gpsimd", lambda e, b, k=k: e.tensor_tensor(wo[:, k, :], wo[:, k, :], gw[:, k:k + 1].broadcast_to([P, D]), ALU.mult),
                    after=["wo"], done="wos" if k == MI - 1 else None)
            r.emit()


def layer1(nc, a, scratch, out, rows):
    with ExitStack() as ctx:
        def sb(name, shape, dt=F32):
            return ctx.enter_context(nc.sbuf_tensor(f"l1_{name}", shape, dt))
        wq, wo = ([sb(f"{n}{h}", [P, KT, D], F32R) for h in "hl"] for n in ("wq", "wo"))
        qb = sb("qb", [P, KT])
        eye = sb("eye", [P, P])
        keep, neg = sb("keep", [P, C]), sb("neg", [P, C])
        o_in, y_in, ss = sb("o_in", [P, TQ, D]), sb("y_in", [P, TQ, D]), sb("ss", [P, TQ])
        h = [sb(f"h{n}", [P, TQ, D]) for n in range(4)]
        xn = sb("xn", [P, TQ, D])
        xt = [sb(f"x{h}", [P, KT, S], F32R) for h in "hl"]
        qt = sb("qt", [P, KT, S])
        kd, km = sb("kd", [P, KT, 2 * C]), sb("km", [P, KT, 2 * C])
        v = sb("v", [C, D])
        sc = sb("sc", [P, TQ, H1, C])
        mx, sm, rs = sb("mx", [P, TQ, H1]), sb("sm", [P, TQ, H1]), sb("rs", [P, TQ, H1])
        pt = sb("pt", [C, H1, S])
        cs = [sb(f"c{h}", [P, KT, S], F32R) for h in "hl"]
        ot = sb("ot", [P, TQ, D])
        vu, ru, t1 = sb("vu", [P, TQ]), sb("ru", [P, TQ]), sb("t1", [P, TQ])
        st, mv = sb("st", [P, TQ, 6]), sb("mv", [P, TQ, 2])
        var, rstd, t2 = sb("var", [P, TQ]), sb("rstd", [P, TQ]), sb("t2", [P, TQ])
        ps = ctx.enter_context(nc.psum_tensor("l1_ps", [P, 8, 512], F32))

        mask, lw, lb = sb("mask", [P, C], U8), sb("lw", [P, KT]), sb("lb", [P, KT])

        with ExitStack() as c2:
            r = Region(nc, c2, "l1", rows, {"W": 0, "L": 0, "A": 1, "M": 1, "K": 2, "W1": 2, "V": 2, "T": 3, "B": 3, "O": 4}, "natural_log_exp_and_others")
            put = lambda *p, **k: r.put("W", *p, **k)
            put("scalar", lambda e, b: e.dma_start(lw[:], tiles(a["lnw"]), allow_slow_non_contiguous=True), dma="lw")
            put("scalar", lambda e, b: e.dma_start(lb[:], tiles(a["lnb"]), allow_slow_non_contiguous=True), dma="lb")
            put("scalar", lambda e, b: e.dma_start(mask[:], a["kmask"].broadcast_to([P, C])), dma="mask")
            put("sync", lambda e, b: e.dma_start(xn[:], a["Wq1"].rearrange("(k p) n -> p k n", p=P)), dma="wq_raw")
            put("sync", lambda e, b: e.dma_start(eye[:], a["eye"]), dma="eye")
            for m in range(KT):
                for k in range(KT):
                    put("tensor", lambda e, b, m=m, k=k: e.matmul(ps[:, 0, m:m + 1], xn[:, k, m * P:(m + 1) * P], lb[:, k:k + 1], start=(k == 0), stop=(k == KT - 1)),
                        after=["wq_raw", "lb"], done="qb_mm" if (m, k) == (KT - 1, KT - 1) else None)
            put("vector", lambda e, b: e.tensor_scalar(qb[:], ps[:, 0, 0:KT], HD1 ** -0.5, None, ALU.mult), after=["qb_mm"], done="qb")
            put("vector", lambda e, b: e.tensor_scalar(lw[:], lw[:], HD1 ** -0.5, None, ALU.mult), after=["lw"], done="columns")
            split_weights(r, [("wq", a["Wq1"].rearrange("(k p) n -> p k n", p=P), h[0], wq, lw),
                              ("wo", a["Wo1"].rearrange("(k p) n -> p k n", p=P), h[1], wo, 1.0)])
            put("vector", lambda e, b: e.tensor_copy(neg[:], mask[:]), after=["mask"], done="mf")
            put("vector", lambda e, b: e.tensor_scalar(keep[:], neg[:], -1.0, 1.0, ALU.mult, ALU.add), after=["mf"], done="keep")
            put("vector", lambda e, b: e.tensor_scalar(neg[:], neg[:], MASKED, None, ALU.mult), after=["keep"], done="neg")
            put("gpsimd", lambda e, b: e.memset(kd[:], 0.0), done="kz")

            def load():
                put = lambda *p, **k: r.put("L", *p, **k)
                rows_of = lambda t, b: t[row(b)].rearrange("b p q d -> (b p) q d")
                put("sync", lambda e, b: e.dma_start(ss[:], scratch["ssq"][row(b)].rearrange("b p q -> (b p) q")), after=[("vu", -1)], dma="ss")
                put("sync", lambda e, b: e.dma_start(o_in[:], rows_of(scratch["o"], b)), after=[("h3", -1)], dma="o_in")
                put("sync", lambda e, b: e.dma_start(y_in[:], rows_of(scratch["y"], b)), after=[("h3", -1)], dma="y_in")
                yield

            def prepare():
                put = lambda *p, **k: r.put("A", *p, **k)
                put("vector", lambda e, b: e.tensor_scalar(vu[:], ss[:], 1.0 / DI, EPS, ALU.mult, ALU.add), after=["ss", ("ru", -1)], done="vu")
                root_guess(r, "A", vu[:], ru[:], ["vu", ("h3", -1)], "ru")
                yield
                root_refine(r, "A", vu[:], ru[:], t1[:], "ru")
                for pair in range(2):
                    for q in range(2 * pair, 2 * pair + 2):
                        put("vector", lambda e, b, q=q: e.scalar_tensor_tensor(out=h[0][:, q, :], in0=o_in[:, q, :], scalar=ru[:, q:q + 1], in1=y_in[:, q, :],
                            op0=ALU.mult, op1=ALU.add), after=["ru", "wq_l3", "o_in", "y_in", (f"h1_{q}", -1)], done=f"h{q}")
                        put("vector", lambda e, b, q=q: e.bn_stats(st[:, q, :], h[0][:, q, :]), after=[f"h{q}"], done=f"st{q}")
                    yield
                for q in range(TQ):
                    put("vector", lambda e, b, q=q: e.bn_aggr(mv[:, q, :], st[:, q, :]), after=[f"st{q}"], done=f"mv{q}", apart=q)
                put("vector", lambda e, b: e.tensor_scalar(var[:], mv[:, :, 1], EPS, None, ALU.add), after=["mv3"], done="var")
                root_guess(r, "A", var[:], rstd[:], ["var"], "rstd")
                yield
                root_refine(r, "A", var[:], rstd[:], t2[:], "rstd")
                for q in range(TQ):
                    put("vector", lambda e, b, q=q: e.tensor_scalar(xn[:, q, :], h[0][:, q, :], mv[:, q, 0:1], rstd[:, q:q + 1], ALU.subtract, ALU.mult),
                        after=["rstd", "qb_mm", (f"tr{q}", -1)], done=f"n{q}")
                yield
                for q in range(TQ):
                    for k in range(KT):
                        put("tensor", lambda e, b, q=q, k=k: e.transpose(ps[:, q % 2, k * P:(k + 1) * P], xn[:, q, k * P:(k + 1) * P], eye[:]),
                            after=[f"n{q}", "eye", "qb", f"xl{q - 2}" if q >= 2 else (f"qt{q + 2}", -1)], done=f"tr{q}" if k == KT - 1 else None)
                    cols = slice(q * P, (q + 1) * P)
                    src = ps[:, q % 2, :].rearrange("p (k t) -> p k t", k=KT)
                    put("scalar", lambda e, b, cols=cols, src=src: e.activation(xt[0][:, :, cols], src, ACT.Copy), after=[f"tr{q}", ("q3", -1)], done=f"xh{q}")
                    put("vector", lambda e, b, cols=cols, src=src: e.tensor_tensor(xt[1][:, :, cols], src, xt[0][:, :, cols].bitcast(F32), ALU.subtract),
                        after=[f"xh{q}"], done=f"xl{q}")
                    yield

            def load_keys():
                put = lambda *p, **k: r.put("M", *p, **k)
                for j in range(2):
                    put("sync", lambda e, b, j=j: e.dma_start(kd[j * HD1:(j + 1) * HD1, :, j * C:(j + 1) * C],
                        scratch["k1"].rearrange("m p t -> p m t")[j * HD1:(j + 1) * HD1, :, row(b, C)]), after=["kz", ("km", -1)], dma="kd", unit=C)
                yield

            def carry(stage, n):
                for q in range(TQ):
                    r.put(stage, "scalar", lambda e, b, q=q: e.activation(h[n][:, q, :], h[n - 1][:, q, :], ACT.Copy),
                          after=["wo_l3", f"h{n - 1}_{q}" if n > 1 else f"h{q}", (f"h{n + 1}_{q}" if n < 3 else f"out{q}", -1)], done=f"h{n}_{q}")

            def mask_keys():
                r.put("K", "gpsimd", lambda e, b: e.tensor_tensor(km[:].rearrange("p m (j c) -> p (m j) c", j=2), kd[:].rearrange("p m (j c) -> p (m j) c", j=2),
                    keep[:].unsqueeze(1).broadcast_to([P, 2 * KT, C]), ALU.mult), after=["kd", "keep", (f"S{TQ - 1}", -1)], done="km")
                yield

            def load_values():
                r.put("V", "sync", lambda e, b: e.dma_start(v[:], scratch["v1"][row(b, C), :]), after=[("pv3", -1)], dma="v", unit=C)
                yield

            def attend(part):
                put = lambda *p, **k: r.put(part, *p, **k)

                def queries():
                    carry("W1", 1)
                    yield
                    for m in range(KT):
                        for k in range(KT):
                            put("tensor", lambda e, b, m=m, k=k: mm3(e, ps[:, m % 2, :], [w_[:, k, m * P:(m + 1) * P] for w_ in wq],
                                [x_[:, k, :] for x_ in xt], k == 0, k == KT - 1),
                                after=["xl3", "wq_l3", f"qt{m - 2}" if m >= 2 else "xl3"], done=f"q{m}" if k == KT - 1 else None)
                        yield
                        put("scalar", lambda e, b, m=m: e.activation(qt[:, m, :], ps[:, m % 2, :], ACT.Identity, bias=qb[:, m:m + 1]),
                            after=[f"q{m}", "qb", (f"S{TQ - 1}", -1)], done=f"qt{m}")
                        yield

                def weigh(q):
                    for m in range(KT):
                        put("tensor", lambda e, b, m=m: e.matmul(ps[:, 2 + m // 2, (m % 2) * 2 * C:(m % 2 + 1) * 2 * C], qt[:, m, q * P:(q + 1) * P], km[:, m, :],
                            start=True, stop=True), after=["qt3", "km", f"add{q - 1}" if q else ("add3", -1)], done=f"S{q}" if m == KT - 1 else None)
                    yield
                    put("vector", lambda e, b: e.tensor_tensor(sc[:, q, :, :].rearrange("p (a h) c -> p a h c", a=2),
                        ps[:, 2:4, 0:4 * C].rearrange("p a (h c) -> p a h c", h=4),
                        neg[:].unsqueeze(1).unsqueeze(1).broadcast_to([P, 2, 4, C]), ALU.add), after=[f"S{q}", "neg", (f"pt{q}_1", -1)], done=f"add{q}")
                    put("vector", lambda e, b: e.tensor_reduce(mx[:, q, :], sc[:, q, :, :], AX_X, ALU.max), after=[f"add{q}"], done=f"mx{q}")
                    put("vector", lambda e, b: e.tensor_tensor(sc[:, q, :, :], sc[:, q, :, :], mx[:, q, :].unsqueeze(2).broadcast_to([P, H1, C]), ALU.subtract),
                        after=[f"mx{q}"], done=f"sub{q}")
                    put("scalar", lambda e, b: e.activation(sc[:, q, :, :], sc[:, q, :, :], ACT.Exp), after=[f"sub{q}"], done=f"e{q}")

                def normalise(q):
                    put("vector", lambda e, b: e.tensor_reduce(sm[:, q, :], sc[:, q, :, :], AX_X, ALU.add), after=[f"e{q}"], done=f"sm{q}")
                    put("vector", lambda e, b: e.reciprocal(rs[:, q, :], sm[:, q, :]), after=[f"sm{q}", (f"nm{q}", -1)], done=f"rs{q}")
                    put("gpsimd", lambda e, b: e.tensor_tensor(sc[:, q, :, :], sc[:, q, :, :], rs[:, q, :].unsqueeze(2).broadcast_to([P, H1, C]), ALU.mult),
                        after=[f"rs{q}"], done=f"nm{q}")

                def turn(q):
                    for half in range(2):
                        for i in range(H1 // 2):
                            put("tensor", lambda e, b, half=half, i=i: e.transpose(ps[0:C, 4 + half, i * P:(i + 1) * P], sc[:, q, half * H1 // 2 + i, :], eye[:]),
                                after=[f"nm{q}", f"pc{q - 1}_{half}" if q else (f"pc3_{half}", -1)], done=f"pt{q}_{half}" if i == H1 // 2 - 1 else None)
                        put("scalar", lambda e, b, half=half: e.activation(pt[:, half * H1 // 2:(half + 1) * H1 // 2, q * P:(q + 1) * P],
                            ps[0:C, 4 + half, :].rearrange("c (h t) -> c h t", h=H1 // 2), ACT.Copy), after=[f"pt{q}_{half}", ("pv3", -1)], done=f"pc{q}_{half}")

                if part == "W1":
                    yield from queries()
                for step in {"W1": ((weigh, 0), (weigh, 1), (normalise, 0)),
                             "T": ((weigh, 2), (weigh, 3), (normalise, 1), (turn, 0), (normalise, 2), (turn, 1), (normalise, 3), (turn, 2), (turn, 3))}[part]:
                    yield from step[0](step[1]) or ()
                    yield

            def finish():
                put = lambda *p, **k: r.put("B", *p, **k)
                carry("B", 2)
                yield
                for m in range(KT):
                    for j in range(2):
                        h = 2 * m + j
                        put("tensor", lambda e, b, m=m, j=j, h=h: e.matmul(ps[j * HD1:(j + 1) * HD1, 6 + m % 2, :], v[:, h * HD1:(h + 1) * HD1], pt[:, h, :], start=True, stop=True),
                            after=["v", "pc3_1", f"cl{m - 2}" if m >= 2 else (f"out{m + 2}", -1)], done=f"pv{m}" if j else None)
                    yield
                    put("scalar", lambda e, b, m=m: e.activation(cs[0][:, m, :], ps[:, 6 + m % 2, :], ACT.Copy), after=[f"pv{m}", ("O3", -1)], done=f"ch{m}")
                    put("vector", lambda e, b, m=m: e.tensor_tensor(cs[1][:, m, :], ps[:, 6 + m % 2, :], cs[0][:, m, :].bitcast(F32), ALU.subtract),
                        after=[f"ch{m}"], done=f"cl{m}")
                    yield

            def out_project():
                put = lambda *p, **k: r.put("O", *p, **k)
                carry("O", 3)
                yield
                for q in range(TQ):
                    for k in range(KT):
                        put("tensor", lambda e, b, q=q, k=k: mm3(e, ps[:, 6 + q % 2, :], [c_[:, k, q * P:(q + 1) * P] for c_ in cs],
                            [w_[:, k, :] for w_ in wo], k == 0, k == KT - 1),
                            after=["cl3", "wo_l3", f"out{q - 2}" if q >= 2 else "cl3"], done=f"O{q}" if k == KT - 1 else None)
                    yield
                    put("vector", lambda e, b, q=q: e.tensor_tensor(ot[:, q, :], ps[:, 6 + q % 2, :], h[3][:, q, :], ALU.add),
                        after=[f"O{q}", f"h3_{q}", (f"store{q}", -1)], done=f"out{q}")
                    put("sync", lambda e, b, q=q: e.dma_start(out[row(b), q * P:(q + 1) * P, :].rearrange("b p d -> (b p) d"), ot[:, q, :]), after=[f"out{q}"], dma=f"store{q}")
                    yield

            interleave("OATTBOOTTWATAOOWWWWTLWWTATWWTTAOOKAMOOTAABBABBWWWWWBBBBV",
                       L=load(), M=load_keys(), A=prepare(), K=mask_keys(), V=load_values(), W=attend("W1"), T=attend("T"),
                       B=finish(), O=out_project())
            r.emit()


def build(nc, a, out):
    rows = a["x"].shape[0]
    tokens = a["ctxT"].shape[1]
    shapes = {"k0h": [KT, P, tokens], "k0l": [KT, P, tokens], "k1": [KT, P, tokens], "v0": [tokens, D], "v1": [tokens, D],
              "y": [rows, P, TQ, D], "o": [rows, P, TQ, D], "rinv": [rows, P, TQ], "ssq": [rows, P, TQ]}
    scratch = {n: nc.dram_tensor(f"scratch_{n}", s, F32).ap() for n, s in shapes.items()}
    keys_values(nc, a, scratch)
    layer0(nc, a, scratch, rows)
    mamba(nc, a, scratch, rows)
    layer1(nc, a, scratch, out, rows)


def kernel(**inputs):
    import numpy as np
    from concourse import bacc
    from concourse.bass_utils import run_bass_kernel_spmd

    get = lambda n: np.asarray(inputs[n])
    l0, l1 = (lambda n: get(f"L0_xattn_{n}")), (lambda n: get(f"L1_xattn_{n}"))
    ctx = get("ctx_1024")
    arrays = {
        "x": get("x"), "xT": get("x").transpose(0, 2, 1), "ctxT": ctx.transpose(2, 0, 1).reshape(ctx.shape[2], -1),
        "maskT": get("mask_Bx1xSxS2_fk0")[:, 0].transpose(0, 2, 1), "kmask": get("mask_1xS2_bf0"),
        "Wq0": l0("Wq"), "bq0": l0("bq"), "Wk0": l0("Wk"), "bk0": l0("bk"), "Wv0": l0("Wv"), "bv0": l0("bv"),
        "Wo0": l0("Wo"), "bo0": l0("bo"), "gamma0": l0("gamma"), "beta0": l0("beta"),
        "norm1": l1("m_norm_w"), "Win": l1("in_proj_w"), "cw": l1("conv_w"), "cb": l1("conv_b"), "dtb": l1("dt_bias"),
        "alog": l1("A_log"), "skip": l1("D_skip"), "gnorm1": l1("gnorm_w"), "Wout": l1("out_proj_w"),
        "lnw": l1("ca_ln_w"), "lnb": l1("ca_ln_b"), "Wq1": l1("Wq"), "Wk1": l1("Wk"), "Wv1": l1("Wv"), "Wo1": l1("Wo"),
        "eye": np.eye(P, dtype=np.float32),
    }
    nc = bacc.Bacc("TRN2", target_bir_lowering=False, num_devices=1)
    maps, args = {}, {}
    for name, array in arrays.items():
        maps[f"in_{name}"] = np.ascontiguousarray(array)
        args[name] = nc.dram_tensor(f"in_{name}", array.shape, mybir.dt.from_np(array.dtype), kind="ExternalInput").ap()
    out = nc.dram_tensor("out", get("x").shape, F32, kind="ExternalOutput").ap()
    build(nc, args, out)
    return run_bass_kernel_spmd(nc, [maps], core_ids=[0]).results[0]["out"]
```
